# Optimizing a Trainium2 kernel written in Bass

```python
import numpy as np
import jax
import jax.numpy as jnp

def _softmax(x, axis=-1):
    return jax.nn.softmax(x, axis=axis)

def _gelu(x):
    return jax.nn.gelu(x, approximate=True)

def _silu(x):
    return jax.nn.silu(x)

def _sigmoid(x):
    return jax.nn.sigmoid(x)

def _layernorm(x, axis=-1, eps=1e-05):
    m = jnp.mean(x, axis=axis, keepdims=True)
    v = jnp.var(x, axis=axis, keepdims=True)
    return (x - m) / jnp.sqrt(v + eps)

def _scatter_add(tgt, idx, src, axis=0):
    return tgt.at[idx].add(src)

def _segment_sum(src, seg, n):
    return jax.ops.segment_sum(src, seg, n)
kernel_name = 'mk_prb_d2_jaxref_r8_879a21'

def setup_inputs(seed: int=0):
    np.random.seed(seed)
    _w = jnp.asarray

    def _L0_attn_setup():
        import jax, jax.numpy as jnp
        import numpy as np
        from jax import lax
        BLOCK_LEN = 128
        NEG_INF = -1000000000.0
        key = jax.random.key(seed)
        ks = jax.random.split(key, 8)
        N, L, Dm = (2, 1024, 512)
        W, H, dh = (128, 16, 64)
        s = lambda fan: 1.0 / np.sqrt(fan)
        return {'inputs': jax.random.normal(ks[0], (N, L, Dm), jnp.float32), 'conv_w': jax.random.normal(ks[1], (3, Dm, 3 * W), jnp.float32) * s(3 * Dm), 'conv_b': jnp.zeros((3 * W,), jnp.float32), 'wq': jax.random.normal(ks[2], (W, H, dh), jnp.float32) * s(W), 'bq': jnp.zeros((H, dh), jnp.float32), 'wk': jax.random.normal(ks[3], (W, H, dh), jnp.float32) * s(W), 'bk': jnp.zeros((H, dh), jnp.float32), 'wv': jax.random.normal(ks[4], (W, H, dh), jnp.float32) * s(W), 'bv': jnp.zeros((H, dh), jnp.float32), 'wo': jax.random.normal(ks[5], (H, dh, W), jnp.float32) * s(H * dh), 'bo': jnp.zeros((W,), jnp.float32), 'proj_w': jax.random.normal(ks[6], (W, Dm), jnp.float32) * s(W), 'proj_b': jnp.zeros((Dm,), jnp.float32)}
    _L0_attn_in = _L0_attn_setup()

    def _L0_ffn_setup():
        import jax, jax.numpy as jnp
        import numpy as np
        D_IN = 512
        D_OUT = 512
        RANK = 16
        NUM_EXPERTS = 8
        TOP_K = 2
        SCALING = 32.0 / RANK
        key = jax.random.key(seed)
        ks = jax.random.split(key, 6)
        x = jax.random.normal(ks[0], (4, 256, D_IN), dtype=jnp.float32)
        W_base = jax.random.normal(ks[1], (D_OUT, D_IN), dtype=jnp.float32) * (1.0 / np.sqrt(D_IN))
        b_base = jax.random.normal(ks[2], (D_OUT,), dtype=jnp.float32) * 0.01
        W_router = jax.random.normal(ks[3], (NUM_EXPERTS, D_IN), dtype=jnp.float32) * 0.01
        A_stack = jax.random.uniform(ks[4], (NUM_EXPERTS, RANK, D_IN), dtype=jnp.float32, minval=-1.0, maxval=1.0) * (1.0 / np.sqrt(D_IN))
        B_stack = jax.random.normal(ks[5], (NUM_EXPERTS, D_OUT, RANK), dtype=jnp.float32) * 0.02
        return {'x': x, 'W_base': W_base, 'b_base': b_base, 'W_router': W_router, 'A_stack': A_stack, 'B_stack': B_stack}
    _L0_ffn_in = _L0_ffn_setup()

    def _L1_attn_setup():
        import jax, jax.numpy as jnp
        import numpy as np
        HIDDEN = 512
        NUM_HEADS = 32
        HEAD_DIM = HIDDEN // NUM_HEADS

        def _fp8_roundtrip(x):
            return x.astype(jnp.float8_e4m3fn).astype(jnp.float32)
        key = jax.random.key(seed)
        ks = jax.random.split(key, 10)
        B, S = (2, 512)
        hidden_states = jax.random.normal(ks[0], (B, S, HIDDEN), dtype=jnp.float32)
        scale = 0.02

        def lin(kw, kb):
            w = jax.random.normal(kw, (HIDDEN, HIDDEN), dtype=jnp.float32) * scale
            b = jax.random.normal(kb, (HIDDEN,), dtype=jnp.float32) * scale
            return (w, b)
        wq, bq = lin(ks[1], ks[2])
        wk, bk = lin(ks[3], ks[4])
        wv, bv = lin(ks[5], ks[6])
        wl, bl = lin(ks[7], ks[8])
        wq, bq = (_fp8_roundtrip(wq), _fp8_roundtrip(bq))
        wk, bk = (_fp8_roundtrip(wk), _fp8_roundtrip(bk))
        wv, bv = (_fp8_roundtrip(wv), _fp8_roundtrip(bv))
        return {'hidden_states': hidden_states, 'wq': wq, 'bq': bq, 'wk': wk, 'bk': bk, 'wv': wv, 'bv': bv, 'wl': wl, 'bl': bl}
    _L1_attn_in = _L1_attn_setup()

    def _L1_ffn_setup():
        import jax, jax.numpy as jnp
        import numpy as np
        HIDDEN = 512
        INTER = 1376
        GROUP = 128
        B, S = (4, 256)
        NIB = jnp.uint32(15)

        def _pack_rows(nib):
            r = nib.reshape(-1, 8, nib.shape[-1])
            shifts = (jnp.arange(8, dtype=jnp.uint32) * 4)[None, :, None]
            return jnp.sum(r << shifts, axis=1, dtype=jnp.uint32)

        def _pack_cols(nib):
            r = nib.reshape(nib.shape[0], -1, 8)
            shifts = (jnp.arange(8, dtype=jnp.uint32) * 4)[None, None, :]
            return jnp.sum(r << shifts, axis=2, dtype=jnp.uint32)

        def _dequant(qw, qz, sc, g_idx):
            shifts = jnp.arange(8, dtype=jnp.uint32) * 4
            wq = qw[:, None, :] >> shifts[None, :, None] & NIB
            wq = wq.reshape(-1, qw.shape[1]).astype(jnp.float32)
            zq = qz[:, :, None] >> shifts[None, None, :] & NIB
            zq = zq.reshape(qz.shape[0], -1).astype(jnp.float32) + 1.0
            return sc[g_idx] * (wq - zq[g_idx])
        key = jax.random.key(seed)
        ks = jax.random.split(key, 7)
        n_groups = HIDDEN // GROUP
        n_groups_d = INTER // GROUP
        x = jax.random.normal(ks[0], (B, S, HIDDEN), jnp.float32)
        nib_w_gu = jax.random.randint(ks[1], (HIDDEN, 2 * INTER), 0, 16).astype(jnp.uint32)
        nib_z_gu = jax.random.randint(ks[2], (n_groups, 2 * INTER), 0, 15).astype(jnp.uint32)
        qweight_gu = _pack_rows(nib_w_gu)
        qzeros_gu = _pack_cols(nib_z_gu)
        scales_gu = jax.random.uniform(ks[3], (n_groups, 2 * INTER), jnp.float32, 0.005, 0.02)
        g_idx_gu = jnp.arange(HIDDEN, dtype=jnp.int32) // GROUP
        nib_w_d = jax.random.randint(ks[4], (INTER, HIDDEN), 0, 16).astype(jnp.uint32)
        nib_z_d = jax.random.randint(ks[5], (n_groups_d, HIDDEN), 0, 15).astype(jnp.uint32)
        qweight_down = _pack_rows(nib_w_d)
        qzeros_down = _pack_cols(nib_z_d)
        scales_down = jax.random.uniform(ks[6], (n_groups_d, HIDDEN), jnp.float32, 0.005, 0.02)
        g_idx_down = jnp.arange(INTER, dtype=jnp.int32) // GROUP
        return {'x': x, 'qweight_gu': qweight_gu, 'qzeros_gu': qzeros_gu, 'scales_gu': scales_gu, 'g_idx_gu': g_idx_gu, 'qweight_down': qweight_down, 'qzeros_down': qzeros_down, 'scales_down': scales_down, 'g_idx_down': g_idx_down}
    _L1_ffn_in = _L1_ffn_setup()
    _d = {'L0_attn_inputs': _L0_attn_in['inputs'], 'L0_attn_conv_w': _L0_attn_in['conv_w'], 'L0_attn_conv_b': _L0_attn_in['conv_b'], 'L0_attn_wq': _L0_attn_in['wq'], 'L0_attn_bq': _L0_attn_in['bq'], 'L0_attn_wk': _L0_attn_in['wk'], 'L0_attn_bk': _L0_attn_in['bk'], 'L0_attn_wv': _L0_attn_in['wv'], 'L0_attn_bv': _L0_attn_in['bv'], 'L0_attn_wo': _L0_attn_in['wo'], 'L0_attn_bo': _L0_attn_in['bo'], 'L0_attn_proj_w': _L0_attn_in['proj_w'], 'L0_attn_proj_b': _L0_attn_in['proj_b'], 'L0_ffn_W_base': _L0_ffn_in['W_base'], 'L0_ffn_b_base': _L0_ffn_in['b_base'], 'L0_ffn_W_router': _L0_ffn_in['W_router'], 'L0_ffn_A_stack': _L0_ffn_in['A_stack'], 'L0_ffn_B_stack': _L0_ffn_in['B_stack'], 'L1_attn_wq': _L1_attn_in['wq'], 'L1_attn_bq': _L1_attn_in['bq'], 'L1_attn_wk': _L1_attn_in['wk'], 'L1_attn_bk': _L1_attn_in['bk'], 'L1_attn_wv': _L1_attn_in['wv'], 'L1_attn_bv': _L1_attn_in['bv'], 'L1_attn_wl': _L1_attn_in['wl'], 'L1_attn_bl': _L1_attn_in['bl'], 'L1_ffn_qweight_gu': _L1_ffn_in['qweight_gu'], 'L1_ffn_qzeros_gu': _L1_ffn_in['qzeros_gu'], 'L1_ffn_scales_gu': _L1_ffn_in['scales_gu'], 'L1_ffn_g_idx_gu': _L1_ffn_in['g_idx_gu'], 'L1_ffn_qweight_down': _L1_ffn_in['qweight_down'], 'L1_ffn_qzeros_down': _L1_ffn_in['qzeros_down'], 'L1_ffn_scales_down': _L1_ffn_in['scales_down'], 'L1_ffn_g_idx_down': _L1_ffn_in['g_idx_down']}
    _x0 = _d['L0_attn_inputs']
    _d['L0_attn_inputs'] = jax.random.normal(jax.random.fold_in(jax.random.key(seed), 1), (4, 512, 512), dtype=_x0.dtype)
    del _x0
    return _d

def reference(L0_attn_inputs, L0_attn_conv_w, L0_attn_conv_b, L0_attn_wq, L0_attn_bq, L0_attn_wk, L0_attn_bk, L0_attn_wv, L0_attn_bv, L0_attn_wo, L0_attn_bo, L0_attn_proj_w, L0_attn_proj_b, L0_ffn_W_base, L0_ffn_b_base, L0_ffn_W_router, L0_ffn_A_stack, L0_ffn_B_stack, L1_attn_wq, L1_attn_bq, L1_attn_wk, L1_attn_bk, L1_attn_wv, L1_attn_bv, L1_attn_wl, L1_attn_bl, L1_ffn_qweight_gu, L1_ffn_qzeros_gu, L1_ffn_scales_gu, L1_ffn_g_idx_gu, L1_ffn_qweight_down, L1_ffn_qzeros_down, L1_ffn_scales_down, L1_ffn_g_idx_down):

    def _L0_attn_ref(inputs, conv_w, conv_b, wq, bq, wk, bk, wv, bv, wo, bo, proj_w, proj_b):
        import jax, jax.numpy as jnp
        import numpy as np
        from jax import lax
        BLOCK_LEN = 128
        NEG_INF = -1000000000.0
        N, L, Dm = inputs.shape
        x = lax.conv_general_dilated(inputs, conv_w, window_strides=(1,), padding='SAME', dimension_numbers=('NWC', 'WIO', 'NWC')) + conv_b
        q, k, v = jnp.split(x, 3, axis=-1)
        W_ = q.shape[-1]
        nb = L // BLOCK_LEN
        q = q.reshape(N * nb, BLOCK_LEN, W_)
        k = k.reshape(N * nb, BLOCK_LEN, W_)
        v = v.reshape(N * nb, BLOCK_LEN, W_)
        dh = wq.shape[-1]
        qh = jnp.einsum('btd,dhe->bthe', q, wq) + bq
        kh = jnp.einsum('btd,dhe->bthe', k, wk) + bk
        vh = jnp.einsum('btd,dhe->bthe', v, wv) + bv
        scale = 1.0 / jnp.sqrt(jnp.asarray(dh, qh.dtype))
        scores = jnp.einsum('bqhe,bkhe->bhqk', qh * scale, kh)
        causal = jnp.tril(jnp.ones((BLOCK_LEN, BLOCK_LEN), bool))
        scores = jnp.where(causal, scores, NEG_INF)
        p = jax.nn.softmax(scores, axis=-1)
        o = jnp.einsum('bhqk,bkhe->bqhe', p, vh)
        o = jnp.einsum('bqhe,hed->bqd', o, wo) + bo
        o = o.reshape(N, L, W_)
        return o @ proj_w + proj_b

    def _L0_ffn_ref(x, W_base, b_base, W_router, A_stack, B_stack):
        import jax, jax.numpy as jnp
        import numpy as np
        D_IN = 512
        D_OUT = 512
        RANK = 16
        NUM_EXPERTS = 8
        TOP_K = 2
        SCALING = 32.0 / RANK
        orig_shape = x.shape
        xf = x.reshape(-1, D_IN)
        logits = xf @ W_router.T
        probs = jax.nn.softmax(logits, axis=-1)
        topk_p, topk_i = jax.lax.top_k(probs, TOP_K)
        topk_p = topk_p / jnp.sum(topk_p, axis=-1, keepdims=True)
        combine = jnp.sum(jax.nn.one_hot(topk_i, NUM_EXPERTS, dtype=xf.dtype) * topk_p[..., None], axis=1)
        h = jnp.einsum('nd,erd->ner', xf, A_stack)
        h = h * combine[..., None]
        lora_out = jnp.einsum('ner,eor->no', h, B_stack) * SCALING
        base_out = xf @ W_base.T + b_base
        out = base_out + lora_out
        return out.reshape(orig_shape[:-1] + (D_OUT,))

    def _L1_attn_ref(hidden_states, wq, bq, wk, bk, wv, bv, wl, bl):
        import jax, jax.numpy as jnp
        import numpy as np
        HIDDEN = 512
        NUM_HEADS = 32
        HEAD_DIM = HIDDEN // NUM_HEADS

        def _fp8_roundtrip(x):
            return x.astype(jnp.float8_e4m3fn).astype(jnp.float32)
        B, S, E = hidden_states.shape
        H, D = (NUM_HEADS, HEAD_DIM)
        q = (hidden_states @ wq.T + bq).reshape(B, S, H, D)
        k = (hidden_states @ wk.T + bk).reshape(B, S, H, D)
        v = (hidden_states @ wv.T + bv).reshape(B, S, H, D)
        latent = hidden_states @ wl.T + bl
        scores = jnp.einsum('bshd,bstd->bsht', q, k) / np.sqrt(D).astype(np.float32)
        probs = jax.nn.softmax(scores, axis=-1)
        context = jnp.einsum('bsht,bstd->bshd', probs, v).reshape(B, S, E)
        return context

    def _L1_ffn_ref(x, qweight_gu, qzeros_gu, scales_gu, g_idx_gu, qweight_down, qzeros_down, scales_down, g_idx_down):
        import jax, jax.numpy as jnp
        import numpy as np
        HIDDEN = 512
        INTER = 1376
        GROUP = 128
        B, S = (4, 256)
        NIB = jnp.uint32(15)

        def _pack_rows(nib):
            r = nib.reshape(-1, 8, nib.shape[-1])
            shifts = (jnp.arange(8, dtype=jnp.uint32) * 4)[None, :, None]
            return jnp.sum(r << shifts, axis=1, dtype=jnp.uint32)

        def _pack_cols(nib):
            r = nib.reshape(nib.shape[0], -1, 8)
            shifts = (jnp.arange(8, dtype=jnp.uint32) * 4)[None, None, :]
            return jnp.sum(r << shifts, axis=2, dtype=jnp.uint32)

        def _dequant(qw, qz, sc, g_idx):
            shifts = jnp.arange(8, dtype=jnp.uint32) * 4
            wq = qw[:, None, :] >> shifts[None, :, None] & NIB
            wq = wq.reshape(-1, qw.shape[1]).astype(jnp.float32)
            zq = qz[:, :, None] >> shifts[None, None, :] & NIB
            zq = zq.reshape(qz.shape[0], -1).astype(jnp.float32) + 1.0
            return sc[g_idx] * (wq - zq[g_idx])
        w_gu = _dequant(qweight_gu, qzeros_gu, scales_gu, g_idx_gu)
        inter = jnp.einsum('bsh,hf->bsf', x, w_gu)
        gate, up = (inter[..., :INTER], inter[..., INTER:])
        h = jax.nn.silu(gate) * up
        w_d = _dequant(qweight_down, qzeros_down, scales_down, g_idx_down)
        return jnp.einsum('bsf,fh->bsh', h, w_d)
    x = L0_attn_inputs
    xn = _layernorm(x, axis=-1)
    x = x + _L0_attn_ref(xn, L0_attn_conv_w, L0_attn_conv_b, L0_attn_wq, L0_attn_bq, L0_attn_wk, L0_attn_bk, L0_attn_wv, L0_attn_bv, L0_attn_wo, L0_attn_bo, L0_attn_proj_w, L0_attn_proj_b) + _L0_ffn_ref(xn, L0_ffn_W_base, L0_ffn_b_base, L0_ffn_W_router, L0_ffn_A_stack, L0_ffn_B_stack)
    xn = _layernorm(x, axis=-1)
    x = x + _L1_attn_ref(xn, L1_attn_wq, L1_attn_bq, L1_attn_wk, L1_attn_bk, L1_attn_wv, L1_attn_bv, L1_attn_wl, L1_attn_bl) + _L1_ffn_ref(xn, L1_ffn_qweight_gu, L1_ffn_qzeros_gu, L1_ffn_scales_gu, L1_ffn_g_idx_gu, L1_ffn_qweight_down, L1_ffn_qzeros_down, L1_ffn_scales_down, L1_ffn_g_idx_down)
    return x

_drawn_inputs = setup_inputs


def setup_inputs(seed=0):
    import zlib

    import numpy as np

    out = dict(_drawn_inputs(seed))
    spreads = {'L0_attn_conv_b': (0.0, 0.1),
     'L0_attn_bq': (0.0, 0.418),
     'L0_attn_bk': (0.0, 2.0),
     'L0_attn_bv': (0.0, 0.1),
     'L0_attn_bo': (0.0, 0.1),
     'L0_attn_proj_b': (0.0, 0.1)}
    factors = {'L0_ffn_b_base': 6.181,
     'L1_attn_wq': 8.0,
     'L1_attn_bq': 8.0,
     'L1_attn_wk': 8.0,
     'L1_attn_bk': 8.0,
     'L1_attn_wv': 4.775,
     'L1_attn_bv': 21.82}
    for name, (base, spread) in spreads.items():
        noise = np.random.default_rng([zlib.crc32(name.encode()), seed]).standard_normal(out[name].shape)
        drawn = base * np.exp(spread * noise) if base else spread * noise
        out[name] = jnp.asarray(drawn.astype(out[name].dtype))
    for name, factor in factors.items():
        out[name] = (out[name] * factor).astype(out[name].dtype)
    return out
```

```python
from contextlib import ExitStack

import concourse.bass as bass
from concourse import mybir

F32 = mybir.dt.float32
F32R = mybir.dt.float32r
BF16 = mybir.dt.bfloat16
U32 = mybir.dt.uint32
I32 = mybir.dt.int32
ALU = mybir.AluOpType
ACT = mybir.ActivationFunctionType
AX_X = mybir.AxisListType.X

P = 128
NSEQ, L, D = 4, 512, 512
NT = L // P
KD = D // P
TAPS = 3
W = 128
H0, DH0 = 16, 64
HG = 4
NHG = H0 // HG
NBLK = L // P
STEPS = NHG * NBLK
NE, RANK = 8, 16
ER = NE * RANK
EPS = 1e-5
LORA_SCALE = 32.0 / RANK
H1, DH1 = 32, 16

C_CONV = 0
C_WQ = C_CONV + TAPS * KD * 3 * W
C_WK = C_WQ + H0 * DH0
C_WV = C_WK + H0 * DH0
C_WO = C_WV + H0 * DH0
C_PROJ = C_WO + (H0 * DH0 // P) * W
C_BASE = C_PROJ + D
C_AR = C_BASE + KD * D
AR = 256
C_B = C_AR + KD * AR
N_A = C_B + D
WCH = 800
N_WCH = N_A // WCH
assert N_WCH * WCH == N_A and N_WCH % 2 == 0
B_CONV, B_Q, B_K, B_V, B_O, B_Q1, B_K1 = 0, 3, 11, 19, 27, 28, 32
N_BF = 36


def spread(ap, n):
    return ap.unsqueeze(2).broadcast_to([ap.shape[0], ap.shape[1], n])


def split3(pe, out, lhs, rhs, start, stop):
    pe.matmul(out, lhs[0], rhs[0], start=start, stop=False, skip_group_check=True)
    pe.matmul(out, lhs[0], rhs[1], start=False, stop=False, skip_group_check=True)
    return pe.matmul(out, lhs[1], rhs[0], start=False, stop=stop, skip_group_check=True)


def bank_uses():
    uses = [("conv", "AD")] * 3 + [("ar", "A")] * NT
    uses += [(n, e) for n, e in (("q", "A"), ("q", "A"), ("k", "AD"), ("k", "AD"), ("v", "D"), ("v", "D"))] * NHG
    uses += [("hT", "AD")] + [("x1", "D")] * NT
    return uses


USES = bank_uses()
assert len(USES) % 2 == 0
ACT_USES = sum("A" in e for _, e in USES)
DVE_USES = sum("D" in e for _, e in USES)


def freed(letter, upto):
    return sum(letter in e for _, e in USES[:upto])


def layer0(nc, x, w0, bias_f, proj_b, base_b, ident, ident_bf, causal, iota8, x1_dram):
    with ExitStack() as ctx:
        def sb(name, shape, dt=F32):
            return ctx.enter_context(nc.sbuf_tensor(name, shape, dt))

        def sem(name):
            return ctx.enter_context(nc.semaphore(name))

        w_hi = sb("w0_hi", [P, N_A], F32R)
        w_lo = sb("w0_lo", [P, N_A], F32R)
        xin = sb("xin", [P, 2, D])
        xres = sb("xres", [P, 2, D])
        xT_hi = sb("xT_hi", [P, KD, L + 2], F32R)
        xT_lo = sb("xT_lo", [P, KD, L + 2], F32R)
        c_hi = sb("c_hi", [P, 3, L], F32R)
        c_lo = sb("c_lo", [P, 3, L], F32R)
        qh = sb("qh", [P, 2, 2, L])
        kh = sb("kh", [P, 2, 2, 2, L])
        vh = sb("vh", [P, 2, NBLK, HG * DH0])
        prob = sb("prob", [P, 3, HG * P])
        probT = sb("probT", [P, 2, HG * P])
        o_hi = sb("o_hi", [P, 2, L], F32R)
        o_lo = sb("o_lo", [P, 2, L], F32R)
        a_hi = sb("a_hi", [P, L], F32R)
        a_lo = sb("a_lo", [P, L], F32R)
        har = sb("har", [P, NT, ER + NE])
        hT_hi = sb("hT_hi", [P, L], F32R)
        hT_lo = sb("hT_lo", [P, L], F32R)
        bf = sb("bf", [P, N_BF])
        brow = sb("brow", [P, D])
        brow2 = sb("brow2", [P, D])
        idf = sb("idf", [P, P])
        idb = sb("idb", [P, P], BF16)
        neg = sb("neg", [P, HG * P], BF16)
        io8 = sb("io8", [P, NT * NE])
        mx = sb("mx", [P, 3, HG])
        nmx = sb("nmx", [P, 3, HG])
        sums = sb("sums", [P, 3, HG])
        rsum = sb("rsum", [P, 3, HG])
        stats = sb("stats", [P, 2, 6])
        mv = sb("mv", [P, 2, 2])
        veps = sb("veps", [P, 2])
        rstd = sb("rstd", [P, 2])
        mhalf = sb("mhalf", [P, 2])
        rmx = sb("rmx", [P, NT])
        rp = sb("rp", [P, NT, NE])
        rs = sb("rs", [P, NT])
        top = sb("top", [P, NT, 8])
        topi = sb("topi", [P, NT, 8], U32)
        topf = sb("topf", [P, NT, 8])
        wsel = sb("wsel", [P, NT, 2])
        eq = sb("eq", [P, 2, NT, NE])
        comb = sb("comb", [P, NT, NE])
        ps = ctx.enter_context(nc.psum_tensor("ps0", [P, 8, 512], F32))
        MM, SC, PT, AV, WO = 0, 2, 4, 5, 7
        XT_BANKS = (SC, SC + 1, PT, AV)
        stage = qh[:].rearrange("p a b t -> p (a b t)").rearrange("p (s n) -> p s n", s=2)

        const_in, carrier = sem("const_in"), sem("carrier")
        w_in = [sem(f"w_in{s}") for s in range(2)]
        x_in = [sem(f"x_in{s}") for s in range(2)]
        res_in = [sem(f"res_in{s}") for s in range(2)]
        x1_out = [sem(f"x1_out{s}") for s in range(2)]
        w_hi_ready, w_lo_ready = sem("w_hi_ready"), sem("w_lo_ready")
        zeroed, mhalf_set = sem("zeroed"), sem("mhalf_set")
        brow_ready = sem("brow_ready")
        st_done, ve_ready, rstd_ready, xn_ready = sem("st_done"), sem("ve_ready"), sem("rstd_ready"), sem("xn_ready")
        xt_done, xT_hi_ready, xT_lo_ready = sem("xt_done"), sem("xT_hi_ready"), sem("xT_lo_ready")
        mm_full, mm_act, mm_dve = sem("mm_full"), sem("mm_act"), sem("mm_dve")
        router_exp, router_chain, comb_ready = sem("router_exp"), sem("router_chain"), sem("comb_ready")
        sc_full, mx_ready, nmx_ready, exp_done = sem("sc_full"), sem("mx_ready"), sem("nmx_ready"), sem("exp_done")
        rsum_ready, prob_ready, tr_full, probT_ready = sem("rsum_ready"), sem("prob_ready"), sem("tr_full"), sem("probT_ready")
        av_done, o_hi_ready, o_lo_ready, wo_done = sem("av_done"), sem("o_hi_ready"), sem("o_lo_ready"), sem("wo_done")
        a_hi_ready, a_lo_ready = sem("a_hi_ready"), sem("a_lo_ready")
        res_ready, x1_ready = sem("res_ready"), sem("x1_ready")

        def carry(eng):
            eng.sem_inc(carrier, 1)

        def wt(c, n):
            return w_hi[:, c:c + n], w_lo[:, c:c + n]

        U_AR = 3
        U_QKV = U_AR + NT
        U_HT = U_QKV + 6 * NHG
        U_X1 = U_HT + 1
        NU = len(USES)

        def use_act(hg, k):
            return U_QKV + 6 * hg + k

        with nc.Block() as block:

            @block.sync
            def _(sp):
                sp.dma_start(bf[:], bias_f).then_inc(const_in, 16)
                sp.dma_start(idf[:], ident).then_inc(const_in, 16)
                for s in range(2):
                    sp.dma_start(xin[:, s, :], x[s * P:(s + 1) * P, :]).then_inc(x_in[s], 16)
                sp.dma_start(idb[:], ident_bf).then_inc(const_in, 16)
                sp.dma_start(neg[:], causal).then_inc(const_in, 16)
                sp.dma_start(io8[:], iota8).then_inc(const_in, 16)
                sp.dma_start(brow[:], bass.AP(proj_b.tensor, 0, [[0, P], [1, D]])).then_inc(const_in, 16)
                sp.dma_start(brow2[:], bass.AP(base_b.tensor, 0, [[0, P], [1, D]])).then_inc(const_in, 16)
                for s in range(2):
                    sp.dma_start(stage[:, s, 0:WCH], w0[:, s * WCH:(s + 1) * WCH]).then_inc(w_in[s], 16)
                with sp.Fori(1, N_WCH // 2) as j:
                    for s in range(2):
                        sp.wait_ge(w_hi_ready, 2 * j - 1 + s)
                        sp.wait_ge(w_lo_ready, 2 * j - 1 + s)
                        sp.dma_start(stage[:, s, 0:WCH], w0[:, bass.ds((2 * j + s) * WCH, WCH)]).then_inc(w_in[s], 16)
                for s in range(2):
                    sp.wait_ge(xt_done, s + 1)
                    sp.dma_start(xin[:, s, :], x[(2 + s) * P:(3 + s) * P, :]).then_inc(x_in[s], 16)

                def body(i, last):
                    for s in range(2):
                        sp.wait_ge(x1_out[s], 32 * i)
                        sp.dma_start(xres[:, s, :], x[bass.ds(i * L + s * P, P), :]).then_inc(res_in[s], 16)
                    if not last:
                        for s in range(2):
                            sp.wait_ge(xt_done, NT * i + NT)
                            sp.dma_start(xin[:, s, :], x[bass.ds(i * L + L + s * P, P), :]).then_inc(x_in[s], 16)
                    for t in range(NT):
                        sp.wait_ge(x1_ready, NT * i + t + 1)
                        sp.dma_start(x1_dram[bass.ds(i * L + t * P, P), :], xres[:, t % 2, :]).then_inc(x1_out[t % 2], 16)
                        if t < 2:
                            sp.wait_ge(x1_out[t], 32 * i + 16)
                            sp.dma_start(xres[:, t, :], x[bass.ds(i * L + (t + 2) * P, P), :]).then_inc(res_in[t], 16)
                    if not last:
                        for s in range(2):
                            sp.wait_ge(xt_done, NT * i + NT + s + 1)
                            sp.dma_start(xin[:, s, :], x[bass.ds(i * L + L + (2 + s) * P, P), :]).then_inc(x_in[s], 16)

                body(0, False)
                with sp.Fori(1, NSEQ - 1) as i:
                    body(i, False)
                body(NSEQ - 1, True)
                for s in range(2):
                    sp.wait_ge(x1_out[s], 32 * NSEQ)

            @block.gpsimd
            def _(pool):
                pool.memset(mhalf[:], -0.5).then_inc(mhalf_set, 1)
                for b in (0, L + 1):
                    pool.memset(xT_hi[:, :, b:b + 1].bitcast(F32), 0.0).then_inc(zeroed, 1)
                    pool.memset(xT_lo[:, :, b:b + 1].bitcast(F32), 0.0).then_inc(zeroed, 1)
                pool.memset(kh[:], 0.0).then_inc(zeroed, 1)
                pool.wait_ge(const_in, 16 * 7)
                pool.tensor_tensor(brow[:], brow[:], brow2[:], ALU.add).then_inc(brow_ready, 1)
                pool.wait_ge(brow_ready, 1)
                pool.wait_ge(mhalf_set, 1)

                def rstds(n):
                    pool.wait_ge(ve_ready, n + 1)
                    pool.tensor_tensor(rstd[:], veps[:], mhalf[:], ALU.pow).then_inc(rstd_ready, 1)

                def residual(i, t):
                    pool.wait_ge(res_in[t % 2], 32 * i + 16 * (t // 2) + 16)
                    pool.tensor_tensor(xres[:, t % 2, :], xres[:, t % 2, :], brow[:], ALU.add).then_inc(res_ready, 1)

                def body(i, last):
                    for s in range(STEPS):
                        pool.wait_ge(rsum_ready, STEPS * i + s + 1)
                        pv = prob[:, s % 3, :].rearrange("p (h k) -> p h k", h=HG)
                        pool.tensor_tensor(pv, pv, spread(rsum[:, s % 3, :], P), ALU.mult).then_inc(prob_ready, 1)
                    for t in range(2):
                        residual(i, t)
                    if not last:
                        rstds(2 * i + 2)
                    for t in range(2, NT):
                        residual(i, t)
                    if not last:
                        rstds(2 * i + 3)

                rstds(0)
                rstds(1)
                body(0, False)
                with pool.Fori(1, NSEQ - 1) as i:
                    body(i, False)
                body(NSEQ - 1, True)

            @block.scalar
            def _(act):
                with act.Fori(0, N_WCH // 2) as j:
                    for s in range(2):
                        act.wait_ge(w_in[s], 16 * j + 16)
                        act.activation(w_hi[:, bass.ds((2 * j + s) * WCH, WCH)], stage[:, s, 0:WCH], ACT.Copy).then_inc(w_hi_ready, 1)

                def xT_hi_copy(i):
                    act.wait_ge(xt_done, NT * i + NT)
                    for k in range(KD):
                        act.activation(xT_hi[:, k, 1:L + 1], ps[:, XT_BANKS[k], :], ACT.Copy).then_inc(xT_hi_ready, 1)

                def full(i, u):
                    act.wait_ge(mm_full, NU * i + u + 1)

                def qk_hi(i, hg):
                    act.wait_ge(av_done, STEPS * i + max(0, NBLK * (hg - 1)))
                    for hp in range(2):
                        full(i, use_act(hg, hp))
                        b = bf[:, B_Q + 2 * hg + hp:B_Q + 2 * hg + hp + 1]
                        act.activation(qh[:, hg % 2, hp, :], ps[:, (use_act(hg, hp)) % 2, :], ACT.Identity, bias=b).then_inc(mm_act, 1)
                    for hp in range(2):
                        u = use_act(hg, 2 + hp)
                        full(i, u)
                        act.activation(kh[0:DH0, hg % 2, hp, 0, :], ps[0:DH0, u % 2, :], ACT.Identity,
                                       bias=bf[0:DH0, B_K + 2 * hg + hp:B_K + 2 * hg + hp + 1]).then_inc(mm_act, 1)

                def exps(i, s):
                    act.wait_ge(nmx_ready, STEPS * i + s + 1)
                    act.wait_ge(tr_full, STEPS * i + max(0, s - 2))
                    for h in range(HG):
                        e = act.activation(prob[:, s % 3, h * P:(h + 1) * P], ps[:, SC + s % 2, h * P:(h + 1) * P], ACT.Exp,
                                           bias=nmx[:, s % 3, h:h + 1], scale=DH0 ** -0.5, accum_out=sums[:, s % 3, h:h + 1])
                    e.then_inc(exp_done, 1)

                def o_his(i, hg):
                    act.wait_ge(av_done, STEPS * i + NBLK * (hg + 1))
                    act.wait_ge(wo_done, NHG * i + hg)
                    for hp in range(2):
                        act.activation(o_hi[:, hp, :], ps[:, AV + hp, :], ACT.Identity,
                                       bias=bf[:, B_V + 2 * hg + hp:B_V + 2 * hg + hp + 1]).then_inc(o_hi_ready, 1)

                def body(i, last):
                    for m in range(3):
                        full(i, m)
                        act.wait_ge(av_done, STEPS * i)
                        act.activation(c_hi[:, m, :], ps[:, m % 2, :], ACT.Identity, bias=bf[:, B_CONV + m:B_CONV + m + 1]).then_inc(mm_act, 1)
                    for t in range(NT):
                        full(i, U_AR + t)
                        act.wait_ge(mm_full, NU * i)
                        act.activation(har[:, t, :], ps[:, (U_AR + t) % 2, 0:ER + NE], ACT.Copy).then_inc(mm_act, 1)
                    act.wait_ge(w_lo_ready, N_WCH)
                    qk_hi(i, 0)
                    for s in range(STEPS + 3):
                        if s % NBLK == 3 and s // NBLK + 1 < NHG:
                            qk_hi(i, s // NBLK + 1)
                        if s < STEPS:
                            exps(i, s)
                        if s == 3:
                            act.wait_ge(router_chain, 13 * i + 2)
                            act.activation(rp[:], rp[:], ACT.Exp).then_inc(router_exp, 1)
                        if s % NBLK == 2 and s >= 6:
                            o_his(i, (s - 6) // NBLK)
                    full(i, U_HT)
                    act.activation(hT_hi[:], ps[:, U_HT % 2, :], ACT.Copy).then_inc(mm_act, 1)
                    act.wait_ge(wo_done, NHG * i + NHG)
                    act.activation(a_hi[:], ps[:, WO, :], ACT.Identity, bias=bf[:, B_O:B_O + 1]).then_inc(a_hi_ready, 1)
                    if not last:
                        xT_hi_copy(i + 1)

                act.wait_ge(const_in, 16 * 7)
                xT_hi_copy(0)
                body(0, False)
                with act.Fori(1, NSEQ - 1) as i:
                    body(i, False)
                body(NSEQ - 1, True)

            @block.vector
            def _(dve):
                def norm_pair(n, first):
                    for s in range(2):
                        dve.wait_ge(x_in[s], 16 * n + 16)
                        dve.bn_stats(stats[:, s, :], xin[:, s, :]).then_inc(st_done, 1)
                    for s in range(2):
                        dve.wait_ge(st_done, 4 * n + 2)
                        carry(dve)
                        dve.bn_aggr(mv[:, s, :], stats[:, s, :]).then_inc(st_done, 1)
                    dve.wait_ge(st_done, 4 * n + 4)
                    dve.tensor_scalar(veps[:], mv[:, :, 1], EPS, None, ALU.add).then_inc(ve_ready, 1)
                    dve.wait_ge(rstd_ready, n + 1)
                    for s in range(2):
                        dve.tensor_scalar(xin[:, s, :], xin[:, s, :], mv[:, s, 0:1], rstd[:, s:s + 1], ALU.subtract, ALU.mult).then_inc(xn_ready, 1)

                def xT_lo_copy(i):
                    for k in range(KD):
                        dve.wait_ge(xT_hi_ready, KD * i + k + 1)
                        dve.tensor_tensor(xT_lo[:, k, 1:L + 1], ps[:, XT_BANKS[k], :], xT_hi[:, k, 1:L + 1].bitcast(F32), ALU.subtract).then_inc(xT_lo_ready, 1)

                def full(i, u):
                    dve.wait_ge(mm_full, NU * i + u + 1)

                def acted(i, u):
                    dve.wait_ge(mm_act, ACT_USES * i + freed("A", u + 1))

                def kv(i, hg):
                    dve.wait_ge(av_done, STEPS * i + max(0, NBLK * (hg - 1)))
                    for hp in range(2):
                        u = use_act(hg, 2 + hp)
                        full(i, u)
                        dve.tensor_scalar(kh[DH0:P, hg % 2, hp, 1, :], ps[DH0:P, u % 2, :],
                                          bf[DH0:P, B_K + 2 * hg + hp:B_K + 2 * hg + hp + 1], None, ALU.add).then_inc(mm_dve, 1)
                    for half in range(2):
                        u = use_act(hg, 4 + half)
                        full(i, u)
                        dve.tensor_copy(vh[:, hg % 2, 2 * half:2 * half + 2, :].rearrange("p b n -> p (b n)"), ps[:, u % 2, :]).then_inc(mm_dve, 1)

                def router(i):
                    n = [0]

                    def step(ins):
                        n[0] += 1
                        ins.then_inc(router_chain, 1)
                        dve.wait_ge(router_chain, 13 * i + n[0])

                    acted(i, U_AR + NT - 1)
                    step(dve.tensor_reduce(rmx[:], har[:, :, ER:ER + NE], AX_X, ALU.max))
                    step(dve.tensor_tensor(rp[:], har[:, :, ER:ER + NE], spread(rmx[:], NE), ALU.subtract))
                    dve.wait_ge(router_exp, i + 1)
                    step(dve.tensor_reduce(rs[:], rp[:], AX_X, ALU.add))
                    step(dve.reciprocal(rs[:], rs[:]))
                    step(dve.tensor_tensor(rp[:], rp[:], spread(rs[:], NE), ALU.mult))
                    carry(dve)
                    for t in range(NT):
                        top_i = dve.max(top[:, t, :], rp[:, t, :])
                    step(top_i)
                    carry(dve)
                    for t in range(NT):
                        idx_i = dve.max_index(topi[:, t, :], top[:, t, :], rp[:, t, :])
                    step(idx_i)
                    dve.tensor_tensor(rs[:], top[:, :, 0], top[:, :, 1], ALU.add)
                    step(dve.tensor_copy(topf[:], topi[:]))
                    step(dve.reciprocal(rs[:], rs[:]))
                    step(dve.tensor_tensor(wsel[:], top[:, :, 0:2], spread(rs[:], 2), ALU.mult))
                    iov = io8[:].rearrange("p (t e) -> p t e", t=NT)
                    for j in range(2):
                        e = dve.tensor_tensor(eq[:, j, :, :], iov, spread(topf[:, :, j], NE), ALU.is_equal)
                    step(e)
                    for j in range(2):
                        e = dve.tensor_tensor(eq[:, j, :, :], eq[:, j, :, :], spread(wsel[:, :, j], NE), ALU.mult)
                    step(e)
                    step(dve.tensor_tensor(comb[:], eq[:, 0, :, :], eq[:, 1, :, :], ALU.add))
                    assert n[0] == 13
                    for t in range(NT):
                        hv = har[:, t, 0:ER].rearrange("p (e r) -> p e r", e=NE)
                        cv = spread(comb[:, t, :], RANK)
                        dve.scalar_tensor_tensor(hv, hv, LORA_SCALE, cv, ALU.mult, ALU.mult).then_inc(comb_ready, 1)

                def maxes(i, s):
                    dve.wait_ge(sc_full, STEPS * i + s + 1)
                    dve.tensor_reduce(mx[:, s % 3, :], ps[:, SC + s % 2, :].rearrange("p (h k) -> p h k", h=HG), AX_X, ALU.max).then_inc(mx_ready, 1)
                    dve.wait_ge(mx_ready, STEPS * i + s + 1)
                    dve.tensor_scalar(nmx[:, s % 3, :], mx[:, s % 3, :], -DH0 ** -0.5, None, ALU.mult).then_inc(nmx_ready, 1)

                def recips(i, s):
                    dve.wait_ge(exp_done, STEPS * i + s + 1)
                    dve.wait_ge(prob_ready, STEPS * i + max(0, s - 2))
                    dve.reciprocal(rsum[:, s % 3, :], sums[:, s % 3, :]).then_inc(rsum_ready, 1)

                def probT_copy(i, s):
                    dve.wait_ge(tr_full, STEPS * i + s + 1)
                    dve.wait_ge(av_done, STEPS * i + max(0, s - 1))
                    dve.tensor_copy(probT[:, s % 2, :], ps[:, PT, :]).then_inc(probT_ready, 1)

                def o_los(i, hg):
                    for hp in range(2):
                        dve.wait_ge(o_hi_ready, 2 * NHG * i + 2 * hg + hp + 1)
                        dve.scalar_tensor_tensor(o_lo[:, hp, :], ps[:, AV + hp, :], bf[:, B_V + 2 * hg + hp:B_V + 2 * hg + hp + 1],
                                                 o_hi[:, hp, :].bitcast(F32), ALU.add, ALU.subtract).then_inc(o_lo_ready, 1)

                def body(i, last):
                    for m in range(3):
                        acted(i, m)
                        dve.scalar_tensor_tensor(c_lo[:, m, :], ps[:, m % 2, :], bf[:, B_CONV + m:B_CONV + m + 1],
                                                 c_hi[:, m, :].bitcast(F32), ALU.add, ALU.subtract).then_inc(mm_dve, 1)
                    kv(i, 0)
                    for s in range(STEPS + 3):
                        if s % NBLK == 3 and s // NBLK + 1 < NHG:
                            kv(i, s // NBLK + 1)
                        if s < STEPS:
                            maxes(i, s)
                        if 1 <= s <= STEPS:
                            recips(i, s - 1)
                        if 2 <= s < STEPS + 2:
                            probT_copy(i, s - 2)
                        if s == 3:
                            router(i)
                        if s % NBLK == 2 and s >= 6:
                            o_los(i, (s - 6) // NBLK)
                    if not last:
                        norm_pair(2 * i + 2, False)
                    acted(i, U_HT)
                    dve.tensor_tensor(hT_lo[:], ps[:, U_HT % 2, :], hT_hi[:].bitcast(F32), ALU.subtract).then_inc(mm_dve, 1)
                    dve.wait_ge(a_hi_ready, i + 1)
                    dve.scalar_tensor_tensor(a_lo[:], ps[:, WO, :], bf[:, B_O:B_O + 1], a_hi[:].bitcast(F32), ALU.add, ALU.subtract).then_inc(a_lo_ready, 1)
                    for t in range(NT):
                        full(i, U_X1 + t)
                        dve.wait_ge(res_ready, NT * i + t + 1)
                        dve.tensor_tensor(xres[:, t % 2, :], ps[:, (U_X1 + t) % 2, :], xres[:, t % 2, :], ALU.add).then_inc(x1_ready, 1)
                    if not last:
                        norm_pair(2 * i + 3, False)
                        xT_lo_copy(i + 1)

                norm_pair(0, True)
                with dve.Fori(0, N_WCH // 2) as j:
                    for s in range(2):
                        dve.wait_ge(w_hi_ready, 2 * j + s + 1)
                        c = bass.ds((2 * j + s) * WCH, WCH)
                        dve.tensor_tensor(w_lo[:, c], stage[:, s, 0:WCH], w_hi[:, c].bitcast(F32), ALU.subtract).then_inc(w_lo_ready, 1)
                norm_pair(1, True)
                dve.wait_ge(const_in, 16 * 7)
                dve.wait_ge(zeroed, 5)
                xT_lo_copy(0)
                body(0, False)
                with dve.Fori(1, NSEQ - 1) as i:
                    body(i, False)
                body(NSEQ - 1, True)

            @block.tensor
            def _(pe):
                def take(i, u):
                    pe.wait_ge(mm_act, ACT_USES * i + (freed("A", u - 1) if u >= 2 else 0))
                    n = [e for k, (w, e) in enumerate(USES[:max(0, u - 1)]) if "D" in e and w != "x1"]
                    pe.wait_ge(mm_dve, (DVE_USES - NT) * i + len(n))
                    pe.wait_ge(x1_ready, NT * i + max(0, u - 1 - U_X1))

                def transposes_in(i):
                    for t in range(NT):
                        pe.wait_ge(xn_ready, NT * i + t + 1)
                        for k in range(KD):
                            last = pe.transpose(ps[:, XT_BANKS[k], t * P:(t + 1) * P], xin[:, t % 2, k * P:(k + 1) * P], idf[:])
                        last.then_inc(xt_done, 1)

                def mm_done(ins):
                    ins.then_inc(mm_full, 1)

                def qkv(i, hg):
                    for n, c0 in ((0, C_WQ), (1, C_WK)):
                        for hp in range(2):
                            u = use_act(hg, 2 * n + hp)
                            take(i, u)
                            mm_done(split3(pe, ps[:, u % 2, :], wt(c0 + (2 * hg + hp) * P, P), (c_hi[:, n, :], c_lo[:, n, :]), True, True))
                    for half in range(2):
                        u = use_act(hg, 4 + half)
                        take(i, u)
                        for b in range(2):
                            tok = slice((2 * half + b) * P, (2 * half + b + 1) * P)
                            last = split3(pe, ps[:, u % 2, b * 256:(b + 1) * 256], (c_hi[:, 2, tok], c_lo[:, 2, tok]),
                                          wt(C_WV + hg * HG * DH0, HG * DH0), True, True)
                        mm_done(last)

                def scores(i, s):
                    hg, b = s // NBLK, s % NBLK
                    if b == 0:
                        pe.wait_ge(mm_act, ACT_USES * i + freed("A", use_act(hg, 3) + 1))
                        pe.wait_ge(mm_dve, (DVE_USES - NT) * i + freed("D", use_act(hg, 3) + 1))
                    pe.wait_ge(exp_done, STEPS * i + max(0, s - 1))
                    bank = ps[:, SC + s % 2, :]
                    pe.matmul(bank, idb[:], neg[:], start=True, stop=False, skip_group_check=True)
                    for hp in range(2):
                        last = pe.matmul(bank[:, hp * 256:(hp + 1) * 256], qh[:, hg % 2, hp, b * P:(b + 1) * P],
                                         kh[:, hg % 2, hp, :, b * P:(b + 1) * P], start=False, stop=(hp == 1), skip_group_check=True)
                    last.then_inc(sc_full, 1)

                def transposes(i, s):
                    pe.wait_ge(prob_ready, STEPS * i + s + 1)
                    pe.wait_ge(probT_ready, STEPS * i + s)
                    for h in range(HG):
                        last = pe.transpose(ps[:, PT, h * P:(h + 1) * P], prob[:, s % 3, h * P:(h + 1) * P], idf[:])
                    last.then_inc(tr_full, 1)

                def weighted(i, s):
                    hg, b = s // NBLK, s % NBLK
                    pe.wait_ge(probT_ready, STEPS * i + s + 1)
                    if b == 0:
                        pe.wait_ge(mm_dve, (DVE_USES - NT) * i + freed("D", use_act(hg, 5) + 1))
                        pe.wait_ge(o_lo_ready, 2 * NHG * i + 2 * hg)
                    for h in range(HG):
                        r = DH0 * (h % 2)
                        last = pe.matmul(ps[r:r + DH0, AV + h // 2, b * P:(b + 1) * P], vh[:, hg % 2, b, h * DH0:(h + 1) * DH0],
                                         probT[:, s % 2, h * P:(h + 1) * P], start=True, stop=True, skip_group_check=True)
                    last.then_inc(av_done, 1)

                def out_proj(i, hg):
                    pe.wait_ge(o_lo_ready, 2 * NHG * i + 2 * hg + 2)
                    if hg == 0:
                        pe.wait_ge(a_lo_ready, i)
                    for hp in range(2):
                        last = split3(pe, ps[:, WO, :], wt(C_WO + (2 * hg + hp) * W, W), (o_hi[:, hp, :], o_lo[:, hp, :]),
                                      hg == 0 and hp == 0, hg == NHG - 1 and hp == 1)
                    last.then_inc(wo_done, 1)

                def body(i, last_seq):
                    pe.wait_ge(xT_lo_ready, KD * i + KD)
                    pe.wait_ge(w_lo_ready, -(-C_WQ // WCH))
                    for m in range(3):
                        take(i, m)
                        for j in range(TAPS):
                            for k in range(KD):
                                last = split3(pe, ps[:, m % 2, :], wt(C_CONV + (j * KD + k) * 3 * W + m * P, P),
                                              (xT_hi[:, k, j:j + L], xT_lo[:, k, j:j + L]), j + k == 0, j == TAPS - 1 and k == KD - 1)
                        mm_done(last)
                    pe.wait_ge(w_lo_ready, N_WCH)
                    for t in range(NT):
                        u = U_AR + t
                        take(i, u)
                        for k in range(KD):
                            tok = slice(1 + t * P, 1 + (t + 1) * P)
                            last = split3(pe, ps[:, u % 2, 0:AR], (xT_hi[:, k, tok], xT_lo[:, k, tok]), wt(C_AR + k * AR, AR), k == 0, k == KD - 1)
                        mm_done(last)
                    qkv(i, 0)
                    for s in range(STEPS + 3):
                        if s % NBLK == 3 and s // NBLK + 1 < NHG:
                            qkv(i, s // NBLK + 1)
                        if s < STEPS:
                            scores(i, s)
                        if 2 <= s < STEPS + 2:
                            transposes(i, s - 2)
                        if s % NBLK == 3 and s >= 7:
                            out_proj(i, (s - 7) // NBLK)
                        if 3 <= s:
                            weighted(i, s - 3)
                    take(i, U_HT)
                    pe.wait_ge(comb_ready, NT * i + NT)
                    for t in range(NT):
                        last = pe.transpose(ps[:, U_HT % 2, t * P:(t + 1) * P], har[:, t, 0:ER], idf[:])
                    mm_done(last)
                    for t in range(NT):
                        u = U_X1 + t
                        take(i, u)
                        tok = slice(1 + t * P, 1 + (t + 1) * P)
                        ts = slice(t * P, (t + 1) * P)
                        for k in range(KD):
                            split3(pe, ps[:, u % 2, :], (xT_hi[:, k, tok], xT_lo[:, k, tok]), wt(C_BASE + k * D, D), k == 0, False)
                        if t == 0:
                            out_proj(i, NHG - 1)
                            pe.wait_ge(mm_dve, (DVE_USES - NT) * i + freed("D", U_HT + 1))
                        split3(pe, ps[:, u % 2, :], (hT_hi[:, ts], hT_lo[:, ts]), wt(C_B, D), False, False)
                        if t == 0:
                            pe.wait_ge(a_lo_ready, i + 1)
                        mm_done(split3(pe, ps[:, u % 2, :], (a_hi[:, ts], a_lo[:, ts]), wt(C_PROJ, D), False, True))
                    if not last_seq:
                        transposes_in(i + 1)

                pe.wait_ge(const_in, 16 * 7)
                pe.wait_ge(zeroed, 5)
                transposes_in(0)
                body(0, False)
                with pe.Fori(1, NSEQ - 1) as i:
                    body(i, False)
                body(NSEQ - 1, True)


N_B = KD * 3 * D
WCH1 = 768
N_WCH1 = N_B // WCH1
QPARTS = (0, 0, 0, 1, 1, 2)
KPARTS = (0, 1, 2, 0, 1, 0)
KS = len(QPARTS) * DH1
TPG = 4
NG = P // TPG
NCH = NT
HB = NG // 2
OB = 4
OA = NG // OB


def attention1(nc, x1_dram, w1, bias_f, bv1, ident, q3, k3, v3, xT_dram, ctx_dram):
    with ExitStack() as ctx:
        def sb(name, shape, dt=F32):
            return ctx.enter_context(nc.sbuf_tensor(name, shape, dt))

        def sem(name):
            return ctx.enter_context(nc.semaphore(name))

        w_hi = sb("w1_hi", [P, N_B], F32R)
        w_lo = sb("w1_lo", [P, N_B], F32R)
        stage = sb("stage1", [P, 2, WCH1])
        xin = sb("xin1", [P, NT, D])
        xT_hi = sb("xT1_hi", [P, KD, L], F32R)
        xT_lo = sb("xT1_lo", [P, KD, L], F32R)
        rf = sb("rf", [P, 2, L])
        yf = sb("yf", [P, 2, D])
        qk3 = sb("qk3", [P, 2, 3, L], BF16)
        vp3 = sb("vp3", [P, 2, H1, 3, DH1], BF16)
        qb = sb("qb", [KS, 2, H1, P], BF16)
        kb = sb("kb", [KS, 2, H1, P], BF16)
        vb = sb("vb", [P, 2, NG, 2, TPG, 2, DH1], BF16)
        S = sb("S", [P, 2, NG, H1])
        T = sb("T", [P, NG * H1])
        pp = sb("pp", [P, 2, 3, NG * H1], BF16)
        osb = sb("osb", [P, OA, OB, H1])
        cx = sb("cx", [P, 2, NG, DH1])
        bf = sb("bf1", [P, N_BF])
        bvb = sb("bvb", [P, D])
        idf = sb("idf1", [P, P])
        mx = sb("mx1", [P, NG])
        sm = sb("sm1", [P, NG])
        rs = sb("rs1", [P, NG])
        stats = sb("stats1", [P, NT, 6])
        mv = sb("mv1", [P, NT, 2])
        veps = sb("veps1", [P, NT])
        rstd = sb("rstd1", [P, NT])
        mhalf = sb("mhalf1", [P, NT])
        ps = ctx.enter_context(nc.psum_tensor("ps1", [P, 8, 512], F32))
        MM, SC, OUT, TR = 0, 2, 4, 6

        const_in, carrier = sem("const1_in"), sem("carrier1")
        w_in = [sem(f"w1_in{s}") for s in range(2)]
        x_in = sem("x1_in")
        qk_out = [sem(f"qk_out{s}") for s in range(2)]
        v_out = [sem(f"v_out{s}") for s in range(2)]
        xT_out = sem("xT_out")
        qk_in = [sem(f"qk_in{s}") for s in range(2)]
        v_in = [sem(f"v_in{s}") for s in range(2)]
        cx_out = [sem(f"cx_out{s}") for s in range(2)]
        names = ("w_hi_ready1 w_lo_ready1 zeroed1 mhalf_set1 st_done1 ve_ready1 rstd_ready1 xn_ready1 xt_done1 xT_hi_ready1 "
                 "xT_lo_ready1 mm_full1 hi_ready r_ready mid_ready lo_ready y_ready sc_full1 mx_ready1 sub_ready exp_ready "
                 "sum_ready rs_ready p_ready T_ready ph_ready T_rest pm_ready pl_ready av_done1 o_ready otr_full cx_ready")
        s_ = {n: sem(n) for n in names.split()}

        def carry(eng):
            eng.sem_inc(carrier, 1)

        NU = 12

        with nc.Block() as block:

            @block.sync
            def _(sp):
                sp.dma_start(bf[:], bias_f).then_inc(const_in, 16)
                sp.dma_start(idf[:], ident).then_inc(const_in, 16)
                sp.dma_start(bvb[:], bass.AP(bv1.tensor, 0, [[0, P], [1, D]])).then_inc(const_in, 16)
                for j in range(N_WCH1):
                    s = j % 2
                    if j >= 2:
                        sp.wait_ge(s_["w_hi_ready1"], j - 1)
                        sp.wait_ge(s_["w_lo_ready1"], j - 1)
                    sp.dma_start(stage[:, s, :], w1[:, j * WCH1:(j + 1) * WCH1]).then_inc(w_in[s], 16)

                def load_qk(a, c):
                    s = c % 2
                    sp.wait_ge(s_["sc_full1"], NCH * a + max(0, c - 1))
                    for dst, src, parts in ((qb, q3, QPARTS), (kb, k3, KPARTS)):
                        for j, part in enumerate(parts):
                            view = src[bass.ds(a, 1), part, :, c * P:(c + 1) * P].rearrange("o (h d) t -> d (o h) t", d=DH1)
                            sp.dma_start(dst[DH1 * j:DH1 * (j + 1), s, :, :], view).then_inc(qk_in[s], 16)

                def load_v(a, c):
                    s = c % 2
                    sp.wait_ge(s_["av_done1"], NCH * a + max(0, c - 1))
                    for q in range(TPG):
                        view = v3[bass.ds(a, 1), c * P:(c + 1) * P, :, :].rearrange("o (g q) t n -> (o q) t g n", q=TPG)[q]
                        own = vb[32 * q:32 * q + 32, s, :, :, q, :, :]
                        sp.dma_start(own[:, :, 0, :, :].rearrange("t g w d -> t g (w d)"), view[:, :, 0:2 * DH1]).then_inc(v_in[s], 16)
                        sp.dma_start(own[:, :, 1, 0, :], view[:, :, 2 * DH1:3 * DH1]).then_inc(v_in[s], 16)

                def store_ctx(a, c):
                    sp.wait_ge(s_["cx_ready"], 2 * NCH * a + 2 * c + 2)
                    for b in range(OB):
                        view = ctx_dram[bass.ds(a, 1), c * P + b * NG:c * P + (b + 1) * NG, :].rearrange("o t (h d) -> h (o t) d", d=DH1)
                        sp.dma_start(view, cx[32 * b:32 * b + 32, c % 2, :, :]).then_inc(cx_out[c % 2], 16)

                def store_qkv(i, u):
                    sp.wait_ge(s_["lo_ready"], NU * i + u + 1)
                    if u < 8:
                        dst = q3 if u < 4 else k3
                        view = dst[bass.ds(i, 1), :, (u % 4) * P:(u % 4 + 1) * P, :].rearrange("o w p t -> p (o w) t")
                        sp.dma_start(view, qk3[:, u % 2, :, :]).then_inc(qk_out[u % 2], 16)
                    else:
                        t = u - 8
                        view = v3[bass.ds(i, 1), t * P:(t + 1) * P, :, :].rearrange("o p t n -> (o p) t n")
                        sp.dma_start(view, vp3[:, u % 2, :, :, :].rearrange("p t w d -> p t (w d)")).then_inc(v_out[u % 2], 16)

                def body(i, qkv, att):
                    if qkv:
                        sp.wait_ge(s_["xt_done1"], KD * i)
                        sp.dma_start(xin[:], x1_dram[bass.ds(i * L, L), :].rearrange("(t p) d -> p t d", p=P)).then_inc(x_in, 16)
                    if att:
                        for s in range(2):
                            sp.wait_ge(qk_out[s], 64 * i)
                            carry(sp)
                            sp.wait_ge(v_out[s], 32 * i)
                        for c in range(2):
                            load_qk(i - 1, c)
                            load_v(i - 1, c)
                    if qkv:
                        sp.wait_ge(s_["xT_lo_ready1"], KD * i + KD)
                        sp.dma_start(xT_dram[bass.ds(i, 1), 0, :, :].rearrange("o p n -> (o p) n"), xT_hi[:].rearrange("p k t -> p (k t)").bitcast(F32)).then_inc(xT_out, 16)
                        sp.dma_start(xT_dram[bass.ds(i, 1), 1, :, :].rearrange("o p n -> (o p) n"), xT_lo[:].rearrange("p k t -> p (k t)").bitcast(F32)).then_inc(xT_out, 16)
                    for c in range(NCH):
                        if att and 1 <= c < NCH - 1:
                            load_qk(i - 1, c + 1)
                        if qkv:
                            for u in range(3 * c, 3 * c + 3):
                                store_qkv(i, u)
                        if att and 1 <= c < NCH - 1:
                            load_v(i - 1, c + 1)
                        if att and c >= 2:
                            store_ctx(i - 1, c - 2)
                    if att:
                        store_ctx(i - 1, NCH - 2)
                        store_ctx(i - 1, NCH - 1)

                body(0, True, False)
                body(1, True, True)
                with sp.Fori(2, NSEQ) as i:
                    body(i, True, True)
                body(NSEQ, False, True)
                sp.wait_ge(xT_out, 32 * NSEQ)
                for s in range(2):
                    sp.wait_ge(cx_out[s], 16 * OB * NCH // 2 * NSEQ)

            @block.gpsimd
            def _(pool):
                pool.memset(mhalf[:], -0.5).then_inc(s_["mhalf_set1"], 1)
                pool.memset(vb[:].rearrange("p s g n q w d -> p (s g n q w d)").bitcast(U32), 0).then_inc(s_["zeroed1"], 1)
                pool.wait_ge(s_["mhalf_set1"], 1)

                def normalise(a, c):
                    pool.wait_ge(s_["rs_ready"], NCH * a + c + 1)
                    v = S[:, c % 2, :, :]
                    pool.tensor_tensor(v, v, spread(rs[:], H1), ALU.mult).then_inc(s_["p_ready"], 1)

                def last_part(a, c):
                    pool.wait_ge(s_["pm_ready"], NCH * a + c + 1)
                    pool.tensor_tensor(pp[:, c % 2, 2, :], T[:], pp[:, c % 2, 1, :], ALU.subtract).then_inc(s_["pl_ready"], 1)

                def parts(i, u):
                    if u >= 8:
                        pool.wait_ge(s_["hi_ready"], NU * i + u + 1)
                        rv = rf[:, u % 2, :].rearrange("p (t d) -> p t d", d=DH1)
                        pool.tensor_tensor(rv, yf[:, u % 2, :].rearrange("p (t d) -> p t d", d=DH1), vp3[:, u % 2, :, 0, :], ALU.subtract).then_inc(s_["r_ready"], 1)
                    pool.wait_ge(s_["mid_ready"], NU * i + u + 1)
                    if u < 8:
                        pool.tensor_tensor(qk3[:, u % 2, 2, :], rf[:, u % 2, :], qk3[:, u % 2, 1, :], ALU.subtract).then_inc(s_["lo_ready"], 1)
                    else:
                        rv = rf[:, u % 2, :].rearrange("p (t d) -> p t d", d=DH1)
                        pool.tensor_tensor(vp3[:, u % 2, :, 2, :], rv, vp3[:, u % 2, :, 1, :], ALU.subtract).then_inc(s_["lo_ready"], 1)

                def body(i, qkv, att):
                    if qkv:
                        pool.wait_ge(s_["ve_ready1"], i + 1)
                        pool.tensor_tensor(rstd[:], veps[:], mhalf[:], ALU.pow).then_inc(s_["rstd_ready1"], 1)
                    for c in range(NCH):
                        if qkv:
                            for u in range(3 * c, 3 * c + 3):
                                parts(i, u)
                        if att:
                            normalise(i - 1, c)
                            last_part(i - 1, c)

                body(0, True, False)
                body(1, True, True)
                with pool.Fori(2, NSEQ) as i:
                    body(i, True, True)
                body(NSEQ, False, True)

            @block.scalar
            def _(act):
                for j in range(N_WCH1):
                    act.wait_ge(w_in[j % 2], 16 * (j // 2) + 16)
                    act.activation(w_hi[:, j * WCH1:(j + 1) * WCH1], stage[:, j % 2, :], ACT.Copy).then_inc(s_["w_hi_ready1"], 1)
                act.wait_ge(const_in, 48)

                def first_part(i, u):
                    s = u % 2
                    if u < 8:
                        act.wait_ge(s_["mm_full1"], NU * i + u + 1)
                        act.wait_ge(qk_out[s], 64 * i + 16 * (u // 2))
                        act.activation(qk3[:, s, 0, :], ps[:, MM + s, :], ACT.Identity, bias=bf[:, B_Q1 + u:B_Q1 + u + 1]).then_inc(s_["hi_ready"], 1)
                    else:
                        act.wait_ge(s_["y_ready"], 4 * i + u - 8 + 1)
                        act.wait_ge(v_out[s], 32 * i + 16 * ((u - 8) // 2))
                        act.activation(vp3[:, s, :, 0, :], yf[:, s, :].rearrange("p (t d) -> p t d", d=DH1), ACT.Copy).then_inc(s_["hi_ready"], 1)

                def mid_part(i, u):
                    s = u % 2
                    act.wait_ge(s_["r_ready"], NU * i + u + 1)
                    if u < 8:
                        act.activation(qk3[:, s, 1, :], rf[:, s, :], ACT.Copy).then_inc(s_["mid_ready"], 1)
                    else:
                        act.activation(vp3[:, s, :, 1, :], rf[:, s, :].rearrange("p (t d) -> p t d", d=DH1), ACT.Copy).then_inc(s_["mid_ready"], 1)

                def exps(a, c):
                    act.wait_ge(s_["sub_ready"], 2 * NCH * a + 2 * c + 2)
                    v = S[:, c % 2, :, :].rearrange("p g t -> p (g t)")
                    act.activation(v, v, ACT.Exp, scale=DH1 ** -0.5).then_inc(s_["exp_ready"], 1)

                def prob_parts(a, c):
                    act.wait_ge(s_["T_ready"], NCH * a + c + 1)
                    act.wait_ge(s_["av_done1"], NCH * a + max(0, c - 1))
                    act.activation(pp[:, c % 2, 0, :], T[:], ACT.Copy).then_inc(s_["ph_ready"], 1)
                    act.wait_ge(s_["T_rest"], NCH * a + c + 1)
                    act.activation(pp[:, c % 2, 1, :], T[:], ACT.Copy).then_inc(s_["pm_ready"], 1)

                def o_copy(a, c):
                    act.wait_ge(s_["av_done1"], NCH * a + c + 1)
                    act.wait_ge(s_["otr_full"], NCH * a + c)
                    for hf in range(2):
                        act.activation(osb[:, :, 2 * hf:2 * hf + 2, :].rearrange("p a b h -> p b a h"),
                                       ps[:, OUT + hf, :].rearrange("p (b a h) -> p b a h", b=2, h=H1), ACT.Copy).then_inc(s_["o_ready"], 1)

                def body(i, qkv, att):
                    if att:
                        exps(i - 1, 0)
                    if qkv:
                        act.wait_ge(xT_out, 32 * i)
                        act.wait_ge(s_["mm_full1"], NU * i)
                        for k in range(KD):
                            act.wait_ge(s_["xt_done1"], KD * i + k + 1)
                            act.activation(xT_hi[:, k, :], ps[:, MM + k % 2, :], ACT.Copy).then_inc(s_["xT_hi_ready1"], 1)
                    for c in range(NCH):
                        if qkv:
                            u = 3 * c
                            first_part(i, u)
                            first_part(i, u + 1)
                            mid_part(i, u)
                            mid_part(i, u + 1)
                            first_part(i, u + 2)
                            mid_part(i, u + 2)
                        if att:
                            if c >= 1:
                                o_copy(i - 1, c - 1)
                            if c + 1 < NCH:
                                exps(i - 1, c + 1)
                            prob_parts(i - 1, c)
                    if att:
                        o_copy(i - 1, NCH - 1)

                body(0, True, False)
                body(1, True, True)
                with act.Fori(2, NSEQ) as i:
                    body(i, True, True)
                body(NSEQ, False, True)

            @block.vector
            def _(dve):
                for j in range(N_WCH1):
                    dve.wait_ge(s_["w_hi_ready1"], j + 1)
                    c = slice(j * WCH1, (j + 1) * WCH1)
                    dve.tensor_tensor(w_lo[:, c], stage[:, j % 2, :], w_hi[:, c].bitcast(F32), ALU.subtract).then_inc(s_["w_lo_ready1"], 1)
                dve.wait_ge(const_in, 48)

                def norm(i):
                    dve.wait_ge(x_in, 16 * i + 16)
                    for t in range(NT):
                        dve.bn_stats(stats[:, t, :], xin[:, t, :]).then_inc(s_["st_done1"], 1)
                    for t in range(NT):
                        dve.wait_ge(s_["st_done1"], 2 * NT * i + NT)
                        carry(dve)
                        dve.bn_aggr(mv[:, t, :], stats[:, t, :]).then_inc(s_["st_done1"], 1)
                    dve.wait_ge(s_["st_done1"], 2 * NT * i + 2 * NT)
                    dve.tensor_scalar(veps[:], mv[:, :, 1], EPS, None, ALU.add).then_inc(s_["ve_ready1"], 1)
                    dve.wait_ge(s_["rstd_ready1"], i + 1)
                    for t in range(NT):
                        dve.tensor_scalar(xin[:, t, :], xin[:, t, :], mv[:, t, 0:1], rstd[:, t:t + 1], ALU.subtract, ALU.mult).then_inc(s_["xn_ready1"], 1)
                    for k in range(KD):
                        dve.wait_ge(s_["xT_hi_ready1"], KD * i + k + 1)
                        dve.tensor_tensor(xT_lo[:, k, :], ps[:, MM + k % 2, :], xT_hi[:, k, :].bitcast(F32), ALU.subtract).then_inc(s_["xT_lo_ready1"], 1)

                def rest(i, u):
                    s = u % 2
                    dve.wait_ge(s_["lo_ready"], NU * i + max(0, u - 1))
                    if u < 8:
                        dve.wait_ge(s_["hi_ready"], NU * i + u + 1)
                        dve.scalar_tensor_tensor(rf[:, s, :], ps[:, MM + s, :], bf[:, B_Q1 + u:B_Q1 + u + 1], qk3[:, s, 0, :], ALU.add, ALU.subtract).then_inc(s_["r_ready"], 1)
                    else:
                        dve.wait_ge(s_["mm_full1"], NU * i + u + 1)
                        dve.tensor_tensor(yf[:, s, :], ps[:, MM + s, :], bvb[:], ALU.add).then_inc(s_["y_ready"], 1)

                def max_sub(a, c):
                    dve.wait_ge(s_["sc_full1"], NCH * a + c + 1)
                    for hf in range(2):
                        g = slice(hf * HB, (hf + 1) * HB)
                        v = ps[:, SC + hf, :].rearrange("p (g t) -> p g t", t=H1)
                        dve.tensor_reduce(mx[:, g], v, AX_X, ALU.max).then_inc(s_["mx_ready1"], 1)
                    for hf in range(2):
                        g = slice(hf * HB, (hf + 1) * HB)
                        v = ps[:, SC + hf, :].rearrange("p (g t) -> p g t", t=H1)
                        dve.wait_ge(s_["mx_ready1"], 2 * NCH * a + 2 * c + 2)
                        dve.tensor_tensor(S[:, c % 2, g, :], v, spread(mx[:, g], H1), ALU.subtract).then_inc(s_["sub_ready"], 1)

                def sums(a, c):
                    dve.wait_ge(s_["exp_ready"], NCH * a + c + 1)
                    dve.tensor_reduce(sm[:], S[:, c % 2, :, :], AX_X, ALU.add).then_inc(s_["sum_ready"], 1)
                    dve.wait_ge(s_["sum_ready"], NCH * a + c + 1)
                    dve.wait_ge(s_["p_ready"], NCH * a + c)
                    dve.reciprocal(rs[:], sm[:]).then_inc(s_["rs_ready"], 1)

                def turn(a, c):
                    dve.wait_ge(s_["p_ready"], NCH * a + c + 1)
                    dve.wait_ge(s_["pl_ready"], NCH * a + c)
                    dve.transpose(T[:], S[:, c % 2, :, :].rearrange("p g t -> p (g t)")).then_inc(s_["T_ready"], 1)
                    dve.wait_ge(s_["ph_ready"], NCH * a + c + 1)
                    dve.tensor_tensor(T[:], T[:], pp[:, c % 2, 0, :], ALU.subtract).then_inc(s_["T_rest"], 1)

                def fold(a, c):
                    dve.wait_ge(s_["otr_full"], NCH * a + c + 1)
                    dve.wait_ge(cx_out[c % 2], 16 * OB * (2 * a + c // 2))
                    for hf in range(2):
                        v = ps[:, TR + hf, :].rearrange("p (n w d) -> p n d w", w=2, d=DH1)
                        dve.tensor_reduce(cx[:, c % 2, hf * HB:(hf + 1) * HB, :], v, AX_X, ALU.add).then_inc(s_["cx_ready"], 1)

                def body(i, qkv, att):
                    if att:
                        max_sub(i - 1, 0)
                    if qkv:
                        norm(i)
                    for c in range(NCH):
                        if att:
                            sums(i - 1, c)
                        if qkv:
                            for u in range(3 * c, 3 * c + 3):
                                rest(i, u)
                        if att:
                            if c + 1 < NCH:
                                max_sub(i - 1, c + 1)
                            turn(i - 1, c)
                            if c >= 2:
                                fold(i - 1, c - 2)
                    if att:
                        fold(i - 1, NCH - 2)
                        fold(i - 1, NCH - 1)

                body(0, True, False)
                body(1, True, True)
                with dve.Fori(2, NSEQ) as i:
                    body(i, True, True)
                body(NSEQ, False, True)

            @block.tensor
            def _(pe):
                def transposes_in(i):
                    pe.wait_ge(s_["xn_ready1"], NT * i + NT)
                    for k in range(KD):
                        if k < 2:
                            pe.wait_ge(s_["y_ready"], 4 * i)
                        else:
                            pe.wait_ge(s_["xT_lo_ready1"], KD * i + k - 1)
                        for t in range(NT):
                            last = pe.transpose(ps[:, MM + k % 2, t * P:(t + 1) * P], xin[:, t, k * P:(k + 1) * P], idf[:])
                        last.then_inc(s_["xt_done1"], 1)

                def project(i, u):
                    if u < 2:
                        pe.wait_ge(s_["xT_lo_ready1"], KD * i + KD)
                    elif u < 10:
                        pe.wait_ge(s_["r_ready"], NU * i + u - 1)
                    else:
                        pe.wait_ge(s_["y_ready"], 4 * i + u - 9)
                    for k in range(KD):
                        if u < 8:
                            c = k * 3 * D + u * P
                            last = split3(pe, ps[:, MM + u % 2, :], (w_hi[:, c:c + P], w_lo[:, c:c + P]), (xT_hi[:, k, :], xT_lo[:, k, :]), k == 0, k == KD - 1)
                        else:
                            c = k * 3 * D + 2 * D
                            t = slice((u - 8) * P, (u - 7) * P)
                            last = split3(pe, ps[:, MM + u % 2, :], (xT_hi[:, k, t], xT_lo[:, k, t]), (w_hi[:, c:c + D], w_lo[:, c:c + D]), k == 0, k == KD - 1)
                    last.then_inc(s_["mm_full1"], 1)

                def scores(a, c):
                    s = c % 2
                    pe.wait_ge(qk_in[s], 16 * 12 * (2 * a + c // 2 + 1))
                    pe.wait_ge(s_["sub_ready"], 2 * NCH * a + 2 * c)
                    for g in range(NG):
                        for q in range(TPG):
                            t = TPG * g + q
                            col = (g % HB) * H1
                            last = pe.matmul(ps[32 * q:32 * q + 32, SC + g // HB, col:col + H1], qb[:, s, :, t], kb[:, s, :, t],
                                             start=True, stop=True, skip_group_check=True)
                    last.then_inc(s_["sc_full1"], 1)

                def weighted(a, c):
                    s = c % 2
                    pe.wait_ge(s_["pl_ready"], NCH * a + c + 1)
                    pe.wait_ge(v_in[s], 16 * 8 * (2 * a + c // 2 + 1))
                    pe.wait_ge(s_["o_ready"], 2 * NCH * a + 2 * c)
                    for g in range(NG):
                        out = ps[:, OUT + g // HB, (g % HB) * H1:(g % HB + 1) * H1]
                        p3 = [pp[:, s, w, g * H1:(g + 1) * H1] for w in range(3)]
                        v_hm, v_l0 = (vb[:, s, g, n, :, :, :].rearrange("p q w d -> p (q w d)") for n in range(2))
                        for w in range(3):
                            pe.matmul(out, v_hm, p3[w], start=(w == 0), stop=False, skip_group_check=True)
                        last = pe.matmul(out, v_l0, p3[0], start=False, stop=True, skip_group_check=True)
                    last.then_inc(s_["av_done1"], 1)

                def transposes_out(a, c):
                    pe.wait_ge(s_["o_ready"], 2 * NCH * a + 2 * c + 2)
                    pe.wait_ge(s_["cx_ready"], 2 * NCH * a + 2 * c)
                    for o in range(OA):
                        last = pe.transpose(ps[:, TR + o // 4, (o % 4) * P:(o % 4 + 1) * P], osb[:, o, :, :].rearrange("p b h -> p (b h)"), idf[:])
                    last.then_inc(s_["otr_full"], 1)

                def body(i, qkv, att):
                    if att:
                        scores(i - 1, 0)
                    if qkv:
                        transposes_in(i)
                    for c in range(NCH):
                        if qkv:
                            for u in range(3 * c, 3 * c + 3):
                                project(i, u)
                        if att:
                            if c + 1 < NCH:
                                scores(i - 1, c + 1)
                            if c >= 1:
                                weighted(i - 1, c - 1)
                            if c >= 2:
                                transposes_out(i - 1, c - 2)
                    if att:
                        weighted(i - 1, NCH - 1)
                        transposes_out(i - 1, NCH - 2)
                        transposes_out(i - 1, NCH - 1)

                pe.wait_ge(const_in, 48)
                pe.wait_ge(s_["w_lo_ready1"], N_WCH1)
                pe.wait_ge(s_["zeroed1"], 1)
                body(0, True, False)
                body(1, True, True)
                with pe.Fori(2, NSEQ) as i:
                    body(i, True, True)
                body(NSEQ, False, True)


INTER = 1376
FT = -(-INTER // P)
FR = INTER - (FT - 1) * P
CC = 256
NPACK = 8
G_GU, G_D = D // P, INTER // P


def gu_chunks():
    return [(c, min(CC, INTER - c)) for c in range(0, INTER, CC)]


def dequant(nc, w, qw_gu, qz_gu, sc_gu, gi_gu, qw_d, qz_d, sc_d, gi_d):
    gu_hi, gu_lo, d_hi, d_lo = w
    tables = [("gu", c, n) for c, n in gu_chunks()] + [("d", 0, D)]
    units = [(n, k) for n, (kind, _, _) in enumerate(tables) for k in range(KD if kind == "gu" else FT)]
    with ExitStack() as ctx:
        def sb(name, shape, dt=F32):
            return ctx.enter_context(nc.sbuf_tensor(name, shape, dt))

        def sem(name):
            return ctx.enter_context(nc.semaphore(name))

        stage = sb("stage2", [P, 2, 512], U32)
        nib = sb("nib", [P, 2, 512], U32)
        wz = sb("wz", [P, 2, 512])
        wf = sb("wf", [P, 2, 512])
        shift = sb("shift", [P, 1], U32)
        part = sb("part", [G_D, 1])
        gi = {"gu": sb("idx_gu", [G_GU, D], I32), "d": sb("idx_d", [G_D, INTER], I32)}
        gf = {"gu": sb("gf_gu", [G_GU, D]), "d": sb("gf_d", [G_D, INTER])}
        gn = {"gu": sb("gn_gu", [G_GU, D]), "d": sb("gn_d", [G_D, INTER])}
        hot = {"gu": sb("hot_gu", [G_GU, D], F32R), "d": sb("hot_d", [G_D, INTER], F32R)}
        hotb = {"gu": sb("hotb_gu", [G_GU, D], BF16), "d": sb("hotb_d", [G_D, INTER], BF16)}
        sraw = sb("sraw", [G_D, 2, 512])
        s_hi = sb("s_hi", [G_D, 2, 512], F32R)
        s_lo = sb("s_lo", [G_D, 2, 512], F32R)
        zraw = sb("zraw", [G_D, 2, 64], U32)
        znib = sb("znib", [G_D, 2, 512], U32)
        zt = sb("zt", [G_D, 2, 512], BF16)
        ps = ctx.enter_context(nc.psum_tensor("ps2", [P, 8, 512], F32))

        gi_in = sem("gi_in")
        q_in = [sem(f"q_in{s}") for s in range(2)]
        tab_in = [sem(f"tab_in{s}") for s in range(2)]
        iota_done, shift_done, hot_done = sem("iota_done"), sem("shift_done"), sem("hot_done")
        s_hi_done, s_lo_done, znib_done, z_done = sem("s_hi_done"), sem("s_lo_done"), sem("znib_done"), sem("z_done")
        nib_done, gathered, wz_done, wf_done = sem("nib_done"), sem("gathered"), sem("wz_done"), sem("wf_done")
        wq_hi_done, wq_lo_done = sem("wq_hi_done"), sem("wq_lo_done")

        def groups(n):
            return G_GU if tables[n][0] == "gu" else G_D

        def rows(u):
            n, k = units[u]
            return FR if tables[n][0] == "d" and k == FT - 1 else P

        def width(n):
            return 2 * tables[n][2] if tables[n][0] == "gu" else D

        def first_unit(n):
            return next(u for u, (m, _) in enumerate(units) if m == n)

        def pieces(n):
            kind, c, m = tables[n]
            return [(c, 0, m), (INTER + c, m, m)] if kind == "gu" else [(0, 0, D)]

        def out_pieces(u, hi):
            n, k = units[u]
            if tables[n][0] == "gu":
                t = gu_hi if hi else gu_lo
                _, c, m = tables[n]
                return t[:, k, :].rearrange("p (s n) -> p s n", s=2)[:, :, c:c + m], m
            t = d_hi if hi else d_lo
            return t[0:rows(u), k, :].rearrange("p (s n) -> p s n", s=2), D // 2

        with nc.Block() as block:

            @block.sync
            def _(sp):
                for kind, src, g, n in (("gu", gi_gu, G_GU, D), ("d", gi_d, G_D, INTER)):
                    sp.dma_start(gi[kind][:], bass.AP(src.tensor, 0, [[0, g], [1, n]])).then_inc(gi_in, 16)

                def table(n):
                    s, g = n % 2, groups(n)
                    if n >= 2:
                        sp.wait_ge(gathered, first_unit(n - 1))
                    sc, qz = (sc_gu, qz_gu) if tables[n][0] == "gu" else (sc_d, qz_d)
                    for c, t, m in pieces(n):
                        sp.dma_start(sraw[0:g, s, t:t + m], sc[:, c:c + m]).then_inc(tab_in[s], 16)
                        sp.dma_start(zraw[0:g, s, t // NPACK:(t + m) // NPACK], qz[:, c // NPACK:(c + m) // NPACK]).then_inc(tab_in[s], 16)

                table(0)
                for u, (n, k) in enumerate(units):
                    if k == 0 and n + 1 < len(tables):
                        table(n + 1)
                    qw = qw_gu if tables[n][0] == "gu" else qw_d
                    cols = qw.shape[1]
                    if u >= 2:
                        sp.wait_ge(nib_done, u - 1)
                    for c, t, m in pieces(n):
                        src = bass.AP(qw.tensor, (k * P // NPACK) * cols + c, [[cols, rows(u) // NPACK], [0, NPACK], [1, m]])
                        sp.dma_start(stage[0:rows(u), u % 2, t:t + m], src).then_inc(q_in[u % 2], 16)

            def loads(s, n_units):
                return sum(len(pieces(units[u][0])) for u in range(n_units) if u % 2 == s)

            def tab_loads(s, n_tabs):
                return sum(2 * len(pieces(n)) for n in range(n_tabs) if n % 2 == s)

            @block.gpsimd
            def _(pool):
                pool.iota(shift[:], [[0, 1]], base=0, channel_multiplier=4).then_inc(iota_done, 1)
                pool.iota(part[:], [[0, 1]], base=0, channel_multiplier=1, allow_small_or_imprecise_dtypes=True).then_inc(iota_done, 1)
                for u in range(len(units)):
                    pool.wait_ge(wq_hi_done, u + 1)
                    (hi, m), (lo, _) = out_pieces(u, True), out_pieces(u, False)
                    v = wf[0:rows(u), u % 2, 0:2 * m].rearrange("p (s n) -> p s n", s=2)
                    pool.tensor_tensor(lo, v, hi.bitcast(F32), ALU.subtract).then_inc(wq_lo_done, 1)

            @block.scalar
            def _(act):
                def table(n):
                    s, g = n % 2, groups(n)
                    act.wait_ge(tab_in[s], 16 * tab_loads(s, n + 1))
                    act.activation(s_hi[0:g, s, 0:width(n)], sraw[0:g, s, 0:width(n)], ACT.Copy).then_inc(s_hi_done, 1)

                table(0)
                for u, (n, k) in enumerate(units):
                    if k == 0 and n + 1 < len(tables):
                        table(n + 1)
                    act.wait_ge(wf_done, u + 1)
                    hi, m = out_pieces(u, True)
                    act.activation(hi, wf[0:rows(u), u % 2, 0:2 * m].rearrange("p (s n) -> p s n", s=2), ACT.Copy).then_inc(wq_hi_done, 1)

            @block.vector
            def _(dve):
                dve.wait_ge(iota_done, 2)
                dve.tensor_scalar(shift[:], shift[:], 31, None, ALU.bitwise_and).then_inc(shift_done, 1)
                dve.wait_ge(gi_in, 32)
                n_hot = [0]

                def step(ins):
                    n_hot[0] += 1
                    ins.then_inc(hot_done, 1)
                    dve.wait_ge(hot_done, n_hot[0])

                for kind, g in (("gu", G_GU), ("d", G_D)):
                    f, t = gf[kind], gn[kind]
                    step(dve.tensor_copy(f[:], gi[kind][:]))
                    step(dve.tensor_scalar(t[:], f[:], 0.0, float(g), ALU.is_lt, ALU.mult))
                    step(dve.tensor_tensor(f[:], f[:], t[:], ALU.add))
                    step(dve.tensor_scalar(f[:], f[:], 0.0, float(g - 1), ALU.max, ALU.min))
                    step(dve.tensor_scalar(hot[kind][:], f[:], part[0:g, :], None, ALU.is_equal))
                    step(dve.tensor_scalar(hotb[kind][:], f[:], part[0:g, :], None, ALU.is_equal))

                def table(n):
                    s, g, m = n % 2, groups(n), width(n)
                    dve.wait_ge(s_hi_done, n + 1)
                    dve.tensor_tensor(s_lo[0:g, s, 0:m], sraw[0:g, s, 0:m], s_hi[0:g, s, 0:m].bitcast(F32), ALU.subtract).then_inc(s_lo_done, 1)
                    zv = znib[0:g, s, 0:m].rearrange("g (c b) -> g c b", b=NPACK)
                    for b in range(NPACK):
                        dve.tensor_scalar(zv[:, :, b], zraw[0:g, s, 0:m // NPACK], 4 * b, 15, ALU.logical_shift_right, ALU.bitwise_and).then_inc(znib_done, 1)
                    dve.wait_ge(znib_done, NPACK * (n + 1))
                    dve.tensor_scalar(zt[0:g, s, 0:m], znib[0:g, s, 0:m], 1.0, None, ALU.add).then_inc(z_done, 1)

                def nibbles(u):
                    r, m = rows(u), width(units[u][0])
                    dve.wait_ge(q_in[u % 2], 16 * loads(u % 2, u + 1))
                    dve.wait_ge(wz_done, max(0, u - 1))
                    dve.tensor_scalar(nib[0:r, u % 2, 0:m], stage[0:r, u % 2, 0:m], shift[0:r, :], 15, ALU.logical_shift_right, ALU.bitwise_and).then_inc(nib_done, 1)

                dve.wait_ge(shift_done, 1)
                table(0)
                nibbles(0)
                for u, (n, k) in enumerate(units):
                    if k == 0 and n + 1 < len(tables):
                        table(n + 1)
                    if u + 1 < len(units):
                        nibbles(u + 1)
                    r, m = rows(u), width(n)
                    b = 2 * (u % 4)
                    dve.wait_ge(gathered, u + 1)
                    dve.wait_ge(nib_done, u + 1)
                    dve.tensor_tensor(wz[0:r, u % 2, 0:m], nib[0:r, u % 2, 0:m], ps[0:r, b + 1, 0:m], ALU.subtract).then_inc(wz_done, 1)
                    dve.wait_ge(wz_done, u + 1)
                    if u >= 2:
                        dve.wait_ge(wq_lo_done, u - 1)
                    dve.tensor_tensor(wf[0:r, u % 2, 0:m], wz[0:r, u % 2, 0:m], ps[0:r, b, 0:m], ALU.mult).then_inc(wf_done, 1)

            @block.tensor
            def _(pe):
                pe.wait_ge(hot_done, 12)
                for u, (n, k) in enumerate(units):
                    kind, s, g, r, m = tables[n][0], n % 2, groups(n), rows(u), width(n)
                    if k == 0:
                        pe.wait_ge(s_lo_done, n + 1)
                        pe.wait_ge(z_done, n + 1)
                    if u >= 4:
                        pe.wait_ge(wf_done, u - 3)
                    b = 2 * (u % 4)
                    oh = hot[kind][:, k * P:k * P + r]
                    pe.matmul(ps[0:r, b, 0:m], oh, s_hi[0:g, s, 0:m], start=True, stop=False)
                    pe.matmul(ps[0:r, b, 0:m], oh, s_lo[0:g, s, 0:m], start=False, stop=True)
                    pe.matmul(ps[0:r, b + 1, 0:m], hotb[kind][:, k * P:k * P + r], zt[0:g, s, 0:m], start=True, stop=True).then_inc(gathered, 1)


def feed_forward(nc, w, x1_dram, ctx_dram, xT_dram, out):
    gu_hi, gu_lo, d_hi, d_lo = w
    with ExitStack() as ctx:
        def sb(name, shape, dt=F32):
            return ctx.enter_context(nc.sbuf_tensor(name, shape, dt))

        def sem(name):
            return ctx.enter_context(nc.semaphore(name))

        xT_hi = sb("xT2_hi", [P, KD, L], F32R)
        xT_lo = sb("xT2_lo", [P, KD, L], F32R)
        th = sb("th", [P, 2, L])
        gs = sb("gs", [P, 2, L])
        hf = sb("hf", [P, 2, L])
        h_hi = sb("h_hi", [P, 2, L], F32R)
        h_lo = sb("h_lo", [P, 2, L], F32R)
        xa = sb("xa", [P, NT, D])
        xb = sb("xb", [P, NT, D])
        ps = ctx.enter_context(nc.psum_tensor("ps3", [P, 8, 512], F32))
        GATE, UP, ACC = 0, 2, 4

        xT_in, res_in, out_out = sem("xT2_in"), sem("res2_in"), sem("out_out")
        res_sum = sem("res_sum")
        gu_full, th_done, gs_done, hf_done = sem("gu_full"), sem("th_done"), sem("gs_done"), sem("hf_done")
        h_hi_done, h_lo_done = sem("h_hi_done"), sem("h_lo_done")
        down_done, y_done = sem("down_done"), sem("y_done")

        def rows(m):
            return FR if m == FT - 1 else P

        with nc.Block() as block:

            @block.sync
            def _(sp):
                def body(i):
                    sp.wait_ge(gu_full, FT * i)
                    for n, t in enumerate((xT_hi, xT_lo)):
                        sp.dma_start(t[:].rearrange("p k t -> p (k t)").bitcast(F32), xT_dram[bass.ds(i, 1), n, :, :].rearrange("o p n -> (o p) n")).then_inc(xT_in, 16)
                    sp.wait_ge(out_out, 64 * i)
                    for dst, src in ((xa, x1_dram), (xb, ctx_dram)):
                        sp.dma_start(dst[:], src[bass.ds(i * L, L), :].rearrange("(t p) d -> p t d", p=P)).then_inc(res_in, 16)
                    for t in range(NT):
                        sp.wait_ge(y_done, NT * i + t + 1)
                        sp.dma_start(out[bass.ds(i * L + t * P, P), :], xa[:, t, :]).then_inc(out_out, 16)

                body(0)
                with sp.Fori(1, NSEQ) as i:
                    body(i)
                sp.wait_ge(out_out, 64 * NSEQ)

            @block.gpsimd
            def _(pool):
                def body(i):
                    pool.wait_ge(res_in, 32 * i + 32)
                    for t in range(NT):
                        pool.tensor_tensor(xa[:, t, :], xa[:, t, :], xb[:, t, :], ALU.add).then_inc(res_sum, 1)
                    for m in range(FT):
                        r = rows(m)
                        pool.wait_ge(h_hi_done, FT * i + m + 1)
                        pool.tensor_tensor(h_lo[0:r, m % 2, :], hf[0:r, m % 2, :], h_hi[0:r, m % 2, :].bitcast(F32), ALU.subtract).then_inc(h_lo_done, 1)

                body(0)
                with pool.Fori(1, NSEQ) as i:
                    body(i)

            @block.scalar
            def _(act):
                def gate_tanh(i, m):
                    r = rows(m)
                    act.wait_ge(gu_full, FT * i + m + 1)
                    act.wait_ge(gs_done, FT * i + max(0, m - 1))
                    act.activation(th[0:r, m % 2, :], ps[0:r, GATE + m % 2, :], ACT.Tanh, scale=0.5).then_inc(th_done, 1)

                def body(i):
                    for m in range(FT):
                        r = rows(m)
                        gate_tanh(i, m)
                        act.wait_ge(hf_done, FT * i + m + 1)
                        act.wait_ge(down_done, FT * i + max(0, m - 1))
                        act.activation(h_hi[0:r, m % 2, :], hf[0:r, m % 2, :], ACT.Copy).then_inc(h_hi_done, 1)

                body(0)
                with act.Fori(1, NSEQ) as i:
                    body(i)

            @block.vector
            def _(dve):
                def body(i):
                    for m in range(FT):
                        r, s = rows(m), m % 2
                        dve.wait_ge(th_done, FT * i + m + 1)
                        dve.wait_ge(h_lo_done, FT * i + max(0, m - 1))
                        dve.scalar_tensor_tensor(gs[0:r, s, :], th[0:r, s, :], 1.0, ps[0:r, GATE + s, :], ALU.add, ALU.mult).then_inc(gs_done, 1)
                        dve.wait_ge(gs_done, FT * i + m + 1)
                        dve.scalar_tensor_tensor(hf[0:r, s, :], gs[0:r, s, :], 0.5, ps[0:r, UP + s, :], ALU.mult, ALU.mult).then_inc(hf_done, 1)
                    dve.wait_ge(res_sum, NT * i + NT)
                    for t in range(NT):
                        dve.wait_ge(down_done, FT * i + FT)
                        dve.tensor_tensor(xa[:, t, :], ps[:, ACC + t, :], xa[:, t, :], ALU.add).then_inc(y_done, 1)

                body(0)
                with dve.Fori(1, NSEQ) as i:
                    body(i)

            @block.tensor
            def _(pe):
                def gate_up(i, m):
                    r = rows(m)
                    pe.wait_ge(hf_done, FT * i + max(0, m - 1))
                    for bank, c0 in ((GATE, 0), (UP, INTER)):
                        c = slice(c0 + m * P, c0 + m * P + r)
                        for k in range(KD):
                            last = split3(pe, ps[0:r, bank + m % 2, :], (gu_hi[:, k, c], gu_lo[:, k, c]), (xT_hi[:, k, :], xT_lo[:, k, :]), k == 0, k == KD - 1)
                    last.then_inc(gu_full, 1)

                def body(i):
                    pe.wait_ge(xT_in, 32 * i + 32)
                    gate_up(i, 0)
                    for m in range(FT):
                        r, s = rows(m), m % 2
                        if m + 1 < FT:
                            gate_up(i, m + 1)
                        pe.wait_ge(h_lo_done, FT * i + m + 1)
                        if m == 0:
                            pe.wait_ge(y_done, NT * i)
                        for t in range(NT):
                            ts = slice(t * P, (t + 1) * P)
                            last = split3(pe, ps[:, ACC + t, :], (h_hi[0:r, s, ts], h_lo[0:r, s, ts]), (d_hi[0:r, m, :], d_lo[0:r, m, :]), m == 0, m == FT - 1)
                        last.then_inc(down_done, 1)

                body(0)
                with pe.Fori(1, NSEQ) as i:
                    body(i)


def block_kernel(nc, x, w0, bias_f, proj_b, base_b, w1, bv1, qw_gu, qz_gu, sc_gu, gi_gu, qw_d, qz_d, sc_d, gi_d,
                 ident, ident_bf, causal, iota8, out):
    def scratch(name, shape, dt=F32):
        return nc.dram_tensor(name, shape, dt, kind="Internal").ap()

    x1_dram = scratch("x1_dram", [NSEQ * L, D])
    ctx_dram = scratch("ctx_dram", [NSEQ, L, D])
    xT_dram = scratch("xT_dram", [NSEQ, 2, P, KD * L])
    q3 = scratch("q3", [NSEQ, 3, D, L], BF16)
    k3 = scratch("k3", [NSEQ, 3, D, L], BF16)
    v3 = scratch("v3", [NSEQ, L, H1, 3 * DH1], BF16)
    layer0(nc, x, w0, bias_f, proj_b, base_b, ident, ident_bf, causal, iota8, x1_dram)
    attention1(nc, x1_dram, w1, bias_f, bv1, ident, q3, k3, v3, xT_dram, ctx_dram)
    with ExitStack() as ctx:
        w = [ctx.enter_context(nc.sbuf_tensor(n, s, F32R)) for n, s in
             (("gu_hi", [P, KD, 2 * INTER]), ("gu_lo", [P, KD, 2 * INTER]), ("d_hi", [P, FT, D]), ("d_lo", [P, FT, D]))]
        dequant(nc, w, qw_gu, qz_gu, sc_gu, gi_gu, qw_d, qz_d, sc_d, gi_d)
        feed_forward(nc, w, x1_dram, ctx_dram.rearrange("s t d -> (s t) d"), xT_dram, out)


def tiles(a):
    import numpy as np
    return np.ascontiguousarray(a.reshape(-1, P, a.shape[1]).transpose(1, 0, 2).reshape(P, -1))


def kernel(**inputs):
    import ml_dtypes
    import numpy as np
    import concourse.bacc as bacc
    from concourse.bass_utils import run_bass_kernel_spmd

    a = {k: np.asarray(v) for k, v in inputs.items()}
    w0 = np.concatenate([
        tiles(a["L0_attn_conv_w"].reshape(TAPS * D, 3 * W)),
        a["L0_attn_wq"].reshape(W, H0 * DH0), a["L0_attn_wk"].reshape(W, H0 * DH0), a["L0_attn_wv"].reshape(W, H0 * DH0),
        tiles(a["L0_attn_wo"].reshape(H0 * DH0, W)), a["L0_attn_proj_w"], tiles(a["L0_ffn_W_base"].T),
        tiles(np.concatenate([a["L0_ffn_A_stack"].reshape(ER, D).T, a["L0_ffn_W_router"].T, np.zeros((D, AR - ER - NE), np.float32)], 1)),
        a["L0_ffn_B_stack"].transpose(0, 2, 1).reshape(ER, D)], 1)
    bias_f = np.concatenate([a[n].reshape(-1, P).T for n in (
        "L0_attn_conv_b", "L0_attn_bq", "L0_attn_bk", "L0_attn_bv", "L0_attn_bo", "L1_attn_bq", "L1_attn_bk")], 1)
    w1 = tiles(np.concatenate([a["L1_attn_wq"].T, a["L1_attn_wk"].T, a["L1_attn_wv"].T], 1))
    above = np.where(np.arange(P)[None, :] <= np.arange(P)[:, None], 0.0, -1e30).astype(ml_dtypes.bfloat16)
    arrays = {
        "x": a["L0_attn_inputs"].reshape(NSEQ * L, D), "w0": w0, "bias_f": bias_f,
        "proj_b": a["L0_attn_proj_b"], "base_b": a["L0_ffn_b_base"], "w1": w1, "bv1": a["L1_attn_bv"],
        "qw_gu": a["L1_ffn_qweight_gu"], "qz_gu": a["L1_ffn_qzeros_gu"], "sc_gu": a["L1_ffn_scales_gu"], "gi_gu": a["L1_ffn_g_idx_gu"],
        "qw_d": a["L1_ffn_qweight_down"], "qz_d": a["L1_ffn_qzeros_down"], "sc_d": a["L1_ffn_scales_down"], "gi_d": a["L1_ffn_g_idx_down"],
        "ident": np.eye(P, dtype=np.float32), "ident_bf": np.eye(P).astype(ml_dtypes.bfloat16),
        "causal": np.tile(above, (1, HG)), "iota8": np.tile(np.arange(NE, dtype=np.float32), (P, NT)),
    }
    arrays = {k: np.ascontiguousarray(v) for k, v in arrays.items()}
    nc = bacc.Bacc("TRN2", target_bir_lowering=False, num_devices=1)
    args = {k: nc.dram_tensor(k, v.shape, mybir.dt.from_np(v.dtype), kind="ExternalInput").ap() for k, v in arrays.items()}
    out = nc.dram_tensor("out", [NSEQ * L, D], F32, kind="ExternalOutput").ap()
    block_kernel(nc, **args, out=out)
    r = run_bass_kernel_spmd(nc, [arrays], core_ids=[0])
    return r.results[0]["out"].reshape(NSEQ, L, D)
```

```python
from contextlib import ExitStack

import concourse.bass as bass
from concourse import mybir

F32 = mybir.dt.float32
F32R = mybir.dt.float32r
BF16 = mybir.dt.bfloat16
U32 = mybir.dt.uint32
I32 = mybir.dt.int32
ALU = mybir.AluOpType
ACT = mybir.ActivationFunctionType
AX_X = mybir.AxisListType.X

P = 128
NSEQ, L, D = 4, 512, 512
NT = L // P
KD = D // P
TAPS = 3
W = 128
H0, DH0 = 16, 64
HG = 4
NHG = H0 // HG
NBLK = L // P
STEPS = NHG * NBLK
NE, RANK = 8, 16
ER = NE * RANK
EPS = 1e-5
LORA_SCALE = 32.0 / RANK
H1, DH1 = 32, 16

C_CONV = 0
C_WQ = C_CONV + TAPS * KD * 3 * W
C_WK = C_WQ + H0 * DH0
C_WV = C_WK + H0 * DH0
C_WO = C_WV + H0 * DH0
C_PROJ = C_WO + (H0 * DH0 // P) * W
C_BASE = C_PROJ + D
C_AR = C_BASE + KD * D
AR = 256
C_B = C_AR + KD * AR
N_A = C_B + D
WCH = 800
N_WCH = N_A // WCH
assert N_WCH * WCH == N_A
STAGED = (2, 4, 2)
NST = sum(STAGED)
CONV_WCH = -(-C_WQ // WCH)
B_CONV, B_Q, B_K, B_V, B_O, B_Q1, B_K1 = 0, 3, 11, 19, 27, 28, 32
N_BF = 36


def spread(ap, n):
    return ap.unsqueeze(2).broadcast_to([ap.shape[0], ap.shape[1], n])


def split3(pe, out, lhs, rhs, start, stop):
    pe.matmul(out, lhs[0], rhs[0], start=start, stop=False, skip_group_check=True)
    pe.matmul(out, lhs[0], rhs[1], start=False, stop=False, skip_group_check=True)
    return pe.matmul(out, lhs[1], rhs[0], start=False, stop=stop, skip_group_check=True)


def bank_uses():
    uses = [("conv", "AD")] * 3 + [("ar", "A")] * NT
    uses += [(n, e) for n, e in (("q", "A"), ("q", "A"), ("k", "AD"), ("k", "AD"), ("v", "D"), ("v", "D"))] * NHG
    uses += [("hT", "AD")] + [("x1", "D")] * NT
    return uses


USES = bank_uses()
assert len(USES) % 2 == 0
ACT_USES = sum("A" in e for _, e in USES)
DVE_USES = sum("D" in e for _, e in USES)


def freed(letter, upto):
    return sum(letter in e for _, e in USES[:upto])


def layer0(nc, x, w0, bias_f, proj_b, base_b, ident, ident_bf, causal, iota8, x1_dram):
    with ExitStack() as ctx:
        def sb(name, shape, dt=F32):
            return ctx.enter_context(nc.sbuf_tensor(name, shape, dt))

        def sem(name):
            return ctx.enter_context(nc.semaphore(name))

        w_hi = sb("w0_hi", [P, N_A], F32R)
        w_lo = sb("w0_lo", [P, N_A], F32R)
        xin = sb("xin", [P, NT, D])
        xres = sb("xres", [P, 2, D])
        xT_hi = sb("xT_hi", [P, KD, L + 2], F32R)
        xT_lo = sb("xT_lo", [P, KD, L + 2], F32R)
        c_hi = sb("c_hi", [P, 3, L], F32R)
        c_lo = sb("c_lo", [P, 3, L], F32R)
        qh = sb("qh", [P, 2, 2, L])
        kh = sb("kh", [P, 2, 2, 2, L])
        vh = sb("vh", [P, 2, NBLK, HG * DH0])
        prob = sb("prob", [P, 3, HG * P])
        probT = sb("probT", [P, 2, HG * P])
        o_hi = sb("o_hi", [P, 2, L], F32R)
        o_lo = sb("o_lo", [P, 2, L], F32R)
        a_hi = sb("a_hi", [P, L], F32R)
        a_lo = sb("a_lo", [P, L], F32R)
        har = sb("har", [P, NT, ER + NE])
        hT_hi = sb("hT_hi", [P, L], F32R)
        hT_lo = sb("hT_lo", [P, L], F32R)
        bf = sb("bf", [P, N_BF])
        brow = sb("brow", [P, D])
        idf = sb("idf", [P, P])
        idb = sb("idb", [P, P], BF16)
        neg = sb("neg", [P, HG * P], BF16)
        io8 = sb("io8", [P, NT * NE])
        mx = sb("mx", [P, 3, HG])
        nmx = sb("nmx", [P, 3, HG])
        sums = sb("sums", [P, 3, HG])
        rsum = sb("rsum", [P, 3, HG])
        stats = sb("stats", [P, NT, 6])
        mv = sb("mv", [P, NT, 2])
        veps = sb("veps", [P, NT])
        rstd = sb("rstd", [P, NT])
        mhalf = sb("mhalf", [P, NT])
        rmx = sb("rmx", [P, NT])
        rp = sb("rp", [P, NT, NE])
        rs = sb("rs", [P, NT])
        top = sb("top", [P, NT, 8])
        topi = sb("topi", [P, NT, 8], U32)
        topf = sb("topf", [P, NT, 8])
        wsel = sb("wsel", [P, NT, 2])
        eq = sb("eq", [P, 2, NT, NE])
        comb = sb("comb", [P, NT, NE])
        ps = ctx.enter_context(nc.psum_tensor("ps0", [P, 8, 512], F32))
        MM, SC, PT, AV, WO = 0, 2, 4, 5, 7
        XT_BANKS = (SC, SC + 1, PT, AV)
        flat = [qh[:].rearrange("p a b t -> p (a b t)"), kh[:].rearrange("p a b c t -> p (a b c t)"), vh[:].rearrange("p a b n -> p (a b n)")]
        stage = [t[:, j * WCH:(j + 1) * WCH] for t, n in zip(flat, STAGED) for j in range(n)]
        brow2 = prob[:, 2, :]

        const_in, ident_in, carrier = sem("const_in"), sem("ident_in"), sem("carrier")
        w_in = [sem(f"w_in{s}") for s in range(NST)]
        x_in = [sem(f"x_in{t}") for t in range(NT)]
        res_in = [sem(f"res_in{s}") for s in range(2)]
        x1_out = [sem(f"x1_out{s}") for s in range(2)]
        w_hi_ready, w_lo_ready = sem("w_hi_ready"), sem("w_lo_ready")
        zeroed, mhalf_set = sem("zeroed"), sem("mhalf_set")
        brow_ready = sem("brow_ready")
        st_done, ve_ready, rstd_ready, xn_ready = sem("st_done"), sem("ve_ready"), sem("rstd_ready"), sem("xn_ready")
        xt_done, xT_hi_ready, xT_lo_ready = sem("xt_done"), sem("xT_hi_ready"), sem("xT_lo_ready")
        mm_full, mm_act, mm_dve = sem("mm_full"), sem("mm_act"), sem("mm_dve")
        router_exp, router_chain, comb_ready = sem("router_exp"), sem("router_chain"), sem("comb_ready")
        sc_full, mx_ready, nmx_ready, exp_done = sem("sc_full"), sem("mx_ready"), sem("nmx_ready"), sem("exp_done")
        rsum_ready, prob_ready, tr_full, probT_ready = sem("rsum_ready"), sem("prob_ready"), sem("tr_full"), sem("probT_ready")
        av_done, o_hi_ready, o_lo_ready, wo_done = sem("av_done"), sem("o_hi_ready"), sem("o_lo_ready"), sem("wo_done")
        a_hi_ready, a_lo_ready = sem("a_hi_ready"), sem("a_lo_ready")
        res_ready, x1_ready = sem("res_ready"), sem("x1_ready")

        def carry(eng):
            eng.sem_inc(carrier, 1)

        def wt(c, n):
            return w_hi[:, c:c + n], w_lo[:, c:c + n]

        U_AR = 3
        U_QKV = U_AR + NT
        U_HT = U_QKV + 6 * NHG
        U_X1 = U_HT + 1
        NU = len(USES)
        N_CONST = 6
        S_STATS, S_RSTD, S_NORM = 5, 6, 8

        def use_act(hg, k):
            return U_QKV + 6 * hg + k

        with nc.Block() as block:

            @block.sync
            def _(sp):
                def load_x(i):
                    for t in range(NT):
                        sp.dma_start(xin[:, t, :], x[bass.ds(i * L + t * P, P), :]).then_inc(x_in[t], 16)

                def load_w(steps):
                    for j in steps:
                        if j >= NST:
                            sp.wait_ge(w_hi_ready, j - NST + 1)
                            sp.wait_ge(w_lo_ready, j - NST + 1)
                        sp.dma_start(stage[j % NST], w0[:, j * WCH:(j + 1) * WCH]).then_inc(w_in[j % NST], 16)

                load_x(0)
                sp.dma_start(idf[:], ident).then_inc(ident_in, 16)
                load_w(range(2))
                sp.dma_start(bf[:], bias_f).then_inc(const_in, 16)
                load_w(range(2, NST))
                sp.dma_start(idb[:], ident_bf).then_inc(const_in, 16)
                sp.dma_start(neg[:], causal).then_inc(const_in, 16)
                sp.dma_start(io8[:], iota8).then_inc(const_in, 16)
                sp.dma_start(brow[:], bass.AP(proj_b.tensor, 0, [[0, P], [1, D]])).then_inc(const_in, 16)
                sp.dma_start(brow2, bass.AP(base_b.tensor, 0, [[0, P], [1, D]])).then_inc(const_in, 16)
                load_w(range(NST, N_WCH))

                def body(i, last):
                    for s in range(2):
                        sp.wait_ge(x1_out[s], 32 * i)
                        sp.dma_start(xres[:, s, :], x[bass.ds(i * L + s * P, P), :]).then_inc(res_in[s], 16)
                    if not last:
                        sp.wait_ge(xt_done, KD * i + KD)
                        load_x(i + 1)
                    for t in range(NT):
                        sp.wait_ge(x1_ready, NT * i + t + 1)
                        sp.dma_start(x1_dram[bass.ds(i * L + t * P, P), :], xres[:, t % 2, :]).then_inc(x1_out[t % 2], 16)
                        if t < 2:
                            sp.wait_ge(x1_out[t], 32 * i + 16)
                            sp.dma_start(xres[:, t, :], x[bass.ds(i * L + (t + 2) * P, P), :]).then_inc(res_in[t], 16)

                body(0, False)
                with sp.Fori(1, NSEQ - 1) as i:
                    body(i, False)
                body(NSEQ - 1, True)
                for s in range(2):
                    sp.wait_ge(x1_out[s], 32 * NSEQ)

            @block.gpsimd
            def _(pool):
                pool.memset(mhalf[:], -0.5).then_inc(mhalf_set, 1)
                for b in (0, L + 1):
                    pool.memset(xT_hi[:, :, b:b + 1].bitcast(F32), 0.0).then_inc(zeroed, 1)
                    pool.memset(xT_lo[:, :, b:b + 1].bitcast(F32), 0.0).then_inc(zeroed, 1)
                pool.wait_ge(mhalf_set, 1)

                def rstds(n):
                    pool.wait_ge(ve_ready, n + 1)
                    pool.tensor_tensor(rstd[:], veps[:], mhalf[:], ALU.pow).then_inc(rstd_ready, 1)

                def residual(i, t):
                    pool.wait_ge(res_in[t % 2], 32 * i + 16 * (t // 2) + 16)
                    pool.tensor_tensor(xres[:, t % 2, :], xres[:, t % 2, :], brow[:], ALU.add).then_inc(res_ready, 1)

                def body(i, last):
                    for s in range(STEPS):
                        pool.wait_ge(rsum_ready, STEPS * i + s + 1)
                        pv = prob[:, s % 3, :].rearrange("p (h k) -> p h k", h=HG)
                        pool.tensor_tensor(pv, pv, spread(rsum[:, s % 3, :], P), ALU.mult).then_inc(prob_ready, 1)
                        if s == S_RSTD and not last:
                            rstds(i + 1)
                    for t in range(NT):
                        residual(i, t)

                rstds(0)
                pool.wait_ge(const_in, 16 * N_CONST)
                pool.tensor_tensor(brow[:], brow[:], brow2, ALU.add).then_inc(brow_ready, 1)
                pool.wait_ge(w_lo_ready, N_WCH)
                pool.wait_ge(w_hi_ready, N_WCH)
                pool.memset(kh[:], 0.0).then_inc(zeroed, 1)
                pool.wait_ge(brow_ready, 1)
                body(0, False)
                with pool.Fori(1, NSEQ - 1) as i:
                    body(i, False)
                body(NSEQ - 1, True)

            @block.scalar
            def _(act):
                def w_his(steps):
                    for j in steps:
                        act.wait_ge(w_in[j % NST], 16 * (j // NST) + 16)
                        act.activation(w_hi[:, j * WCH:(j + 1) * WCH], stage[j % NST], ACT.Copy).then_inc(w_hi_ready, 1)

                def xT_hi_copy(i):
                    act.wait_ge(mm_full, NU * i)
                    for k in range(KD):
                        act.wait_ge(xt_done, KD * i + k + 1)
                        act.activation(xT_hi[:, k, 1:L + 1], ps[:, XT_BANKS[k], :], ACT.Copy).then_inc(xT_hi_ready, 1)

                def full(i, u):
                    act.wait_ge(mm_full, NU * i + u + 1)

                def qk_hi(i, hg):
                    act.wait_ge(av_done, STEPS * i + max(0, NBLK * (hg - 1)))
                    for hp in range(2):
                        full(i, use_act(hg, hp))
                        b = bf[:, B_Q + 2 * hg + hp:B_Q + 2 * hg + hp + 1]
                        act.activation(qh[:, hg % 2, hp, :], ps[:, (use_act(hg, hp)) % 2, :], ACT.Identity, bias=b).then_inc(mm_act, 1)
                    for hp in range(2):
                        u = use_act(hg, 2 + hp)
                        full(i, u)
                        act.activation(kh[0:DH0, hg % 2, hp, 0, :], ps[0:DH0, u % 2, :], ACT.Identity,
                                       bias=bf[0:DH0, B_K + 2 * hg + hp:B_K + 2 * hg + hp + 1]).then_inc(mm_act, 1)

                def exps(i, s):
                    act.wait_ge(nmx_ready, STEPS * i + s + 1)
                    act.wait_ge(tr_full, STEPS * i + max(0, s - 2))
                    for h in range(HG):
                        e = act.activation(prob[:, s % 3, h * P:(h + 1) * P], ps[:, SC + s % 2, h * P:(h + 1) * P], ACT.Exp,
                                           bias=nmx[:, s % 3, h:h + 1], scale=DH0 ** -0.5, accum_out=sums[:, s % 3, h:h + 1])
                    e.then_inc(exp_done, 1)

                def o_his(i, hg):
                    act.wait_ge(av_done, STEPS * i + NBLK * (hg + 1))
                    act.wait_ge(wo_done, NHG * i + hg)
                    for hp in range(2):
                        act.activation(o_hi[:, hp, :], ps[:, AV + hp, :], ACT.Identity,
                                       bias=bf[:, B_V + 2 * hg + hp:B_V + 2 * hg + hp + 1]).then_inc(o_hi_ready, 1)

                def body(i, last):
                    for m in range(3):
                        full(i, m)
                        act.wait_ge(av_done, STEPS * i)
                        act.activation(c_hi[:, m, :], ps[:, m % 2, :], ACT.Identity, bias=bf[:, B_CONV + m:B_CONV + m + 1]).then_inc(mm_act, 1)
                    for t in range(NT):
                        full(i, U_AR + t)
                        act.wait_ge(mm_full, NU * i)
                        act.activation(har[:, t, :], ps[:, (U_AR + t) % 2, 0:ER + NE], ACT.Copy).then_inc(mm_act, 1)
                    if isinstance(i, int) and i == 0:
                        act.wait_ge(w_lo_ready, N_WCH)
                        act.wait_ge(zeroed, 5)
                    qk_hi(i, 0)
                    for s in range(STEPS + 3):
                        if s % NBLK == 3 and s // NBLK + 1 < NHG:
                            qk_hi(i, s // NBLK + 1)
                        if s < STEPS:
                            exps(i, s)
                        if s == 3:
                            act.wait_ge(router_chain, 13 * i + 2)
                            act.activation(rp[:], rp[:], ACT.Exp).then_inc(router_exp, 1)
                        if s % NBLK == 2 and s >= 6:
                            o_his(i, (s - 6) // NBLK)
                    full(i, U_HT)
                    act.activation(hT_hi[:], ps[:, U_HT % 2, :], ACT.Copy).then_inc(mm_act, 1)
                    act.wait_ge(wo_done, NHG * i + NHG)
                    act.activation(a_hi[:], ps[:, WO, :], ACT.Identity, bias=bf[:, B_O:B_O + 1]).then_inc(a_hi_ready, 1)
                    if not last:
                        xT_hi_copy(i + 1)

                w_his(range(CONV_WCH))
                act.wait_ge(zeroed, 4)
                xT_hi_copy(0)
                w_his(range(CONV_WCH, N_WCH))
                act.wait_ge(const_in, 16 * N_CONST)
                act.wait_ge(brow_ready, 1)
                body(0, False)
                with act.Fori(1, NSEQ - 1) as i:
                    body(i, False)
                body(NSEQ - 1, True)

            @block.vector
            def _(dve):
                def norm_stats(i):
                    for t in range(NT):
                        dve.wait_ge(x_in[t], 16 * i + 16)
                        dve.bn_stats(stats[:, t, :], xin[:, t, :]).then_inc(st_done, 1)
                    for t in range(NT):
                        dve.wait_ge(st_done, 2 * NT * i + NT)
                        carry(dve)
                        dve.bn_aggr(mv[:, t, :], stats[:, t, :]).then_inc(st_done, 1)
                    dve.wait_ge(st_done, 2 * NT * i + 2 * NT)
                    dve.tensor_scalar(veps[:], mv[:, :, 1], EPS, None, ALU.add).then_inc(ve_ready, 1)

                def norm(i):
                    dve.wait_ge(rstd_ready, i + 1)
                    for t in range(NT):
                        dve.tensor_scalar(xin[:, t, :], xin[:, t, :], mv[:, t, 0:1], rstd[:, t:t + 1], ALU.subtract, ALU.mult).then_inc(xn_ready, 1)

                def w_los(steps):
                    for j in steps:
                        dve.wait_ge(w_hi_ready, j + 1)
                        c = slice(j * WCH, (j + 1) * WCH)
                        dve.tensor_tensor(w_lo[:, c], stage[j % NST], w_hi[:, c].bitcast(F32), ALU.subtract).then_inc(w_lo_ready, 1)

                def xT_lo_copy(i):
                    for k in range(KD):
                        dve.wait_ge(xT_hi_ready, KD * i + k + 1)
                        dve.tensor_tensor(xT_lo[:, k, 1:L + 1], ps[:, XT_BANKS[k], :], xT_hi[:, k, 1:L + 1].bitcast(F32), ALU.subtract).then_inc(xT_lo_ready, 1)

                def full(i, u):
                    dve.wait_ge(mm_full, NU * i + u + 1)

                def acted(i, u):
                    dve.wait_ge(mm_act, ACT_USES * i + freed("A", u + 1))

                def kv(i, hg):
                    dve.wait_ge(av_done, STEPS * i + max(0, NBLK * (hg - 1)))
                    for hp in range(2):
                        u = use_act(hg, 2 + hp)
                        full(i, u)
                        dve.tensor_scalar(kh[DH0:P, hg % 2, hp, 1, :], ps[DH0:P, u % 2, :],
                                          bf[DH0:P, B_K + 2 * hg + hp:B_K + 2 * hg + hp + 1], None, ALU.add).then_inc(mm_dve, 1)
                    for half in range(2):
                        u = use_act(hg, 4 + half)
                        full(i, u)
                        dve.tensor_copy(vh[:, hg % 2, 2 * half:2 * half + 2, :].rearrange("p b n -> p (b n)"), ps[:, u % 2, :]).then_inc(mm_dve, 1)

                def router(i):
                    n = [0]

                    def step(ins):
                        n[0] += 1
                        ins.then_inc(router_chain, 1)
                        dve.wait_ge(router_chain, 13 * i + n[0])

                    acted(i, U_AR + NT - 1)
                    step(dve.tensor_reduce(rmx[:], har[:, :, ER:ER + NE], AX_X, ALU.max))
                    step(dve.tensor_tensor(rp[:], har[:, :, ER:ER + NE], spread(rmx[:], NE), ALU.subtract))
                    dve.wait_ge(router_exp, i + 1)
                    step(dve.tensor_reduce(rs[:], rp[:], AX_X, ALU.add))
                    step(dve.reciprocal(rs[:], rs[:]))
                    step(dve.tensor_tensor(rp[:], rp[:], spread(rs[:], NE), ALU.mult))
                    carry(dve)
                    for t in range(NT):
                        top_i = dve.max(top[:, t, :], rp[:, t, :])
                    step(top_i)
                    carry(dve)
                    for t in range(NT):
                        idx_i = dve.max_index(topi[:, t, :], top[:, t, :], rp[:, t, :])
                    step(idx_i)
                    dve.tensor_tensor(rs[:], top[:, :, 0], top[:, :, 1], ALU.add)
                    step(dve.tensor_copy(topf[:], topi[:]))
                    step(dve.reciprocal(rs[:], rs[:]))
                    step(dve.tensor_tensor(wsel[:], top[:, :, 0:2], spread(rs[:], 2), ALU.mult))
                    iov = io8[:].rearrange("p (t e) -> p t e", t=NT)
                    for j in range(2):
                        e = dve.tensor_tensor(eq[:, j, :, :], iov, spread(topf[:, :, j], NE), ALU.is_equal)
                    step(e)
                    for j in range(2):
                        e = dve.tensor_tensor(eq[:, j, :, :], eq[:, j, :, :], spread(wsel[:, :, j], NE), ALU.mult)
                    step(e)
                    step(dve.tensor_tensor(comb[:], eq[:, 0, :, :], eq[:, 1, :, :], ALU.add))
                    assert n[0] == 13
                    for t in range(NT):
                        hv = har[:, t, 0:ER].rearrange("p (e r) -> p e r", e=NE)
                        cv = spread(comb[:, t, :], RANK)
                        dve.scalar_tensor_tensor(hv, hv, LORA_SCALE, cv, ALU.mult, ALU.mult).then_inc(comb_ready, 1)

                def maxes(i, s):
                    dve.wait_ge(sc_full, STEPS * i + s + 1)
                    dve.tensor_reduce(mx[:, s % 3, :], ps[:, SC + s % 2, :].rearrange("p (h k) -> p h k", h=HG), AX_X, ALU.max).then_inc(mx_ready, 1)
                    dve.wait_ge(mx_ready, STEPS * i + s + 1)
                    dve.tensor_scalar(nmx[:, s % 3, :], mx[:, s % 3, :], -DH0 ** -0.5, None, ALU.mult).then_inc(nmx_ready, 1)

                def recips(i, s):
                    dve.wait_ge(exp_done, STEPS * i + s + 1)
                    dve.wait_ge(prob_ready, STEPS * i + max(0, s - 2))
                    dve.reciprocal(rsum[:, s % 3, :], sums[:, s % 3, :]).then_inc(rsum_ready, 1)

                def probT_copy(i, s):
                    dve.wait_ge(tr_full, STEPS * i + s + 1)
                    dve.wait_ge(av_done, STEPS * i + max(0, s - 1))
                    dve.tensor_copy(probT[:, s % 2, :], ps[:, PT, :]).then_inc(probT_ready, 1)

                def o_los(i, hg):
                    for hp in range(2):
                        dve.wait_ge(o_hi_ready, 2 * NHG * i + 2 * hg + hp + 1)
                        dve.scalar_tensor_tensor(o_lo[:, hp, :], ps[:, AV + hp, :], bf[:, B_V + 2 * hg + hp:B_V + 2 * hg + hp + 1],
                                                 o_hi[:, hp, :].bitcast(F32), ALU.add, ALU.subtract).then_inc(o_lo_ready, 1)

                def body(i, last):
                    for m in range(3):
                        acted(i, m)
                        dve.scalar_tensor_tensor(c_lo[:, m, :], ps[:, m % 2, :], bf[:, B_CONV + m:B_CONV + m + 1],
                                                 c_hi[:, m, :].bitcast(F32), ALU.add, ALU.subtract).then_inc(mm_dve, 1)
                    if isinstance(i, int) and i == 0:
                        dve.wait_ge(zeroed, 5)
                    kv(i, 0)
                    for s in range(STEPS + 3):
                        if s % NBLK == 3 and s // NBLK + 1 < NHG:
                            kv(i, s // NBLK + 1)
                        if s < STEPS:
                            maxes(i, s)
                        if 1 <= s <= STEPS:
                            recips(i, s - 1)
                        if 2 <= s < STEPS + 2:
                            probT_copy(i, s - 2)
                        if s == 3:
                            router(i)
                        if s % NBLK == 2 and s >= 6:
                            o_los(i, (s - 6) // NBLK)
                        if s == S_STATS and not last:
                            norm_stats(i + 1)
                        if s == S_NORM and not last:
                            norm(i + 1)
                    acted(i, U_HT)
                    dve.tensor_tensor(hT_lo[:], ps[:, U_HT % 2, :], hT_hi[:].bitcast(F32), ALU.subtract).then_inc(mm_dve, 1)
                    dve.wait_ge(a_hi_ready, i + 1)
                    dve.scalar_tensor_tensor(a_lo[:], ps[:, WO, :], bf[:, B_O:B_O + 1], a_hi[:].bitcast(F32), ALU.add, ALU.subtract).then_inc(a_lo_ready, 1)
                    for t in range(NT):
                        if t == NT - 1 and not last:
                            xT_lo_copy(i + 1)
                        full(i, U_X1 + t)
                        dve.wait_ge(res_ready, NT * i + t + 1)
                        dve.tensor_tensor(xres[:, t % 2, :], ps[:, (U_X1 + t) % 2, :], xres[:, t % 2, :], ALU.add).then_inc(x1_ready, 1)

                norm_stats(0)
                w_los(range(2))
                norm(0)
                w_los(range(2, CONV_WCH))
                dve.wait_ge(zeroed, 4)
                xT_lo_copy(0)
                w_los(range(CONV_WCH, N_WCH))
                dve.wait_ge(const_in, 16 * N_CONST)
                body(0, False)
                with dve.Fori(1, NSEQ - 1) as i:
                    body(i, False)
                body(NSEQ - 1, True)

            @block.tensor
            def _(pe):
                def take(i, u):
                    pe.wait_ge(mm_act, ACT_USES * i + (freed("A", u - 1) if u >= 2 else 0))
                    n = [e for k, (w, e) in enumerate(USES[:max(0, u - 1)]) if "D" in e and w != "x1"]
                    pe.wait_ge(mm_dve, (DVE_USES - NT) * i + len(n))
                    pe.wait_ge(x1_ready, NT * i + max(0, u - 1 - U_X1))

                def transposes_in(i):
                    pe.wait_ge(xn_ready, NT * i + NT)
                    for k in range(KD):
                        for t in range(NT):
                            last = pe.transpose(ps[:, XT_BANKS[k], t * P:(t + 1) * P], xin[:, t, k * P:(k + 1) * P], idf[:])
                        last.then_inc(xt_done, 1)

                def mm_done(ins):
                    ins.then_inc(mm_full, 1)

                def qkv(i, hg):
                    for n, c0 in ((0, C_WQ), (1, C_WK)):
                        for hp in range(2):
                            u = use_act(hg, 2 * n + hp)
                            take(i, u)
                            mm_done(split3(pe, ps[:, u % 2, :], wt(c0 + (2 * hg + hp) * P, P), (c_hi[:, n, :], c_lo[:, n, :]), True, True))
                    for half in range(2):
                        u = use_act(hg, 4 + half)
                        take(i, u)
                        for b in range(2):
                            tok = slice((2 * half + b) * P, (2 * half + b + 1) * P)
                            last = split3(pe, ps[:, u % 2, b * 256:(b + 1) * 256], (c_hi[:, 2, tok], c_lo[:, 2, tok]),
                                          wt(C_WV + hg * HG * DH0, HG * DH0), True, True)
                        mm_done(last)

                def scores(i, s):
                    hg, b = s // NBLK, s % NBLK
                    if b == 0:
                        pe.wait_ge(mm_act, ACT_USES * i + freed("A", use_act(hg, 3) + 1))
                        pe.wait_ge(mm_dve, (DVE_USES - NT) * i + freed("D", use_act(hg, 3) + 1))
                    pe.wait_ge(exp_done, STEPS * i + max(0, s - 1))
                    bank = ps[:, SC + s % 2, :]
                    pe.matmul(bank, idb[:], neg[:], start=True, stop=False, skip_group_check=True)
                    for hp in range(2):
                        last = pe.matmul(bank[:, hp * 256:(hp + 1) * 256], qh[:, hg % 2, hp, b * P:(b + 1) * P],
                                         kh[:, hg % 2, hp, :, b * P:(b + 1) * P], start=False, stop=(hp == 1), skip_group_check=True)
                    last.then_inc(sc_full, 1)

                def transposes(i, s):
                    pe.wait_ge(prob_ready, STEPS * i + s + 1)
                    pe.wait_ge(probT_ready, STEPS * i + s)
                    for h in range(HG):
                        last = pe.transpose(ps[:, PT, h * P:(h + 1) * P], prob[:, s % 3, h * P:(h + 1) * P], idf[:])
                    last.then_inc(tr_full, 1)

                def weighted(i, s):
                    hg, b = s // NBLK, s % NBLK
                    pe.wait_ge(probT_ready, STEPS * i + s + 1)
                    if b == 0:
                        pe.wait_ge(mm_dve, (DVE_USES - NT) * i + freed("D", use_act(hg, 5) + 1))
                        pe.wait_ge(o_lo_ready, 2 * NHG * i + 2 * hg)
                    for h in range(HG):
                        r = DH0 * (h % 2)
                        last = pe.matmul(ps[r:r + DH0, AV + h // 2, b * P:(b + 1) * P], vh[:, hg % 2, b, h * DH0:(h + 1) * DH0],
                                         probT[:, s % 2, h * P:(h + 1) * P], start=True, stop=True, skip_group_check=True)
                    last.then_inc(av_done, 1)

                def out_proj(i, hg):
                    pe.wait_ge(o_lo_ready, 2 * NHG * i + 2 * hg + 2)
                    if hg == 0:
                        pe.wait_ge(a_lo_ready, i)
                    for hp in range(2):
                        last = split3(pe, ps[:, WO, :], wt(C_WO + (2 * hg + hp) * W, W), (o_hi[:, hp, :], o_lo[:, hp, :]),
                                      hg == 0 and hp == 0, hg == NHG - 1 and hp == 1)
                    last.then_inc(wo_done, 1)

                def body(i, last_seq):
                    for m in range(3):
                        take(i, m)
                        for j in range(TAPS):
                            for k in range(KD):
                                if m + j == 0:
                                    pe.wait_ge(xT_lo_ready, KD * i + k + 1)
                                if m == 0 and isinstance(i, int) and i == 0:
                                    pe.wait_ge(w_lo_ready, -(-(C_CONV + (j * KD + k + 1) * 3 * W) // WCH))
                                last = split3(pe, ps[:, m % 2, :], wt(C_CONV + (j * KD + k) * 3 * W + m * P, P),
                                              (xT_hi[:, k, j:j + L], xT_lo[:, k, j:j + L]), j + k == 0, j == TAPS - 1 and k == KD - 1)
                        mm_done(last)
                    if isinstance(i, int) and i == 0:
                        pe.wait_ge(w_lo_ready, N_WCH)
                    for t in range(NT):
                        u = U_AR + t
                        take(i, u)
                        for k in range(KD):
                            tok = slice(1 + t * P, 1 + (t + 1) * P)
                            last = split3(pe, ps[:, u % 2, 0:AR], (xT_hi[:, k, tok], xT_lo[:, k, tok]), wt(C_AR + k * AR, AR), k == 0, k == KD - 1)
                        mm_done(last)
                    qkv(i, 0)
                    for s in range(STEPS + 3):
                        if s % NBLK == 3 and s // NBLK + 1 < NHG:
                            qkv(i, s // NBLK + 1)
                        if s < STEPS:
                            scores(i, s)
                        if 2 <= s < STEPS + 2:
                            transposes(i, s - 2)
                        if s % NBLK == 3 and s >= 7:
                            out_proj(i, (s - 7) // NBLK)
                        if 3 <= s:
                            weighted(i, s - 3)
                    take(i, U_HT)
                    pe.wait_ge(comb_ready, NT * i + NT)
                    for t in range(NT):
                        last = pe.transpose(ps[:, U_HT % 2, t * P:(t + 1) * P], har[:, t, 0:ER], idf[:])
                    mm_done(last)
                    for t in range(NT):
                        u = U_X1 + t
                        if t == NT - 1 and not last_seq:
                            transposes_in(i + 1)
                        take(i, u)
                        tok = slice(1 + t * P, 1 + (t + 1) * P)
                        ts = slice(t * P, (t + 1) * P)
                        for k in range(KD):
                            split3(pe, ps[:, u % 2, :], (xT_hi[:, k, tok], xT_lo[:, k, tok]), wt(C_BASE + k * D, D), k == 0, False)
                        if t == 0:
                            out_proj(i, NHG - 1)
                            pe.wait_ge(mm_dve, (DVE_USES - NT) * i + freed("D", U_HT + 1))
                        split3(pe, ps[:, u % 2, :], (hT_hi[:, ts], hT_lo[:, ts]), wt(C_B, D), False, False)
                        if t == 0:
                            pe.wait_ge(a_lo_ready, i + 1)
                        mm_done(split3(pe, ps[:, u % 2, :], (a_hi[:, ts], a_lo[:, ts]), wt(C_PROJ, D), False, True))

                pe.wait_ge(ident_in, 16)
                pe.wait_ge(zeroed, 4)
                transposes_in(0)
                pe.wait_ge(const_in, 16 * N_CONST)
                body(0, False)
                with pe.Fori(1, NSEQ - 1) as i:
                    body(i, False)
                body(NSEQ - 1, True)


N_B = KD * 3 * D
WCH1 = 1024
N_WCH1 = N_B // WCH1
WCH1_Q = KD * D // WCH1
QPARTS = (0, 0, 0, 1, 1, 2)
KPARTS = (0, 1, 2, 0, 1, 0)
KS = len(QPARTS) * DH1
TPG = 4
NG = P // TPG
NCH = NT
HB = NG // 2
OB = 4
OA = NG // OB


def attention1(nc, x1_dram, w1, bias_f, bv1, ident, q3, k3, v3, xT_dram, ctx_dram):
    with ExitStack() as ctx:
        def sb(name, shape, dt=F32):
            return ctx.enter_context(nc.sbuf_tensor(name, shape, dt))

        def sem(name):
            return ctx.enter_context(nc.semaphore(name))

        w_hi = sb("w1_hi", [P, N_B], F32R)
        w_lo = sb("w1_lo", [P, N_B], F32R)
        stage = sb("stage1", [P, 2, WCH1])
        xin = sb("xin1", [P, NT, D])
        xT_hi = sb("xT1_hi", [P, KD, L], F32R)
        xT_lo = sb("xT1_lo", [P, KD, L], F32R)
        rf = sb("rf", [P, 2, L])
        yf = sb("yf", [P, 2, D])
        qk3 = sb("qk3", [P, 2, 3, L], BF16)
        vp3 = sb("vp3", [P, 2, H1, 3, DH1], BF16)
        qb = sb("qb", [KS, 2, H1, P], BF16)
        kb = sb("kb", [KS, 2, H1, P], BF16)
        vb = sb("vb", [P, 2, NG, 2, TPG, 2, DH1], BF16)
        S = sb("S", [P, 2, NG, H1])
        T = sb("T", [P, NG * H1])
        pp = sb("pp", [P, 2, 3, NG * H1], BF16)
        osb = sb("osb", [P, OA, OB, H1])
        cx = sb("cx", [P, 2, NG, DH1])
        bf = sb("bf1", [P, N_BF])
        bvb = sb("bvb", [P, D])
        idf = sb("idf1", [P, P])
        mx = sb("mx1", [P, NG])
        sm = sb("sm1", [P, NG])
        rs = sb("rs1", [P, NG])
        stats = sb("stats1", [P, NT, 6])
        mv = sb("mv1", [P, NT, 2])
        veps = sb("veps1", [P, NT])
        rstd = sb("rstd1", [P, NT])
        mhalf = sb("mhalf1", [P, NT])
        ps = ctx.enter_context(nc.psum_tensor("ps1", [P, 8, 512], F32))
        MM, SC, OUT, TR = 0, 2, 4, 6
        XT = (MM, MM + 1, TR, TR + 1)

        const_in, ident_in, carrier = sem("const1_in"), sem("ident1_in"), sem("carrier1")
        w_in = [sem(f"w1_in{s}") for s in range(2)]
        x_in = sem("x1_in")
        qk_out = [sem(f"qk_out{s}") for s in range(2)]
        v_out = [sem(f"v_out{s}") for s in range(2)]
        xT_out = sem("xT_out")
        qk_in = [sem(f"qk_in{s}") for s in range(2)]
        v_in = [sem(f"v_in{s}") for s in range(2)]
        cx_out = [sem(f"cx_out{s}") for s in range(2)]
        names = ("w_hi_ready1 w_lo_ready1 zeroed1 mhalf_set1 st_done1 ve_ready1 rstd_ready1 xn_ready1 xt_done1 xT_hi_ready1 "
                 "xT_lo_ready1 mm_full1 hi_ready r_ready mid_ready lo_ready y_ready sc_full1 mx_ready1 sub_ready exp_ready "
                 "sum_ready rs_ready p_ready T_ready ph_ready T_rest pm_ready pl_ready av_done1 o_ready otr_full cx_ready")
        s_ = {n: sem(n) for n in names.split()}

        def carry(eng):
            eng.sem_inc(carrier, 1)

        NU = 12

        def chunk(i, c, lag):
            return (i - 1, c - lag) if c >= lag else (i - 2, c - lag + NCH)

        def has(i, c, lag, att, carried):
            return att if c >= lag else carried

        def upto(n):
            return max(0, n) if isinstance(n, int) else n

        with nc.Block() as block:

            @block.sync
            def _(sp):
                sp.dma_start(xin[:], x1_dram[0:L, :].rearrange("(t p) d -> p t d", p=P)).then_inc(x_in, 16)
                sp.dma_start(idf[:], ident).then_inc(ident_in, 16)
                for j in range(N_WCH1):
                    s = j % 2
                    if j >= 2:
                        sp.wait_ge(s_["w_hi_ready1"], j - 1)
                        sp.wait_ge(s_["w_lo_ready1"], j - 1)
                    sp.dma_start(stage[:, s, :], w1[:, j * WCH1:(j + 1) * WCH1]).then_inc(w_in[s], 16)
                    if j == 1:
                        sp.dma_start(bf[:], bias_f).then_inc(const_in, 16)
                        sp.dma_start(bvb[:], bass.AP(bv1.tensor, 0, [[0, P], [1, D]])).then_inc(const_in, 16)

                def load_qk(a, c):
                    s = c % 2
                    if c == 0:
                        for o in range(2):
                            sp.wait_ge(qk_out[o], 64 * a + 64)
                            carry(sp)
                    sp.wait_ge(s_["sc_full1"], upto(NCH * a + c - 1))
                    for dst, src, parts in ((qb, q3, QPARTS), (kb, k3, KPARTS)):
                        for j, part in enumerate(parts):
                            view = src[bass.ds(a, 1), part, :, c * P:(c + 1) * P].rearrange("o (h d) t -> d (o h) t", d=DH1)
                            sp.dma_start(dst[DH1 * j:DH1 * (j + 1), s, :, :], view).then_inc(qk_in[s], 16)

                def load_v(a, c):
                    s = c % 2
                    if c == 0:
                        sp.wait_ge(s_["zeroed1"], 1)
                        for o in range(2):
                            sp.wait_ge(v_out[o], 32 * a + 32)
                            carry(sp)
                    sp.wait_ge(s_["av_done1"], upto(NCH * a + c - 1))
                    for q in range(TPG):
                        view = v3[bass.ds(a, 1), c * P:(c + 1) * P, :, :].rearrange("o (g q) t n -> (o q) t g n", q=TPG)[q]
                        own = vb[32 * q:32 * q + 32, s, :, :, q, :, :]
                        sp.dma_start(own[:, :, 0, :, :].rearrange("t g w d -> t g (w d)"), view[:, :, 0:2 * DH1]).then_inc(v_in[s], 16)
                        sp.dma_start(own[:, :, 1, 0, :], view[:, :, 2 * DH1:3 * DH1]).then_inc(v_in[s], 16)

                def store_ctx(a, c):
                    sp.wait_ge(s_["cx_ready"], 2 * NCH * a + 2 * c + 2)
                    for b in range(OB):
                        view = ctx_dram[bass.ds(a, 1), c * P + b * NG:c * P + (b + 1) * NG, :].rearrange("o t (h d) -> h (o t) d", d=DH1)
                        sp.dma_start(view, cx[32 * b:32 * b + 32, c % 2, :, :]).then_inc(cx_out[c % 2], 16)

                def store_qkv(i, u):
                    sp.wait_ge(s_["lo_ready"], NU * i + u + 1)
                    if u < 8:
                        dst = q3 if u < 4 else k3
                        view = dst[bass.ds(i, 1), :, (u % 4) * P:(u % 4 + 1) * P, :].rearrange("o w p t -> p (o w) t")
                        sp.dma_start(view, qk3[:, u % 2, :, :]).then_inc(qk_out[u % 2], 16)
                    else:
                        t = u - 8
                        view = v3[bass.ds(i, 1), t * P:(t + 1) * P, :, :].rearrange("o p t n -> (o p) t n")
                        sp.dma_start(view, vp3[:, u % 2, :, :, :].rearrange("p t w d -> p t (w d)")).then_inc(v_out[u % 2], 16)

                def steps(i, c, qkv, att, carried):
                    if att and c < NCH - 1:
                        load_qk(i - 1, c + 1)
                    if qkv and c == NCH - 1:
                        load_qk(i, 0)
                    if has(i, c, 1, att, carried):
                        load_v(*chunk(i, c, 1))
                    if has(i, c, 3, att, carried):
                        store_ctx(*chunk(i, c, 3))
                    if qkv:
                        for u in range(3 * c, 3 * c + 3):
                            store_qkv(i, u)

                def body(i, before, qkv, att, carried):
                    if qkv:
                        sp.wait_ge(s_["xt_done1"], KD * i)
                        sp.dma_start(xin[:], x1_dram[bass.ds(i * L, L), :].rearrange("(t p) d -> p t d", p=P)).then_inc(x_in, 16)
                    steps(i - 1, NCH - 1, *before, False)
                    first_steps(i, qkv, att, carried)

                def first_steps(i, qkv, att, carried):
                    for c in range(NCH - 1):
                        steps(i, c, qkv, att, carried)
                        if qkv and c < 2:
                            sp.wait_ge(s_["xT_lo_ready1"], KD * i + KD)
                            view = xT_dram[bass.ds(i, 1), c, :, :].rearrange("o p n -> (o p) n")
                            sp.dma_start(view, (xT_hi, xT_lo)[c][:].rearrange("p k t -> p (k t)").bitcast(F32)).then_inc(xT_out, 16)

                first_steps(0, True, False, False)
                body(1, (True, False), True, True, False)
                with sp.Fori(2, NSEQ) as i:
                    body(i, (True, True), True, True, True)
                body(NSEQ, (True, True), False, True, True)
                body(NSEQ + 1, (False, True), False, False, True)
                sp.wait_ge(xT_out, 32 * NSEQ)
                for s in range(2):
                    sp.wait_ge(cx_out[s], 16 * OB * NCH // 2 * NSEQ)

            @block.gpsimd
            def _(pool):
                pool.memset(mhalf[:], -0.5).then_inc(s_["mhalf_set1"], 1)
                pool.wait_ge(s_["mhalf_set1"], 1)

                def normalise(a, c):
                    pool.wait_ge(s_["rs_ready"], NCH * a + c + 1)
                    v = S[:, c % 2, :, :]
                    pool.tensor_tensor(v, v, spread(rs[:], H1), ALU.mult).then_inc(s_["p_ready"], 1)

                def last_part(a, c):
                    pool.wait_ge(s_["pm_ready"], NCH * a + c + 1)
                    pool.tensor_tensor(pp[:, c % 2, 2, :], T[:], pp[:, c % 2, 1, :], ALU.subtract).then_inc(s_["pl_ready"], 1)

                def parts(i, u):
                    if u >= 8:
                        pool.wait_ge(s_["hi_ready"], NU * i + u + 1)
                        rv = rf[:, u % 2, :].rearrange("p (t d) -> p t d", d=DH1)
                        pool.tensor_tensor(rv, yf[:, u % 2, :].rearrange("p (t d) -> p t d", d=DH1), vp3[:, u % 2, :, 0, :], ALU.subtract).then_inc(s_["r_ready"], 1)
                    pool.wait_ge(s_["mid_ready"], NU * i + u + 1)
                    if u < 8:
                        pool.tensor_tensor(qk3[:, u % 2, 2, :], rf[:, u % 2, :], qk3[:, u % 2, 1, :], ALU.subtract).then_inc(s_["lo_ready"], 1)
                    else:
                        rv = rf[:, u % 2, :].rearrange("p (t d) -> p t d", d=DH1)
                        pool.tensor_tensor(vp3[:, u % 2, :, 2, :], rv, vp3[:, u % 2, :, 1, :], ALU.subtract).then_inc(s_["lo_ready"], 1)

                def body(i, qkv, att, carried):
                    if qkv:
                        pool.wait_ge(s_["ve_ready1"], i + 1)
                        pool.tensor_tensor(rstd[:], veps[:], mhalf[:], ALU.pow).then_inc(s_["rstd_ready1"], 1)
                        if isinstance(i, int) and i == 0:
                            pool.memset(vb[:].rearrange("p s g n q w d -> p (s g n q w d)").bitcast(U32), 0).then_inc(s_["zeroed1"], 1)
                    for c in range(NCH):
                        if qkv:
                            parts(i, 3 * c)
                            parts(i, 3 * c + 1)
                        if att:
                            normalise(i - 1, c)
                        if has(i, c, 1, att, carried):
                            last_part(*chunk(i, c, 1))
                        if qkv:
                            parts(i, 3 * c + 2)

                body(0, True, False, False)
                body(1, True, True, False)
                with pool.Fori(2, NSEQ) as i:
                    body(i, True, True, True)
                body(NSEQ, False, True, True)
                body(NSEQ + 1, False, False, True)

            @block.scalar
            def _(act):
                def w_his(steps):
                    for j in steps:
                        act.wait_ge(w_in[j % 2], 16 * (j // 2) + 16)
                        act.activation(w_hi[:, j * WCH1:(j + 1) * WCH1], stage[:, j % 2, :], ACT.Copy).then_inc(s_["w_hi_ready1"], 1)

                def first_part(i, u):
                    s = u % 2
                    if u < 8:
                        act.wait_ge(s_["mm_full1"], NU * i + u + 1)
                        act.wait_ge(qk_out[s], 64 * i + 16 * (u // 2))
                        act.activation(qk3[:, s, 0, :], ps[:, MM + s, :], ACT.Identity, bias=bf[:, B_Q1 + u:B_Q1 + u + 1]).then_inc(s_["hi_ready"], 1)
                    else:
                        act.wait_ge(s_["y_ready"], 4 * i + u - 8 + 1)
                        act.wait_ge(v_out[s], 32 * i + 16 * ((u - 8) // 2))
                        act.activation(vp3[:, s, :, 0, :], yf[:, s, :].rearrange("p (t d) -> p t d", d=DH1), ACT.Copy).then_inc(s_["hi_ready"], 1)

                def mid_part(i, u):
                    s = u % 2
                    act.wait_ge(s_["r_ready"], NU * i + u + 1)
                    if u < 8:
                        act.activation(qk3[:, s, 1, :], rf[:, s, :], ACT.Copy).then_inc(s_["mid_ready"], 1)
                    else:
                        act.activation(vp3[:, s, :, 1, :], rf[:, s, :].rearrange("p (t d) -> p t d", d=DH1), ACT.Copy).then_inc(s_["mid_ready"], 1)

                def exps(a, c):
                    act.wait_ge(s_["sub_ready"], 2 * NCH * a + 2 * c + 2)
                    v = S[:, c % 2, :, :].rearrange("p g t -> p (g t)")
                    act.activation(v, v, ACT.Exp, scale=DH1 ** -0.5).then_inc(s_["exp_ready"], 1)

                def prob_hi(a, c):
                    act.wait_ge(s_["T_ready"], NCH * a + c + 1)
                    act.wait_ge(s_["av_done1"], upto(NCH * a + c - 1))
                    act.activation(pp[:, c % 2, 0, :], T[:], ACT.Copy).then_inc(s_["ph_ready"], 1)

                def prob_mid(a, c):
                    act.wait_ge(s_["T_rest"], NCH * a + c + 1)
                    act.activation(pp[:, c % 2, 1, :], T[:], ACT.Copy).then_inc(s_["pm_ready"], 1)

                def o_copy(a, c):
                    act.wait_ge(s_["av_done1"], NCH * a + c + 1)
                    act.wait_ge(s_["otr_full"], NCH * a + c)
                    for hf in range(2):
                        act.activation(osb[:, :, 2 * hf:2 * hf + 2, :].rearrange("p a b h -> p b a h"),
                                       ps[:, OUT + hf, :].rearrange("p (b a h) -> p b a h", b=2, h=H1), ACT.Copy).then_inc(s_["o_ready"], 1)

                def body(i, qkv, att, carried):
                    if isinstance(i, int) and i == 0:
                        w_his(range(WCH1_Q))
                    if has(i, 0, 2, att, carried):
                        o_copy(*chunk(i, 0, 2))
                    if qkv:
                        act.wait_ge(xT_out, 32 * i)
                        act.wait_ge(s_["mm_full1"], NU * i)
                        for k in range(KD):
                            act.wait_ge(s_["xt_done1"], KD * i + k + 1)
                            act.activation(xT_hi[:, k, :], ps[:, XT[k], :], ACT.Copy).then_inc(s_["xT_hi_ready1"], 1)
                    if has(i, 0, 1, att, carried):
                        prob_hi(*chunk(i, 0, 1))
                    if isinstance(i, int) and i == 0:
                        w_his(range(WCH1_Q, N_WCH1))
                        act.wait_ge(const_in, 32)
                    for c in range(NCH):
                        u = 3 * c
                        if qkv:
                            first_part(i, u)
                            mid_part(i, u)
                        if c > 0 and has(i, c, 1, att, carried):
                            prob_hi(*chunk(i, c, 1))
                        if qkv:
                            first_part(i, u + 1)
                        if att:
                            exps(i - 1, c)
                        if qkv:
                            mid_part(i, u + 1)
                        if has(i, c, 1, att, carried):
                            prob_mid(*chunk(i, c, 1))
                        if c > 0 and has(i, c, 2, att, carried):
                            o_copy(*chunk(i, c, 2))
                        if qkv:
                            first_part(i, u + 2)
                            mid_part(i, u + 2)

                body(0, True, False, False)
                body(1, True, True, False)
                with act.Fori(2, NSEQ) as i:
                    body(i, True, True, True)
                body(NSEQ, False, True, True)
                body(NSEQ + 1, False, False, True)

            @block.vector
            def _(dve):
                def w_los(steps):
                    for j in steps:
                        dve.wait_ge(s_["w_hi_ready1"], j + 1)
                        c = slice(j * WCH1, (j + 1) * WCH1)
                        dve.tensor_tensor(w_lo[:, c], stage[:, j % 2, :], w_hi[:, c].bitcast(F32), ALU.subtract).then_inc(s_["w_lo_ready1"], 1)

                def norm_stats(i):
                    dve.wait_ge(x_in, 16 * i + 16)
                    for t in range(NT):
                        dve.bn_stats(stats[:, t, :], xin[:, t, :]).then_inc(s_["st_done1"], 1)
                    for t in range(NT):
                        dve.wait_ge(s_["st_done1"], 2 * NT * i + NT)
                        carry(dve)
                        dve.bn_aggr(mv[:, t, :], stats[:, t, :]).then_inc(s_["st_done1"], 1)
                    dve.wait_ge(s_["st_done1"], 2 * NT * i + 2 * NT)
                    dve.tensor_scalar(veps[:], mv[:, :, 1], EPS, None, ALU.add).then_inc(s_["ve_ready1"], 1)

                def normalised(i):
                    dve.wait_ge(s_["rstd_ready1"], i + 1)
                    for t in range(NT):
                        dve.tensor_scalar(xin[:, t, :], xin[:, t, :], mv[:, t, 0:1], rstd[:, t:t + 1], ALU.subtract, ALU.mult).then_inc(s_["xn_ready1"], 1)

                def xT_los(i):
                    for k in range(KD):
                        dve.wait_ge(s_["xT_hi_ready1"], KD * i + k + 1)
                        dve.tensor_tensor(xT_lo[:, k, :], ps[:, XT[k], :], xT_hi[:, k, :].bitcast(F32), ALU.subtract).then_inc(s_["xT_lo_ready1"], 1)

                def rest(i, u):
                    s = u % 2
                    dve.wait_ge(s_["lo_ready"], NU * i + max(0, u - 1))
                    if u < 8:
                        dve.wait_ge(s_["hi_ready"], NU * i + u + 1)
                        dve.scalar_tensor_tensor(rf[:, s, :], ps[:, MM + s, :], bf[:, B_Q1 + u:B_Q1 + u + 1], qk3[:, s, 0, :], ALU.add, ALU.subtract).then_inc(s_["r_ready"], 1)
                    else:
                        dve.wait_ge(s_["mm_full1"], NU * i + u + 1)
                        dve.tensor_tensor(yf[:, s, :], ps[:, MM + s, :], bvb[:], ALU.add).then_inc(s_["y_ready"], 1)

                def max_sub(a, c):
                    dve.wait_ge(s_["sc_full1"], NCH * a + c + 1)
                    for hf in range(2):
                        g = slice(hf * HB, (hf + 1) * HB)
                        v = ps[:, SC + hf, :].rearrange("p (g t) -> p g t", t=H1)
                        dve.tensor_reduce(mx[:, g], v, AX_X, ALU.max).then_inc(s_["mx_ready1"], 1)
                    for hf in range(2):
                        g = slice(hf * HB, (hf + 1) * HB)
                        v = ps[:, SC + hf, :].rearrange("p (g t) -> p g t", t=H1)
                        dve.wait_ge(s_["mx_ready1"], 2 * NCH * a + 2 * c + 2)
                        dve.tensor_tensor(S[:, c % 2, g, :], v, spread(mx[:, g], H1), ALU.subtract).then_inc(s_["sub_ready"], 1)

                def sums(a, c):
                    dve.wait_ge(s_["exp_ready"], NCH * a + c + 1)
                    dve.tensor_reduce(sm[:], S[:, c % 2, :, :], AX_X, ALU.add).then_inc(s_["sum_ready"], 1)
                    dve.wait_ge(s_["sum_ready"], NCH * a + c + 1)
                    dve.wait_ge(s_["p_ready"], NCH * a + c)
                    dve.reciprocal(rs[:], sm[:]).then_inc(s_["rs_ready"], 1)

                def turn(a, c):
                    dve.wait_ge(s_["p_ready"], NCH * a + c + 1)
                    dve.wait_ge(s_["pl_ready"], NCH * a + c)
                    dve.transpose(T[:], S[:, c % 2, :, :].rearrange("p g t -> p (g t)")).then_inc(s_["T_ready"], 1)

                def prob_rest(a, c):
                    dve.wait_ge(s_["ph_ready"], NCH * a + c + 1)
                    dve.tensor_tensor(T[:], T[:], pp[:, c % 2, 0, :], ALU.subtract).then_inc(s_["T_rest"], 1)

                def fold(a, c):
                    dve.wait_ge(s_["otr_full"], NCH * a + c + 1)
                    dve.wait_ge(cx_out[c % 2], 16 * OB * (2 * a + c // 2))
                    for hf in range(2):
                        v = ps[:, TR + hf, :].rearrange("p (n w d) -> p n d w", w=2, d=DH1)
                        dve.tensor_reduce(cx[:, c % 2, hf * HB:(hf + 1) * HB, :], v, AX_X, ALU.add).then_inc(s_["cx_ready"], 1)

                def body(i, qkv, att, carried):
                    if qkv:
                        norm_stats(i)
                    if att:
                        max_sub(i - 1, 0)
                    if qkv:
                        normalised(i)
                    if isinstance(i, int) and i == 0:
                        w_los(range(WCH1_Q))
                    if qkv:
                        xT_los(i)
                    if has(i, 0, 1, att, carried):
                        turn(*chunk(i, 0, 1))
                    if isinstance(i, int) and i == 0:
                        w_los(range(WCH1_Q, N_WCH1))
                        dve.wait_ge(const_in, 32)
                    for c in range(NCH):
                        u = 3 * c
                        if qkv:
                            rest(i, u)
                        if c > 0 and has(i, c, 1, att, carried):
                            turn(*chunk(i, c, 1))
                        if att and c > 0:
                            max_sub(i - 1, c)
                        if has(i, c, 1, att, carried):
                            prob_rest(*chunk(i, c, 1))
                        if qkv:
                            rest(i, u + 1)
                        if att:
                            sums(i - 1, c)
                        if qkv:
                            rest(i, u + 2)
                        if has(i, c, 2, att, carried):
                            fold(*chunk(i, c, 2))

                body(0, True, False, False)
                body(1, True, True, False)
                with dve.Fori(2, NSEQ) as i:
                    body(i, True, True, True)
                body(NSEQ, False, True, True)
                body(NSEQ + 1, False, False, True)

            @block.tensor
            def _(pe):
                def transposes_in(i):
                    pe.wait_ge(s_["xn_ready1"], NT * i + NT)
                    for k in range(KD):
                        if k < 2:
                            pe.wait_ge(s_["y_ready"], 4 * i)
                        else:
                            pe.wait_ge(s_["cx_ready"], upto(2 * NCH * (i - 1) - 4))
                        for t in range(NT):
                            last = pe.transpose(ps[:, XT[k], t * P:(t + 1) * P], xin[:, t, k * P:(k + 1) * P], idf[:])
                        last.then_inc(s_["xt_done1"], 1)

                def project(i, u):
                    if 2 <= u < 10:
                        pe.wait_ge(s_["r_ready"], NU * i + u - 1)
                    elif u >= 10:
                        pe.wait_ge(s_["y_ready"], 4 * i + u - 9)
                    if isinstance(i, int) and i == 0 and u % 4 == 0:
                        pe.wait_ge(s_["w_lo_ready1"], WCH1_Q * (u // 4 + 1))
                    for k in range(KD):
                        if u == 0:
                            pe.wait_ge(s_["xT_lo_ready1"], KD * i + k + 1)
                        if u < 8:
                            c = (u // 4 * KD + k) * D + u % 4 * P
                            last = split3(pe, ps[:, MM + u % 2, :], (w_hi[:, c:c + P], w_lo[:, c:c + P]), (xT_hi[:, k, :], xT_lo[:, k, :]), k == 0, k == KD - 1)
                        else:
                            c = (2 * KD + k) * D
                            t = slice((u - 8) * P, (u - 7) * P)
                            last = split3(pe, ps[:, MM + u % 2, :], (xT_hi[:, k, t], xT_lo[:, k, t]), (w_hi[:, c:c + D], w_lo[:, c:c + D]), k == 0, k == KD - 1)
                    last.then_inc(s_["mm_full1"], 1)

                def scores(a, c):
                    s = c % 2
                    pe.wait_ge(qk_in[s], 16 * 12 * (2 * a + c // 2 + 1))
                    pe.wait_ge(s_["sub_ready"], 2 * NCH * a + 2 * c)
                    for g in range(NG):
                        for q in range(TPG):
                            t = TPG * g + q
                            col = (g % HB) * H1
                            last = pe.matmul(ps[32 * q:32 * q + 32, SC + g // HB, col:col + H1], qb[:, s, :, t], kb[:, s, :, t],
                                             start=True, stop=True, skip_group_check=True)
                    last.then_inc(s_["sc_full1"], 1)

                def weighted(a, c):
                    s = c % 2
                    pe.wait_ge(s_["pl_ready"], NCH * a + c + 1)
                    pe.wait_ge(v_in[s], 16 * 8 * (2 * a + c // 2 + 1))
                    pe.wait_ge(s_["o_ready"], 2 * NCH * a + 2 * c)
                    for g in range(NG):
                        out = ps[:, OUT + g // HB, (g % HB) * H1:(g % HB + 1) * H1]
                        p3 = [pp[:, s, w, g * H1:(g + 1) * H1] for w in range(3)]
                        v_hm, v_l0 = (vb[:, s, g, n, :, :, :].rearrange("p q w d -> p (q w d)") for n in range(2))
                        for w in range(3):
                            pe.matmul(out, v_hm, p3[w], start=(w == 0), stop=False, skip_group_check=True)
                        last = pe.matmul(out, v_l0, p3[0], start=False, stop=True, skip_group_check=True)
                    last.then_inc(s_["av_done1"], 1)

                def transposes_out(a, c):
                    pe.wait_ge(s_["o_ready"], 2 * NCH * a + 2 * c + 2)
                    pe.wait_ge(s_["cx_ready"], 2 * NCH * a + 2 * c)
                    for o in range(OA):
                        last = pe.transpose(ps[:, TR + o // 4, (o % 4) * P:(o % 4 + 1) * P], osb[:, o, :, :].rearrange("p b h -> p (b h)"), idf[:])
                    last.then_inc(s_["otr_full"], 1)

                def body(i, qkv, att, carried):
                    if att:
                        scores(i - 1, 0)
                    if has(i, 0, 2, att, carried):
                        weighted(*chunk(i, 0, 2))
                    if qkv:
                        transposes_in(i)
                    for c in range(NCH):
                        u = 3 * c
                        if qkv:
                            project(i, u)
                        if att and c > 0:
                            scores(i - 1, c)
                        if qkv:
                            project(i, u + 1)
                        if c > 0 and has(i, c, 2, att, carried):
                            weighted(*chunk(i, c, 2))
                        if qkv:
                            project(i, u + 2)
                        if has(i, c, 2, att, carried):
                            transposes_out(*chunk(i, c, 2))

                pe.wait_ge(ident_in, 16)
                body(0, True, False, False)
                body(1, True, True, False)
                with pe.Fori(2, NSEQ) as i:
                    body(i, True, True, True)
                body(NSEQ, False, True, True)
                body(NSEQ + 1, False, False, True)


INTER = 1376
FT = -(-INTER // P)
FR = INTER - (FT - 1) * P
CC = 256
NPACK = 8
G_GU, G_D = D // P, INTER // P


def gu_chunks():
    return [(c, min(CC, INTER - c)) for c in range(0, INTER, CC)]


def feed_forward(nc, x1_dram, ctx_dram, xT_dram, out, qw_gu, qz_gu, sc_gu, gi_gu, qw_d, qz_d, sc_d, gi_d):
    gu_tables = [("gu", c, n) for c, n in gu_chunks()]
    DOWN = 2
    tables = gu_tables[:DOWN] + [("d", 0, D)] + gu_tables[DOWN:]

    def gu_table(j):
        return j if j < DOWN else j + 1

    first_units = [(gu_table(0), k) for k in range(KD)]
    step_units = []
    for m in range(FT):
        ahead = [(gu_table(m // 2 + 1), 2 * (m % 2) + n) for n in range(2)] if m // 2 + 1 < len(gu_tables) else []
        step_units.append(ahead + [(DOWN, n) for n in {FT - 2: (m, FT - 1), FT - 1: ()}.get(m, (m,))])
    units = first_units + [u for us in step_units for u in us]
    NUN = len(units)
    with ExitStack() as ctx:
        def sb(name, shape, dt=F32, scope=ctx):
            return scope.enter_context(nc.sbuf_tensor(name, shape, dt))

        def sem(name):
            return ctx.enter_context(nc.semaphore(name))

        gu_hi = sb("gu_hi", [P, KD, 2 * INTER], F32R)
        gu_lo = sb("gu_lo", [P, KD, 2 * INTER], F32R)
        d_hi = sb("d_hi", [P, FT, D], F32R)
        d_lo = sb("d_lo", [P, FT, D], F32R)
        xT_hi = sb("xT2_hi", [P, KD, L], F32R)
        xT_lo = sb("xT2_lo", [P, KD, L], F32R)
        with ExitStack() as index_scope:
            gi = {"gu": sb("idx_gu", [G_GU, D], I32, index_scope), "d": sb("idx_d", [G_D, INTER], I32, index_scope)}
            gf = sb("gf", [G_D, INTER], F32, index_scope)
            gn = sb("gn", [G_D, INTER], F32, index_scope)
        th = sb("th", [P, 2, L])
        gs = sb("gs", [P, 2, L])
        hf = sb("hf", [P, 2, L])
        h_hi = sb("h_hi", [P, 2, L], F32R)
        h_lo = sb("h_lo", [P, 2, L], F32R)
        with ExitStack() as weight_scope:
            shift = sb("shift", [P, 1], U32, weight_scope)
            part = sb("part", [G_D, 1], F32, weight_scope)
            hot = {"gu": sb("hot_gu", [G_GU, D], F32R, weight_scope), "d": sb("hot_d", [G_D, INTER], F32R, weight_scope)}
            stage = sb("stage2", [P, 2, 512], U32, weight_scope)
            nib = sb("nib", [P, 2, 512], U32, weight_scope)
            wf = sb("wf", [P, 2, 512], F32, weight_scope)
            s_hi = sb("s_hi", [G_D, 3, 512], F32R, weight_scope)
            s_lo = sb("s_lo", [G_D, 3, 512], F32R, weight_scope)
            sraw = sb("sraw", [G_D, 512], F32, weight_scope)
            zt = sb("zt", [G_D, 3, 512], F32R, weight_scope)
            znib = sb("znib", [G_D, 512], U32, weight_scope)
            zraw = sb("zraw", [G_D, 64], U32, weight_scope)
        xst = sb("xst", [P, 2, KD, L])
        xa = sb("xa", [P, NT, D])
        xb = sb("xb", [P, NT, D])
        ps = ctx.enter_context(nc.psum_tensor("ps3", [P, 8, 512], F32))
        GATE, UP, ACC = 0, 2, 4
        SG, ZG = GATE + 1, UP + 1

        gi_in = sem("gi_in")
        q_in = [sem(f"q_in{s}") for s in range(2)]
        tab_in = sem("tab_in")
        iota_done, shift_done, hot_done = sem("iota_done"), sem("shift_done"), sem("hot_done")
        s_hi_done, s_lo_done, znib_done, z_done = sem("s_hi_done"), sem("s_lo_done"), sem("znib_done"), sem("z_done")
        nib_done, gathered, wz_done, wf_done = sem("nib_done"), sem("gathered"), sem("wz_done"), sem("wf_done")
        wq_hi_done, wq_lo_done = sem("wq_hi_done"), sem("wq_lo_done")
        xT_in, xst_in, res_in, out_out = sem("xT2_in"), sem("xst_in"), sem("res2_in"), sem("out_out")
        x_hi_done, x_lo_done = sem("x_hi_done"), sem("x_lo_done")
        ctx_in, acc_out = sem("ctx_in"), sem("acc_out")
        gate_full, gu_full, th_done, gs_done, hf_done = sem("gate_full"), sem("gu_full"), sem("th_done"), sem("gs_done"), sem("hf_done")
        h_hi_done, h_lo_done = sem("h_hi_done"), sem("h_lo_done")
        down_done, y_done = sem("down_done"), sem("y_done")

        def groups(n):
            return G_GU if tables[n][0] == "gu" else G_D

        def urows(u):
            n, k = units[u]
            return FR if n == DOWN and k == FT - 1 else P

        def width(n):
            return 2 * tables[n][2] if tables[n][0] == "gu" else D

        def slot(n):
            return 2 if n == DOWN else gu_tables.index(tables[n]) % 2

        def unit_of(n, k):
            return units.index((n, k))

        def slot_used(n):
            j = gu_tables.index(tables[n]) - 2 if n != DOWN else -1
            return unit_of(gu_table(j), KD - 1) + 1 if j >= 0 else 0

        def tab_loads(n):
            return sum(2 * len(pieces(t)) for t in range(n + 1))

        def pieces(n):
            kind, c, m = tables[n]
            return [(c, 0, m), (INTER + c, m, m)] if kind == "gu" else [(0, 0, D)]

        def out_pieces(u, hi):
            n, k = units[u]
            if n != DOWN:
                _, c, m = tables[n]
                return (gu_hi if hi else gu_lo)[:, k, :].rearrange("p (s n) -> p s n", s=2)[:, :, c:c + m], m
            return (d_hi if hi else d_lo)[0:urows(u), k, :].rearrange("p (s n) -> p s n", s=2), D // 2

        def units_of(m):
            first = len(first_units) + sum(len(us) for us in step_units[:m])
            return list(range(first, first + len(step_units[m])))

        def tables_at(m):
            j = m // 2 + 2
            return [gu_table(j)] if m % 2 == 0 and j < len(gu_tables) else []

        def places(m):
            us = units_of(m)
            return us[:-2], us[-2:-1] if len(us) > 1 else us, us[-1:] if len(us) > 1 else []

        FIRST_TABLES = (gu_table(0), gu_table(1), DOWN)

        def rows(m):
            return FR if m == FT - 1 else P

        with nc.Block() as block:

            @block.sync
            def _(sp):
                for kind, src, g, n in (("gu", gi_gu, G_GU, D), ("d", gi_d, G_D, INTER)):
                    sp.dma_start(gi[kind][:], bass.AP(src.tensor, 0, [[0, g], [1, n]])).then_inc(gi_in, 16)

                def table(n):
                    g = groups(n)
                    sp.wait_ge(s_lo_done, n)
                    sp.wait_ge(znib_done, NPACK * n)
                    sc, qz = (sc_d, qz_d) if n == DOWN else (sc_gu, qz_gu)
                    for c, t, m in pieces(n):
                        sp.dma_start(sraw[0:g, t:t + m], sc[:, c:c + m]).then_inc(tab_in, 16)
                        sp.dma_start(zraw[0:g, t // NPACK:(t + m) // NPACK], qz[:, c // NPACK:(c + m) // NPACK]).then_inc(tab_in, 16)

                def packed(u):
                    n, k = units[u]
                    qw = qw_d if n == DOWN else qw_gu
                    cols = qw.shape[1]
                    if u >= 2:
                        sp.wait_ge(nib_done, u - 1)
                    for c, t, m in pieces(n):
                        src = bass.AP(qw.tensor, (k * P // NPACK) * cols + c, [[cols, urows(u) // NPACK], [0, NPACK], [1, m]])
                        sp.dma_start(stage[0:urows(u), u % 2, t:t + m], src).then_inc(q_in[u % 2], 16)

                def load_xst(i):
                    sp.dma_start(xst[:].rearrange("p s k t -> p s (k t)"), xT_dram[bass.ds(i, 1), :, :, :].rearrange("o s p n -> p (o s) n")).then_inc(xst_in, 16)

                def load_res(i):
                    for dst, src, done in ((xa, x1_dram, res_in), (xb, ctx_dram, ctx_in)):
                        sp.dma_start(dst[:], src[bass.ds(i * L, L), :].rearrange("(t p) d -> p t d", p=P)).then_inc(done, 16)

                def store(i):
                    for t in range(NT):
                        sp.wait_ge(y_done, NT * i + t + 1)
                        sp.dma_start(out[bass.ds(i * L + t * P, P), :], xa[:, t, :]).then_inc(out_out, 16)

                def body(i, last):
                    if not last:
                        sp.wait_ge(x_hi_done, KD * i)
                        sp.wait_ge(x_lo_done, KD * i)
                        load_xst(i + 1)
                    store(i - 1)
                    sp.wait_ge(out_out, 64 * i)
                    load_res(i)

                table(gu_table(0))
                packed(0)
                packed(1)
                table(gu_table(1))
                for u in range(2, len(first_units)):
                    packed(u)
                table(DOWN)
                for part, xT in ((0, xT_hi), (1, xT_lo)):
                    sp.dma_start(xT[:].rearrange("p k t -> p (k t)").bitcast(F32), xT_dram[0, part, :, :]).then_inc(xT_in, 16)
                for m in range(FT):
                    for u in units_of(m):
                        packed(u)
                    for n in tables_at(m):
                        table(n)
                sp.wait_ge(wq_lo_done, NUN)
                load_xst(1)
                load_res(0)
                with sp.Fori(1, NSEQ - 1) as i:
                    body(i, False)
                body(NSEQ - 1, True)
                store(NSEQ - 1)
                sp.wait_ge(out_out, 64 * NSEQ)

            @block.gpsimd
            def _(pool):
                pool.iota(shift[:], [[0, 1]], base=0, channel_multiplier=4).then_inc(iota_done, 1)
                pool.iota(part[:], [[0, 1]], base=0, channel_multiplier=1, allow_small_or_imprecise_dtypes=True).then_inc(iota_done, 1)

                def table(n):
                    s, g, m = slot(n), groups(n), width(n)
                    pool.wait_ge(s_hi_done, n + 1)
                    pool.tensor_tensor(s_lo[0:g, s, 0:m], sraw[0:g, 0:m], s_hi[0:g, s, 0:m].bitcast(F32), ALU.subtract).then_inc(s_lo_done, 1)

                def split(u):
                    pool.wait_ge(wq_hi_done, u + 1)
                    (hi, m), (lo, _) = out_pieces(u, True), out_pieces(u, False)
                    v = wf[0:urows(u), u % 2, 0:2 * m].rearrange("p (s n) -> p s n", s=2)
                    pool.tensor_tensor(lo, v, hi.bitcast(F32), ALU.subtract).then_inc(wq_lo_done, 1)

                def body(i):
                    pool.wait_ge(ctx_in, 16 * i + 16)
                    for t in range(NT):
                        pool.wait_ge(acc_out, NT * i + t + 1)
                        pool.tensor_tensor(xa[:, t, :], xa[:, t, :], xb[:, t, :], ALU.add).then_inc(y_done, 1)

                for n in FIRST_TABLES[:2]:
                    table(n)
                for u in range(len(first_units)):
                    split(u)
                table(DOWN)
                for m in range(FT):
                    for u in units_of(m):
                        split(u)
                    for n in tables_at(m):
                        table(n)
                body(0)
                with pool.Fori(1, NSEQ) as i:
                    body(i)

            @block.scalar
            def _(act):
                def table(n):
                    s, g, m = slot(n), groups(n), width(n)
                    act.wait_ge(tab_in, 16 * tab_loads(n))
                    act.wait_ge(gathered, slot_used(n))
                    act.activation(s_hi[0:g, s, 0:m], sraw[0:g, 0:m], ACT.Copy).then_inc(s_hi_done, 1)

                def split(u):
                    act.wait_ge(wf_done, u + 1)
                    hi, m = out_pieces(u, True)
                    act.activation(hi, wf[0:urows(u), u % 2, 0:2 * m].rearrange("p (s n) -> p s n", s=2), ACT.Copy).then_inc(wq_hi_done, 1)

                def gate_tanh(i, m, s):
                    r = rows(m)
                    act.wait_ge(gate_full, FT * i + m + 1)
                    act.wait_ge(gs_done, FT * i + max(0, m - 1))
                    act.activation(th[0:r, m % 2, :], ps[0:r, GATE + s, :], ACT.Tanh, scale=0.5).then_inc(th_done, 1)

                def h_first(i, m):
                    r = rows(m)
                    act.wait_ge(hf_done, FT * i + m + 1)
                    act.wait_ge(down_done, FT * i + max(0, m - 1))
                    act.activation(h_hi[0:r, m % 2, :], hf[0:r, m % 2, :], ACT.Copy).then_inc(h_hi_done, 1)

                def body(i):
                    act.wait_ge(xst_in, 16 * i)
                    act.wait_ge(gu_full, FT * i)
                    for k in range(KD):
                        act.activation(xT_hi[:, k, :], xst[:, 0, k, :], ACT.Copy).then_inc(x_hi_done, 1)
                    for m in range(FT):
                        gate_tanh(i, m, m % 2)
                        h_first(i, m)

                for n in FIRST_TABLES[:2]:
                    table(n)
                for u in range(len(first_units)):
                    split(u)
                table(DOWN)
                for m in range(FT):
                    early, mid, late = places(m)
                    for u in early:
                        split(u)
                    gate_tanh(0, m, 0)
                    h_first(0, m)
                    for u in mid + late:
                        split(u)
                    for n in tables_at(m):
                        table(n)
                with act.Fori(1, NSEQ) as i:
                    body(i)

            @block.vector
            def _(dve):
                n_hot = [0]

                def step(ins):
                    n_hot[0] += 1
                    ins.then_inc(hot_done, 1)
                    dve.wait_ge(hot_done, n_hot[0])

                def one_hot(kind, g, n):
                    f, t = gf[0:g, 0:n], gn[0:g, 0:n]
                    step(dve.tensor_copy(f, gi[kind][:]))
                    step(dve.tensor_scalar(t, f, 0.0, float(g), ALU.is_lt, ALU.mult))
                    step(dve.tensor_tensor(f, f, t, ALU.add))
                    step(dve.tensor_scalar(f, f, 0.0, float(g - 1), ALU.max, ALU.min))
                    step(dve.tensor_scalar(hot[kind][:], f, part[0:g, :], None, ALU.is_equal))

                def table(n):
                    s, g, m = slot(n), groups(n), width(n)
                    dve.wait_ge(tab_in, 16 * tab_loads(n))
                    dve.wait_ge(z_done, n)
                    dve.wait_ge(gathered, slot_used(n))
                    zv = znib[0:g, 0:m].rearrange("g (c b) -> g c b", b=NPACK)
                    for b in range(NPACK):
                        dve.tensor_scalar(zv[:, :, b], zraw[0:g, 0:m // NPACK], 4 * b, 15, ALU.logical_shift_right, ALU.bitwise_and).then_inc(znib_done, 1)
                    dve.wait_ge(znib_done, NPACK * (n + 1))
                    dve.tensor_scalar(zt[0:g, s, 0:m], znib[0:g, 0:m], 1.0, None, ALU.add).then_inc(z_done, 1)

                def nibbles(u):
                    r, m = urows(u), width(units[u][0])
                    dve.wait_ge(q_in[u % 2], 16 * sum(len(pieces(units[v][0])) for v in range(u + 1) if v % 2 == u % 2))
                    dve.wait_ge(wz_done, max(0, u - 1))
                    dve.tensor_scalar(nib[0:r, u % 2, 0:m], stage[0:r, u % 2, 0:m], shift[0:r, :], 15, ALU.logical_shift_right, ALU.bitwise_and).then_inc(nib_done, 1)

                def scaled(u):
                    if u + 1 < NUN:
                        nibbles(u + 1)
                    r, m = urows(u), width(units[u][0])
                    v = wf[0:r, u % 2, 0:m]
                    dve.wait_ge(gathered, u + 1)
                    dve.wait_ge(nib_done, u + 1)
                    if u >= 2:
                        dve.wait_ge(wq_lo_done, u - 1)
                    dve.tensor_tensor(v, nib[0:r, u % 2, 0:m], ps[0:r, ZG, 0:m], ALU.subtract).then_inc(wz_done, 1)
                    dve.wait_ge(wz_done, u + 1)
                    dve.tensor_tensor(v, v, ps[0:r, SG, 0:m], ALU.mult).then_inc(wf_done, 1)

                def gated(i, m, s):
                    r, o = rows(m), m % 2
                    dve.wait_ge(th_done, FT * i + m + 1)
                    dve.wait_ge(h_lo_done, FT * i + max(0, m - 1))
                    dve.scalar_tensor_tensor(gs[0:r, o, :], th[0:r, o, :], 1.0, ps[0:r, GATE + s, :], ALU.add, ALU.mult).then_inc(gs_done, 1)
                    dve.wait_ge(gs_done, FT * i + m + 1)
                    dve.wait_ge(gu_full, FT * i + m + 1)
                    dve.scalar_tensor_tensor(hf[0:r, o, :], gs[0:r, o, :], 0.5, ps[0:r, UP + s, :], ALU.mult, ALU.mult).then_inc(hf_done, 1)

                def h_rest(i, m):
                    r, o = rows(m), m % 2
                    dve.wait_ge(h_hi_done, FT * i + m + 1)
                    dve.tensor_tensor(h_lo[0:r, o, :], hf[0:r, o, :], h_hi[0:r, o, :].bitcast(F32), ALU.subtract).then_inc(h_lo_done, 1)

                def sums(i):
                    dve.wait_ge(res_in, 16 * i + 16)
                    dve.wait_ge(down_done, FT * i + FT)
                    for t in range(NT):
                        dve.tensor_tensor(xa[:, t, :], ps[:, ACC + t, :], xa[:, t, :], ALU.add).then_inc(acc_out, 1)

                def next_x(i):
                    dve.wait_ge(xst_in, 16 * i)
                    dve.wait_ge(gu_full, FT * i)
                    for k in range(KD):
                        dve.tensor_copy(xT_lo[:, k, :], xst[:, 1, k, :]).then_inc(x_lo_done, 1)

                def body(i):
                    next_x(i)
                    sums(i - 1)
                    for m in range(FT):
                        gated(i, m, m % 2)
                        h_rest(i, m)

                dve.wait_ge(iota_done, 2)
                dve.tensor_scalar(shift[:], shift[:], 31, None, ALU.bitwise_and).then_inc(shift_done, 1)
                dve.wait_ge(gi_in, 32)
                dve.wait_ge(shift_done, 1)
                one_hot("gu", G_GU, D)
                table(gu_table(0))
                nibbles(0)
                for u in range(len(first_units)):
                    scaled(u)
                    if u == 0:
                        table(gu_table(1))
                        one_hot("d", G_D, INTER)
                for m in range(FT):
                    early, mid, late = places(m)
                    for u in early:
                        scaled(u)
                    if m == 0:
                        table(DOWN)
                    gated(0, m, 0)
                    for u in mid:
                        scaled(u)
                    h_rest(0, m)
                    for u in late:
                        scaled(u)
                    for n in tables_at(m):
                        table(n)
                body(1)
                with dve.Fori(2, NSEQ) as i:
                    body(i)
                sums(NSEQ - 1)

            @block.tensor
            def _(pe):
                def gather(u):
                    n, k = units[u]
                    kind, s, g, r, m = tables[n][0], slot(n), groups(n), urows(u), width(n)
                    pe.wait_ge(hot_done, 5 if kind == "gu" else 10)
                    pe.wait_ge(s_lo_done, n + 1)
                    pe.wait_ge(z_done, n + 1)
                    pe.wait_ge(wf_done, u)
                    oh = hot[kind][:, k * P:k * P + r]
                    pe.matmul(ps[0:r, ZG, 0:m], oh, zt[0:g, s, 0:m], start=True, stop=True)
                    pe.matmul(ps[0:r, SG, 0:m], oh, s_hi[0:g, s, 0:m], start=True, stop=False)
                    pe.matmul(ps[0:r, SG, 0:m], oh, s_lo[0:g, s, 0:m], start=False, stop=True).then_inc(gathered, 1)

                def half(i, m, s, bank, c0):
                    r = rows(m)
                    c = slice(c0 + m * P, c0 + m * P + r)
                    for k in range(KD):
                        if m == 0 and bank == GATE and not (isinstance(i, int) and i == 0):
                            pe.wait_ge(x_hi_done, KD * (i - 1) + k + 1)
                            pe.wait_ge(x_lo_done, KD * (i - 1) + k + 1)
                        if isinstance(i, int) and i == 0:
                            pe.wait_ge(wq_lo_done, unit_of(gu_table(m // 2), k) + 1)
                        last = split3(pe, ps[0:r, bank + s, :], (gu_hi[:, k, c], gu_lo[:, k, c]), (xT_hi[:, k, :], xT_lo[:, k, :]), k == 0, k == KD - 1)
                    last.then_inc(gate_full if bank == GATE else gu_full, 1)

                def gate_up(i, m):
                    pe.wait_ge(hf_done, FT * i + max(0, m - 1))
                    half(i, m, m % 2, GATE, 0)
                    half(i, m, m % 2, UP, INTER)

                def down(i, m):
                    r, s = rows(m), m % 2
                    pe.wait_ge(h_lo_done, FT * i + m + 1)
                    if m == 0:
                        pe.wait_ge(acc_out, NT * i)
                    if isinstance(i, int) and i == 0:
                        pe.wait_ge(wq_lo_done, unit_of(DOWN, m) + 1)
                    for t in range(NT):
                        ts = slice(t * P, (t + 1) * P)
                        last = split3(pe, ps[:, ACC + t, :], (h_hi[0:r, s, ts], h_lo[0:r, s, ts]), (d_hi[0:r, m, :], d_lo[0:r, m, :]), m == 0, m == FT - 1)
                    last.then_inc(down_done, 1)

                def body(i):
                    gate_up(i, 0)
                    for m in range(FT):
                        if m + 1 < FT:
                            gate_up(i, m + 1)
                        down(i, m)

                for u in range(len(first_units)):
                    gather(u)
                pe.wait_ge(xT_in, 32)
                for m in range(FT):
                    early, mid, late = places(m)
                    pe.wait_ge(hf_done, m)
                    half(0, m, 0, GATE, 0)
                    for u in early:
                        gather(u)
                    half(0, m, 0, UP, INTER)
                    for u in mid:
                        gather(u)
                    if m > 0:
                        down(0, m - 1)
                    for u in late:
                        gather(u)
                down(0, FT - 1)
                with pe.Fori(1, NSEQ) as i:
                    body(i)


def block_kernel(nc, x, w0, bias_f, proj_b, base_b, w1, bv1, qw_gu, qz_gu, sc_gu, gi_gu, qw_d, qz_d, sc_d, gi_d,
                 ident, ident_bf, causal, iota8, out):
    def scratch(name, shape, dt=F32):
        return nc.dram_tensor(name, shape, dt, kind="Internal").ap()

    x1_dram = scratch("x1_dram", [NSEQ * L, D])
    ctx_dram = scratch("ctx_dram", [NSEQ, L, D])
    xT_dram = scratch("xT_dram", [NSEQ, 2, P, KD * L])
    q3 = scratch("q3", [NSEQ, 3, D, L], BF16)
    k3 = scratch("k3", [NSEQ, 3, D, L], BF16)
    v3 = scratch("v3", [NSEQ, L, H1, 3 * DH1], BF16)
    layer0(nc, x, w0, bias_f, proj_b, base_b, ident, ident_bf, causal, iota8, x1_dram)
    attention1(nc, x1_dram, w1, bias_f, bv1, ident, q3, k3, v3, xT_dram, ctx_dram)
    feed_forward(nc, x1_dram, ctx_dram.rearrange("s t d -> (s t) d"), xT_dram, out, qw_gu, qz_gu, sc_gu, gi_gu, qw_d, qz_d, sc_d, gi_d)


def tiles(a):
    import numpy as np
    return np.ascontiguousarray(a.reshape(-1, P, a.shape[1]).transpose(1, 0, 2).reshape(P, -1))


def kernel(**inputs):
    import ml_dtypes
    import numpy as np
    import concourse.bacc as bacc
    from concourse.bass_utils import run_bass_kernel_spmd

    a = {k: np.asarray(v) for k, v in inputs.items()}
    w0 = np.concatenate([
        tiles(a["L0_attn_conv_w"].reshape(TAPS * D, 3 * W)),
        a["L0_attn_wq"].reshape(W, H0 * DH0), a["L0_attn_wk"].reshape(W, H0 * DH0), a["L0_attn_wv"].reshape(W, H0 * DH0),
        tiles(a["L0_attn_wo"].reshape(H0 * DH0, W)), a["L0_attn_proj_w"], tiles(a["L0_ffn_W_base"].T),
        tiles(np.concatenate([a["L0_ffn_A_stack"].reshape(ER, D).T, a["L0_ffn_W_router"].T, np.zeros((D, AR - ER - NE), np.float32)], 1)),
        a["L0_ffn_B_stack"].transpose(0, 2, 1).reshape(ER, D)], 1)
    bias_f = np.concatenate([a[n].reshape(-1, P).T for n in (
        "L0_attn_conv_b", "L0_attn_bq", "L0_attn_bk", "L0_attn_bv", "L0_attn_bo", "L1_attn_bq", "L1_attn_bk")], 1)
    w1 = np.concatenate([tiles(a[n].T) for n in ("L1_attn_wq", "L1_attn_wk", "L1_attn_wv")], 1)
    above = np.where(np.arange(P)[None, :] <= np.arange(P)[:, None], 0.0, -1e30).astype(ml_dtypes.bfloat16)
    arrays = {
        "x": a["L0_attn_inputs"].reshape(NSEQ * L, D), "w0": w0, "bias_f": bias_f,
        "proj_b": a["L0_attn_proj_b"], "base_b": a["L0_ffn_b_base"], "w1": w1, "bv1": a["L1_attn_bv"],
        "qw_gu": a["L1_ffn_qweight_gu"], "qz_gu": a["L1_ffn_qzeros_gu"], "sc_gu": a["L1_ffn_scales_gu"], "gi_gu": a["L1_ffn_g_idx_gu"],
        "qw_d": a["L1_ffn_qweight_down"], "qz_d": a["L1_ffn_qzeros_down"], "sc_d": a["L1_ffn_scales_down"], "gi_d": a["L1_ffn_g_idx_down"],
        "ident": np.eye(P, dtype=np.float32), "ident_bf": np.eye(P).astype(ml_dtypes.bfloat16),
        "causal": np.tile(above, (1, HG)), "iota8": np.tile(np.arange(NE, dtype=np.float32), (P, NT)),
    }
    arrays = {k: np.ascontiguousarray(v) for k, v in arrays.items()}
    nc = bacc.Bacc("TRN2", target_bir_lowering=False, num_devices=1)
    args = {k: nc.dram_tensor(k, v.shape, mybir.dt.from_np(v.dtype), kind="ExternalInput").ap() for k, v in arrays.items()}
    out = nc.dram_tensor("out", [NSEQ * L, D], F32, kind="ExternalOutput").ap()
    block_kernel(nc, **args, out=out)
    r = run_bass_kernel_spmd(nc, [arrays], core_ids=[0])
    return r.results[0]["out"].reshape(NSEQ, L, D)
```

```python
from contextlib import ExitStack

import concourse.bass as bass
from concourse import mybir

F32 = mybir.dt.float32
F32R = mybir.dt.float32r
BF16 = mybir.dt.bfloat16
U32 = mybir.dt.uint32
I32 = mybir.dt.int32
ALU = mybir.AluOpType
ACT = mybir.ActivationFunctionType
AX_X = mybir.AxisListType.X

P = 128
NSEQ, L, D = 4, 512, 512
NT = L // P
KD = D // P
TAPS = 3
W = 128
H0, DH0 = 16, 64
HG = 4
NHG = H0 // HG
NBLK = L // P
STEPS = NHG * NBLK
NE, RANK = 8, 16
ER = NE * RANK
EPS = 1e-5
LORA_SCALE = 32.0 / RANK
H1, DH1 = 32, 16

C_CONV = 0
C_WQ = C_CONV + TAPS * KD * 3 * W
C_WK = C_WQ + H0 * DH0
C_WV = C_WK + H0 * DH0
C_WO = C_WV + H0 * DH0
C_PROJ = C_WO + (H0 * DH0 // P) * W
C_BASE = C_PROJ + D
C_AR = C_BASE + KD * D
AR = 256
C_B = C_AR + KD * AR
N_A = C_B + D
WCH = 800
N_WCH = N_A // WCH
assert N_WCH * WCH == N_A
STAGED = (2, 4, 2)
NST = sum(STAGED)
CONV_WCH = -(-C_WQ // WCH)
B_CONV, B_Q, B_K, B_V, B_O, B_Q1, B_K1 = 0, 3, 11, 19, 27, 28, 32
N_BF = 36


def spread(ap, n):
    return ap.unsqueeze(2).broadcast_to([ap.shape[0], ap.shape[1], n])


def split3(pe, out, lhs, rhs, start, stop):
    pe.matmul(out, lhs[0], rhs[0], start=start, stop=False, skip_group_check=True)
    pe.matmul(out, lhs[0], rhs[1], start=False, stop=False, skip_group_check=True)
    return pe.matmul(out, lhs[1], rhs[0], start=False, stop=stop, skip_group_check=True)


def bank_uses():
    uses = [("conv", "AD")] * 3 + [("ar", "A")] * NT
    uses += [(n, e) for n, e in (("q", "A"), ("q", "A"), ("k", "AD"), ("k", "AD"), ("v", "D"), ("v", "D"))] * NHG
    uses += [("hT", "AD")] + [("x1", "D")] * NT
    return uses


USES = bank_uses()
assert len(USES) % 2 == 0
ACT_USES = sum("A" in e for _, e in USES)
DVE_USES = sum("D" in e for _, e in USES)


def freed(letter, upto):
    return sum(letter in e for _, e in USES[:upto])


def layer0(nc, x, w0, bias_f, proj_b, base_b, ident, ident_bf, causal, iota8, x1_dram):
    with ExitStack() as ctx:
        def sb(name, shape, dt=F32):
            return ctx.enter_context(nc.sbuf_tensor(name, shape, dt))

        def sem(name):
            return ctx.enter_context(nc.semaphore(name))

        w_hi = sb("w0_hi", [P, N_A], F32R)
        w_lo = sb("w0_lo", [P, N_A], F32R)
        xin = sb("xin", [P, NT, D])
        xres = sb("xres", [P, 2, D])
        xT_hi = sb("xT_hi", [P, KD, L + 2], F32R)
        xT_lo = sb("xT_lo", [P, KD, L + 2], F32R)
        c_hi = sb("c_hi", [P, 3, L], F32R)
        c_lo = sb("c_lo", [P, 3, L], F32R)
        qh = sb("qh", [P, 2, 2, L])
        kh = sb("kh", [P, 2, 2, 2, L])
        vh = sb("vh", [P, 2, NBLK, HG * DH0])
        prob = sb("prob", [P, 3, HG * P])
        probT = sb("probT", [P, 2, HG * P])
        o_hi = sb("o_hi", [P, 2, L], F32R)
        o_lo = sb("o_lo", [P, 2, L], F32R)
        a_hi = sb("a_hi", [P, L], F32R)
        a_lo = sb("a_lo", [P, L], F32R)
        har = sb("har", [P, NT, ER + NE])
        hT_hi = sb("hT_hi", [P, L], F32R)
        hT_lo = sb("hT_lo", [P, L], F32R)
        bf = sb("bf", [P, N_BF])
        brow = sb("brow", [P, D])
        idf = sb("idf", [P, P])
        idb = sb("idb", [P, P], BF16)
        neg = sb("neg", [P, HG * P], BF16)
        io8 = sb("io8", [P, NT * NE])
        mx = sb("mx", [P, 3, HG])
        nmx = sb("nmx", [P, 3, HG])
        sums = sb("sums", [P, 3, HG])
        rsum = sb("rsum", [P, 3, HG])
        stats = sb("stats", [P, NT, 6])
        mv = sb("mv", [P, NT, 2])
        veps = sb("veps", [P, NT])
        rstd = sb("rstd", [P, NT])
        mhalf = sb("mhalf", [P, NT])
        rmx = sb("rmx", [P, NT])
        rp = sb("rp", [P, NT, NE])
        rs = sb("rs", [P, NT])
        top = sb("top", [P, NT, 8])
        topi = sb("topi", [P, NT, 8], U32)
        topf = sb("topf", [P, NT, 8])
        wsel = sb("wsel", [P, NT, 2])
        eq = sb("eq", [P, 2, NT, NE])
        comb = sb("comb", [P, NT, NE])
        ps = ctx.enter_context(nc.psum_tensor("ps0", [P, 8, 512], F32))
        MM, SC, PT, AV, WO = 0, 2, 4, 5, 7
        XT_BANKS = (SC, SC + 1, PT, AV)
        flat = [qh[:].rearrange("p a b t -> p (a b t)"), kh[:].rearrange("p a b c t -> p (a b c t)"), vh[:].rearrange("p a b n -> p (a b n)")]
        stage = [t[:, j * WCH:(j + 1) * WCH] for t, n in zip(flat, STAGED) for j in range(n)]
        brow2 = prob[:, 2, :]

        const_in, ident_in, carrier = sem("const_in"), sem("ident_in"), sem("carrier")
        w_in = [sem(f"w_in{s}") for s in range(NST)]
        x_in = [sem(f"x_in{t}") for t in range(NT)]
        res_in = [sem(f"res_in{s}") for s in range(2)]
        x1_out = [sem(f"x1_out{s}") for s in range(2)]
        w_hi_ready, w_lo_ready = sem("w_hi_ready"), sem("w_lo_ready")
        zeroed, mhalf_set = sem("zeroed"), sem("mhalf_set")
        brow_ready = sem("brow_ready")
        st_done, ve_ready, rstd_ready, xn_ready = sem("st_done"), sem("ve_ready"), sem("rstd_ready"), sem("xn_ready")
        xt_done, xT_hi_ready, xT_lo_ready = sem("xt_done"), sem("xT_hi_ready"), sem("xT_lo_ready")
        mm_full, mm_act, mm_dve = sem("mm_full"), sem("mm_act"), sem("mm_dve")
        router_exp, router_chain, comb_ready = sem("router_exp"), sem("router_chain"), sem("comb_ready")
        sc_full, mx_ready, nmx_ready, exp_done = sem("sc_full"), sem("mx_ready"), sem("nmx_ready"), sem("exp_done")
        rsum_ready, prob_ready, tr_full, probT_ready = sem("rsum_ready"), sem("prob_ready"), sem("tr_full"), sem("probT_ready")
        av_done, o_hi_ready, o_lo_ready, wo_done = sem("av_done"), sem("o_hi_ready"), sem("o_lo_ready"), sem("wo_done")
        a_hi_ready, a_lo_ready = sem("a_hi_ready"), sem("a_lo_ready")
        res_ready, x1_ready = sem("res_ready"), sem("x1_ready")

        def carry(eng):
            eng.sem_inc(carrier, 1)

        def wt(c, n):
            return w_hi[:, c:c + n], w_lo[:, c:c + n]

        U_AR = 3
        U_QKV = U_AR + NT
        U_HT = U_QKV + 6 * NHG
        U_X1 = U_HT + 1
        NU = len(USES)
        N_CONST = 6
        S_Q, S_K, S_V = 1, 2, 3
        S_STATS, S_RSTD, S_NORM = range(6, 6 + NT), 11, range(15, 15 + NT)
        S_ROUTER = (0, 4, 5, 6, 12, 13)
        R_STEPS = 13

        def use_act(hg, k):
            return U_QKV + 6 * hg + k

        with nc.Block() as block:

            @block.sync
            def _(sp):
                def load_x(i):
                    for t in range(NT):
                        sp.dma_start(xin[:, t, :], x[bass.ds(i * L + t * P, P), :]).then_inc(x_in[t], 16)

                def load_w(steps):
                    for j in steps:
                        if j >= NST:
                            sp.wait_ge(w_hi_ready, j - NST + 1)
                            sp.wait_ge(w_lo_ready, j - NST + 1)
                        sp.dma_start(stage[j % NST], w0[:, j * WCH:(j + 1) * WCH]).then_inc(w_in[j % NST], 16)

                load_x(0)
                sp.dma_start(idf[:], ident).then_inc(ident_in, 16)
                load_w(range(2))
                sp.dma_start(bf[:], bias_f).then_inc(const_in, 16)
                load_w(range(2, NST))
                sp.dma_start(idb[:], ident_bf).then_inc(const_in, 16)
                sp.dma_start(neg[:], causal).then_inc(const_in, 16)
                sp.dma_start(io8[:], iota8).then_inc(const_in, 16)
                sp.dma_start(brow[:], bass.AP(proj_b.tensor, 0, [[0, P], [1, D]])).then_inc(const_in, 16)
                sp.dma_start(brow2, bass.AP(base_b.tensor, 0, [[0, P], [1, D]])).then_inc(const_in, 16)
                load_w(range(NST, N_WCH))

                def body(i, last):
                    for s in range(2):
                        sp.wait_ge(x1_out[s], 32 * i)
                        sp.dma_start(xres[:, s, :], x[bass.ds(i * L + s * P, P), :]).then_inc(res_in[s], 16)
                    if not last:
                        sp.wait_ge(xt_done, KD * i + KD)
                        load_x(i + 1)
                    for t in range(NT):
                        sp.wait_ge(x1_ready, NT * i + t + 1)
                        sp.dma_start(x1_dram[bass.ds(i * L + t * P, P), :], xres[:, t % 2, :]).then_inc(x1_out[t % 2], 16)
                        if t < 2:
                            sp.wait_ge(x1_out[t], 32 * i + 16)
                            sp.dma_start(xres[:, t, :], x[bass.ds(i * L + (t + 2) * P, P), :]).then_inc(res_in[t], 16)

                body(0, False)
                with sp.Fori(1, NSEQ - 1) as i:
                    body(i, False)
                body(NSEQ - 1, True)
                for s in range(2):
                    sp.wait_ge(x1_out[s], 32 * NSEQ)

            @block.gpsimd
            def _(pool):
                pool.memset(mhalf[:], -0.5).then_inc(mhalf_set, 1)
                for b in (0, L + 1):
                    pool.memset(xT_hi[:, :, b:b + 1].bitcast(F32), 0.0).then_inc(zeroed, 1)
                    pool.memset(xT_lo[:, :, b:b + 1].bitcast(F32), 0.0).then_inc(zeroed, 1)
                pool.wait_ge(mhalf_set, 1)

                def rstds(n):
                    pool.wait_ge(ve_ready, n + 1)
                    pool.tensor_tensor(rstd[:], veps[:], mhalf[:], ALU.pow).then_inc(rstd_ready, 1)

                def residual(i, t):
                    pool.wait_ge(res_in[t % 2], 32 * i + 16 * (t // 2) + 16)
                    pool.tensor_tensor(xres[:, t % 2, :], xres[:, t % 2, :], brow[:], ALU.add).then_inc(res_ready, 1)

                def body(i, last):
                    for s in range(STEPS):
                        pool.wait_ge(rsum_ready, STEPS * i + s + 1)
                        pv = prob[:, s % 3, :].rearrange("p (h k) -> p h k", h=HG)
                        pool.tensor_tensor(pv, pv, spread(rsum[:, s % 3, :], P), ALU.mult).then_inc(prob_ready, 1)
                        if s == S_RSTD and not last:
                            rstds(i + 1)
                    for t in range(NT):
                        residual(i, t)

                rstds(0)
                pool.wait_ge(const_in, 16 * N_CONST)
                pool.tensor_tensor(brow[:], brow[:], brow2, ALU.add).then_inc(brow_ready, 1)
                pool.wait_ge(w_lo_ready, N_WCH)
                pool.wait_ge(w_hi_ready, N_WCH)
                pool.memset(kh[:], 0.0).then_inc(zeroed, 1)
                pool.wait_ge(brow_ready, 1)
                body(0, False)
                with pool.Fori(1, NSEQ - 1) as i:
                    body(i, False)
                body(NSEQ - 1, True)

            @block.scalar
            def _(act):
                def w_his(steps):
                    for j in steps:
                        act.wait_ge(w_in[j % NST], 16 * (j // NST) + 16)
                        act.activation(w_hi[:, j * WCH:(j + 1) * WCH], stage[j % NST], ACT.Copy).then_inc(w_hi_ready, 1)

                def xT_hi_copy(i):
                    act.wait_ge(mm_full, NU * i)
                    for k in range(KD):
                        act.wait_ge(xt_done, KD * i + k + 1)
                        act.activation(xT_hi[:, k, 1:L + 1], ps[:, XT_BANKS[k], :], ACT.Copy).then_inc(xT_hi_ready, 1)

                def full(i, u):
                    act.wait_ge(mm_full, NU * i + u + 1)

                def q_full(i, hg):
                    act.wait_ge(sc_full, STEPS * i + max(0, NBLK * (hg - 1)))
                    for hp in range(2):
                        full(i, use_act(hg, hp))
                        b = bf[:, B_Q + 2 * hg + hp:B_Q + 2 * hg + hp + 1]
                        act.activation(qh[:, hg % 2, hp, :], ps[:, (use_act(hg, hp)) % 2, :], ACT.Identity, bias=b).then_inc(mm_act, 1)

                def k_even(i, hg):
                    for hp in range(2):
                        u = use_act(hg, 2 + hp)
                        full(i, u)
                        act.activation(kh[0:DH0, hg % 2, hp, 0, :], ps[0:DH0, u % 2, :], ACT.Identity,
                                       bias=bf[0:DH0, B_K + 2 * hg + hp:B_K + 2 * hg + hp + 1]).then_inc(mm_act, 1)

                def exps(i, s):
                    act.wait_ge(nmx_ready, STEPS * i + s + 1)
                    act.wait_ge(tr_full, STEPS * i + max(0, s - 2))
                    for h in range(HG):
                        e = act.activation(prob[:, s % 3, h * P:(h + 1) * P], ps[:, SC + s % 2, h * P:(h + 1) * P], ACT.Exp,
                                           bias=nmx[:, s % 3, h:h + 1], scale=DH0 ** -0.5, accum_out=sums[:, s % 3, h:h + 1])
                    e.then_inc(exp_done, 1)

                def o_his(i, hg):
                    act.wait_ge(av_done, STEPS * i + NBLK * (hg + 1))
                    act.wait_ge(wo_done, NHG * i + hg)
                    for hp in range(2):
                        act.activation(o_hi[:, hp, :], ps[:, AV + hp, :], ACT.Identity,
                                       bias=bf[:, B_V + 2 * hg + hp:B_V + 2 * hg + hp + 1]).then_inc(o_hi_ready, 1)

                def body(i, last):
                    for m in range(3):
                        full(i, m)
                        act.wait_ge(av_done, STEPS * i)
                        act.activation(c_hi[:, m, :], ps[:, m % 2, :], ACT.Identity, bias=bf[:, B_CONV + m:B_CONV + m + 1]).then_inc(mm_act, 1)
                    for t in range(NT):
                        full(i, U_AR + t)
                        act.wait_ge(mm_full, NU * i)
                        act.activation(har[:, t, :], ps[:, (U_AR + t) % 2, 0:ER + NE], ACT.Copy).then_inc(mm_act, 1)
                    if isinstance(i, int) and i == 0:
                        act.wait_ge(w_lo_ready, N_WCH)
                        act.wait_ge(zeroed, 5)
                    q_full(i, 0)
                    k_even(i, 0)
                    for s in range(STEPS + 3):
                        if s % NBLK == S_Q and s // NBLK + 1 < NHG:
                            q_full(i, s // NBLK + 1)
                        if s % NBLK == S_K and s // NBLK + 1 < NHG:
                            k_even(i, s // NBLK + 1)
                        if s % NBLK == 2 and s >= 6:
                            o_his(i, (s - 6) // NBLK)
                        if s < STEPS:
                            exps(i, s)
                        if s == S_ROUTER[0] + 1:
                            act.wait_ge(router_chain, R_STEPS * i + 2)
                            act.activation(rp[:], rp[:], ACT.Exp).then_inc(router_exp, 1)
                    full(i, U_HT)
                    act.activation(hT_hi[:], ps[:, U_HT % 2, :], ACT.Copy).then_inc(mm_act, 1)
                    act.wait_ge(wo_done, NHG * i + NHG)
                    act.activation(a_hi[:], ps[:, WO, :], ACT.Identity, bias=bf[:, B_O:B_O + 1]).then_inc(a_hi_ready, 1)
                    if not last:
                        xT_hi_copy(i + 1)

                w_his(range(CONV_WCH))
                act.wait_ge(zeroed, 4)
                xT_hi_copy(0)
                w_his(range(CONV_WCH, N_WCH))
                act.wait_ge(const_in, 16 * N_CONST)
                act.wait_ge(brow_ready, 1)
                body(0, False)
                with act.Fori(1, NSEQ - 1) as i:
                    body(i, False)
                body(NSEQ - 1, True)

            @block.vector
            def _(dve):
                def norm_stats(i, t):
                    dve.wait_ge(x_in[t], 16 * i + 16)
                    dve.bn_stats(stats[:, t, :], xin[:, t, :]).then_inc(st_done, 1)

                def norm_var(i):
                    for t in range(NT):
                        dve.wait_ge(st_done, 2 * NT * i + NT)
                        carry(dve)
                        dve.bn_aggr(mv[:, t, :], stats[:, t, :]).then_inc(st_done, 1)
                    dve.wait_ge(st_done, 2 * NT * i + 2 * NT)
                    dve.tensor_scalar(veps[:], mv[:, :, 1], EPS, None, ALU.add).then_inc(ve_ready, 1)

                def norm(i, t):
                    if t == 0:
                        dve.wait_ge(rstd_ready, i + 1)
                    dve.tensor_scalar(xin[:, t, :], xin[:, t, :], mv[:, t, 0:1], rstd[:, t:t + 1], ALU.subtract, ALU.mult).then_inc(xn_ready, 1)

                def w_los(steps):
                    for j in steps:
                        dve.wait_ge(w_hi_ready, j + 1)
                        c = slice(j * WCH, (j + 1) * WCH)
                        dve.tensor_tensor(w_lo[:, c], stage[j % NST], w_hi[:, c].bitcast(F32), ALU.subtract).then_inc(w_lo_ready, 1)

                def xT_lo_copy(i):
                    for k in range(KD):
                        dve.wait_ge(xT_hi_ready, KD * i + k + 1)
                        dve.tensor_tensor(xT_lo[:, k, 1:L + 1], ps[:, XT_BANKS[k], :], xT_hi[:, k, 1:L + 1].bitcast(F32), ALU.subtract).then_inc(xT_lo_ready, 1)

                def full(i, u):
                    dve.wait_ge(mm_full, NU * i + u + 1)

                def acted(i, u):
                    dve.wait_ge(mm_act, ACT_USES * i + freed("A", u + 1))

                def k_odd(i, hg):
                    dve.wait_ge(sc_full, STEPS * i + max(0, NBLK * (hg - 1)))
                    for hp in range(2):
                        u = use_act(hg, 2 + hp)
                        full(i, u)
                        dve.tensor_scalar(kh[DH0:P, hg % 2, hp, 1, :], ps[DH0:P, u % 2, :],
                                          bf[DH0:P, B_K + 2 * hg + hp:B_K + 2 * hg + hp + 1], None, ALU.add).then_inc(mm_dve, 1)

                def v_full(i, hg):
                    dve.wait_ge(av_done, STEPS * i + max(0, NBLK * (hg - 1)))
                    for half in range(2):
                        u = use_act(hg, 4 + half)
                        full(i, u)
                        dve.tensor_copy(vh[:, hg % 2, 2 * half:2 * half + 2, :].rearrange("p b n -> p (b n)"), ps[:, u % 2, :]).then_inc(mm_dve, 1)

                def chain(i, n, ins):
                    ins.then_inc(router_chain, 1)
                    dve.wait_ge(router_chain, R_STEPS * i + n)

                def router_shift(i):
                    acted(i, U_AR + NT - 1)
                    chain(i, 1, dve.tensor_reduce(rmx[:], har[:, :, ER:ER + NE], AX_X, ALU.max))
                    chain(i, 2, dve.tensor_tensor(rp[:], har[:, :, ER:ER + NE], spread(rmx[:], NE), ALU.subtract))

                def router_probs(i):
                    dve.wait_ge(router_exp, i + 1)
                    chain(i, 3, dve.tensor_reduce(rs[:], rp[:], AX_X, ALU.add))
                    chain(i, 4, dve.reciprocal(rs[:], rs[:]))
                    chain(i, 5, dve.tensor_tensor(rp[:], rp[:], spread(rs[:], NE), ALU.mult))

                def router_top(i):
                    carry(dve)
                    for t in range(NT):
                        top_i = dve.max(top[:, t, :], rp[:, t, :])
                    chain(i, 6, top_i)
                    carry(dve)
                    for t in range(NT):
                        idx_i = dve.max_index(topi[:, t, :], top[:, t, :], rp[:, t, :])
                    chain(i, 7, idx_i)

                def router_share(i):
                    dve.tensor_tensor(rs[:], top[:, :, 0], top[:, :, 1], ALU.add)
                    chain(i, 8, dve.tensor_copy(topf[:], topi[:]))
                    chain(i, 9, dve.reciprocal(rs[:], rs[:]))
                    chain(i, 10, dve.tensor_tensor(wsel[:], top[:, :, 0:2], spread(rs[:], 2), ALU.mult))

                def router_combine(i):
                    iov = io8[:].rearrange("p (t e) -> p t e", t=NT)
                    for j in range(2):
                        e = dve.tensor_tensor(eq[:, j, :, :], iov, spread(topf[:, :, j], NE), ALU.is_equal)
                    chain(i, 11, e)
                    for j in range(2):
                        e = dve.tensor_tensor(eq[:, j, :, :], eq[:, j, :, :], spread(wsel[:, :, j], NE), ALU.mult)
                    chain(i, 12, e)
                    chain(i, R_STEPS, dve.tensor_tensor(comb[:], eq[:, 0, :, :], eq[:, 1, :, :], ALU.add))

                def router_weigh(i):
                    for t in range(NT):
                        hv = har[:, t, 0:ER].rearrange("p (e r) -> p e r", e=NE)
                        cv = spread(comb[:, t, :], RANK)
                        dve.scalar_tensor_tensor(hv, hv, LORA_SCALE, cv, ALU.mult, ALU.mult).then_inc(comb_ready, 1)

                ROUTER = (router_shift, router_probs, router_top, router_share, router_combine, router_weigh)

                def maxes(i, s):
                    dve.wait_ge(sc_full, STEPS * i + s + 1)
                    dve.tensor_reduce(mx[:, s % 3, :], ps[:, SC + s % 2, :].rearrange("p (h k) -> p h k", h=HG), AX_X, ALU.max).then_inc(mx_ready, 1)
                    dve.wait_ge(mx_ready, STEPS * i + s + 1)
                    dve.tensor_scalar(nmx[:, s % 3, :], mx[:, s % 3, :], -DH0 ** -0.5, None, ALU.mult).then_inc(nmx_ready, 1)

                def recips(i, s):
                    dve.wait_ge(exp_done, STEPS * i + s + 1)
                    dve.wait_ge(prob_ready, STEPS * i + max(0, s - 2))
                    dve.reciprocal(rsum[:, s % 3, :], sums[:, s % 3, :]).then_inc(rsum_ready, 1)

                def probT_copy(i, s):
                    dve.wait_ge(tr_full, STEPS * i + s + 1)
                    dve.wait_ge(av_done, STEPS * i + max(0, s - 1))
                    dve.tensor_copy(probT[:, s % 2, :], ps[:, PT, :]).then_inc(probT_ready, 1)

                def o_los(i, hg):
                    for hp in range(2):
                        dve.wait_ge(o_hi_ready, 2 * NHG * i + 2 * hg + hp + 1)
                        dve.scalar_tensor_tensor(o_lo[:, hp, :], ps[:, AV + hp, :], bf[:, B_V + 2 * hg + hp:B_V + 2 * hg + hp + 1],
                                                 o_hi[:, hp, :].bitcast(F32), ALU.add, ALU.subtract).then_inc(o_lo_ready, 1)

                def body(i, last):
                    for m in range(3):
                        acted(i, m)
                        dve.scalar_tensor_tensor(c_lo[:, m, :], ps[:, m % 2, :], bf[:, B_CONV + m:B_CONV + m + 1],
                                                 c_hi[:, m, :].bitcast(F32), ALU.add, ALU.subtract).then_inc(mm_dve, 1)
                    if isinstance(i, int) and i == 0:
                        dve.wait_ge(zeroed, 5)
                    k_odd(i, 0)
                    v_full(i, 0)
                    for s in range(STEPS + 3):
                        if s < STEPS:
                            maxes(i, s)
                        if s % NBLK == S_K and s // NBLK + 1 < NHG:
                            k_odd(i, s // NBLK + 1)
                        if 1 <= s <= STEPS:
                            recips(i, s - 1)
                        if 2 <= s < STEPS + 2:
                            probT_copy(i, s - 2)
                        if s % NBLK == S_V and s // NBLK + 1 < NHG:
                            v_full(i, s // NBLK + 1)
                        if s in S_ROUTER:
                            ROUTER[S_ROUTER.index(s)](i)
                        if s % NBLK == 2 and s >= 6:
                            o_los(i, (s - 6) // NBLK)
                        if s in S_STATS and not last:
                            norm_stats(i + 1, s - S_STATS[0])
                        if s == S_STATS[-1] and not last:
                            norm_var(i + 1)
                        if s in S_NORM and not last:
                            norm(i + 1, s - S_NORM[0])
                    acted(i, U_HT)
                    dve.tensor_tensor(hT_lo[:], ps[:, U_HT % 2, :], hT_hi[:].bitcast(F32), ALU.subtract).then_inc(mm_dve, 1)
                    dve.wait_ge(a_hi_ready, i + 1)
                    dve.scalar_tensor_tensor(a_lo[:], ps[:, WO, :], bf[:, B_O:B_O + 1], a_hi[:].bitcast(F32), ALU.add, ALU.subtract).then_inc(a_lo_ready, 1)
                    for t in range(NT):
                        if t == NT - 1 and not last:
                            xT_lo_copy(i + 1)
                        full(i, U_X1 + t)
                        dve.wait_ge(res_ready, NT * i + t + 1)
                        dve.tensor_tensor(xres[:, t % 2, :], ps[:, (U_X1 + t) % 2, :], xres[:, t % 2, :], ALU.add).then_inc(x1_ready, 1)

                for t in range(NT):
                    norm_stats(0, t)
                norm_var(0)
                w_los(range(2))
                for t in range(NT):
                    norm(0, t)
                w_los(range(2, CONV_WCH))
                dve.wait_ge(zeroed, 4)
                xT_lo_copy(0)
                w_los(range(CONV_WCH, N_WCH))
                dve.wait_ge(const_in, 16 * N_CONST)
                body(0, False)
                with dve.Fori(1, NSEQ - 1) as i:
                    body(i, False)
                body(NSEQ - 1, True)

            @block.tensor
            def _(pe):
                def take(i, u):
                    pe.wait_ge(mm_act, ACT_USES * i + (freed("A", u - 1) if u >= 2 else 0))
                    n = [e for k, (w, e) in enumerate(USES[:max(0, u - 1)]) if "D" in e and w != "x1"]
                    pe.wait_ge(mm_dve, (DVE_USES - NT) * i + len(n))
                    if u > 0 or not isinstance(i, int) or i > 0:
                        pe.wait_ge(x1_ready, NT * i + max(0, u - 1 - U_X1) - (u == 0))

                def transposes_in(i):
                    pe.wait_ge(xn_ready, NT * i + NT)
                    for k in range(KD):
                        for t in range(NT):
                            last = pe.transpose(ps[:, XT_BANKS[k], t * P:(t + 1) * P], xin[:, t, k * P:(k + 1) * P], idf[:])
                        last.then_inc(xt_done, 1)

                def mm_done(ins):
                    ins.then_inc(mm_full, 1)

                def project_qk(i, hg, n):
                    for hp in range(2):
                        u = use_act(hg, 2 * n + hp)
                        take(i, u)
                        mm_done(split3(pe, ps[:, u % 2, :], wt((C_WQ, C_WK)[n] + (2 * hg + hp) * P, P), (c_hi[:, n, :], c_lo[:, n, :]), True, True))

                def project_v(i, hg):
                    for half in range(2):
                        u = use_act(hg, 4 + half)
                        take(i, u)
                        for b in range(2):
                            tok = slice((2 * half + b) * P, (2 * half + b + 1) * P)
                            last = split3(pe, ps[:, u % 2, b * 256:(b + 1) * 256], (c_hi[:, 2, tok], c_lo[:, 2, tok]),
                                          wt(C_WV + hg * HG * DH0, HG * DH0), True, True)
                        mm_done(last)

                def scores(i, s):
                    hg, b = s // NBLK, s % NBLK
                    if b == 0:
                        pe.wait_ge(mm_act, ACT_USES * i + freed("A", use_act(hg, 3) + 1))
                        pe.wait_ge(mm_dve, (DVE_USES - NT) * i + freed("D", use_act(hg, 3) + 1))
                    pe.wait_ge(exp_done, STEPS * i + max(0, s - 1))
                    bank = ps[:, SC + s % 2, :]
                    pe.matmul(bank, idb[:], neg[:], start=True, stop=False, skip_group_check=True)
                    for hp in range(2):
                        last = pe.matmul(bank[:, hp * 256:(hp + 1) * 256], qh[:, hg % 2, hp, b * P:(b + 1) * P],
                                         kh[:, hg % 2, hp, :, b * P:(b + 1) * P], start=False, stop=(hp == 1), skip_group_check=True)
                    last.then_inc(sc_full, 1)

                def transposes(i, s):
                    pe.wait_ge(prob_ready, STEPS * i + s + 1)
                    pe.wait_ge(probT_ready, STEPS * i + s)
                    for h in range(HG):
                        last = pe.transpose(ps[:, PT, h * P:(h + 1) * P], prob[:, s % 3, h * P:(h + 1) * P], idf[:])
                    last.then_inc(tr_full, 1)

                def weighted(i, s):
                    hg, b = s // NBLK, s % NBLK
                    pe.wait_ge(probT_ready, STEPS * i + s + 1)
                    if b == 0:
                        pe.wait_ge(mm_dve, (DVE_USES - NT) * i + freed("D", use_act(hg, 5) + 1))
                        pe.wait_ge(o_lo_ready, 2 * NHG * i + 2 * hg)
                    for h in range(HG):
                        r = DH0 * (h % 2)
                        last = pe.matmul(ps[r:r + DH0, AV + h // 2, b * P:(b + 1) * P], vh[:, hg % 2, b, h * DH0:(h + 1) * DH0],
                                         probT[:, s % 2, h * P:(h + 1) * P], start=True, stop=True, skip_group_check=True)
                    last.then_inc(av_done, 1)

                def out_proj(i, hg):
                    pe.wait_ge(o_lo_ready, 2 * NHG * i + 2 * hg + 2)
                    if hg == 0:
                        pe.wait_ge(a_lo_ready, i)
                    for hp in range(2):
                        last = split3(pe, ps[:, WO, :], wt(C_WO + (2 * hg + hp) * W, W), (o_hi[:, hp, :], o_lo[:, hp, :]),
                                      hg == 0 and hp == 0, hg == NHG - 1 and hp == 1)
                    last.then_inc(wo_done, 1)

                def body(i, last_seq):
                    for m in range(3):
                        take(i, m)
                        for j in range(TAPS):
                            for k in range(KD):
                                if m + j == 0:
                                    pe.wait_ge(xT_lo_ready, KD * i + k + 1)
                                if m == 0 and isinstance(i, int) and i == 0:
                                    pe.wait_ge(w_lo_ready, -(-(C_CONV + (j * KD + k + 1) * 3 * W) // WCH))
                                last = split3(pe, ps[:, m % 2, :], wt(C_CONV + (j * KD + k) * 3 * W + m * P, P),
                                              (xT_hi[:, k, j:j + L], xT_lo[:, k, j:j + L]), j + k == 0, j == TAPS - 1 and k == KD - 1)
                        mm_done(last)
                    if isinstance(i, int) and i == 0:
                        pe.wait_ge(w_lo_ready, N_WCH)
                    for t in range(NT):
                        u = U_AR + t
                        take(i, u)
                        for k in range(KD):
                            tok = slice(1 + t * P, 1 + (t + 1) * P)
                            last = split3(pe, ps[:, u % 2, 0:AR], (xT_hi[:, k, tok], xT_lo[:, k, tok]), wt(C_AR + k * AR, AR), k == 0, k == KD - 1)
                        mm_done(last)
                    project_qk(i, 0, 0)
                    project_qk(i, 0, 1)
                    project_v(i, 0)
                    for s in range(STEPS + 3):
                        if s < STEPS:
                            scores(i, s)
                        for n, at in ((0, S_Q), (1, S_K)):
                            if s % NBLK == at and s // NBLK + 1 < NHG:
                                project_qk(i, s // NBLK + 1, n)
                        if s % NBLK == S_V and s // NBLK + 1 < NHG:
                            project_v(i, s // NBLK + 1)
                        if 2 <= s < STEPS + 2:
                            transposes(i, s - 2)
                        if s % NBLK == 3 and s >= 7:
                            out_proj(i, (s - 7) // NBLK)
                        if 3 <= s:
                            weighted(i, s - 3)
                    take(i, U_HT)
                    pe.wait_ge(comb_ready, NT * i + NT)
                    for t in range(NT):
                        last = pe.transpose(ps[:, U_HT % 2, t * P:(t + 1) * P], har[:, t, 0:ER], idf[:])
                    mm_done(last)
                    for t in range(NT):
                        u = U_X1 + t
                        if t == NT - 1 and not last_seq:
                            transposes_in(i + 1)
                        take(i, u)
                        tok = slice(1 + t * P, 1 + (t + 1) * P)
                        ts = slice(t * P, (t + 1) * P)
                        for k in range(KD):
                            split3(pe, ps[:, u % 2, :], (xT_hi[:, k, tok], xT_lo[:, k, tok]), wt(C_BASE + k * D, D), k == 0, False)
                        if t == 0:
                            out_proj(i, NHG - 1)
                            pe.wait_ge(mm_dve, (DVE_USES - NT) * i + freed("D", U_HT + 1))
                        split3(pe, ps[:, u % 2, :], (hT_hi[:, ts], hT_lo[:, ts]), wt(C_B, D), False, False)
                        if t == 0:
                            pe.wait_ge(a_lo_ready, i + 1)
                        mm_done(split3(pe, ps[:, u % 2, :], (a_hi[:, ts], a_lo[:, ts]), wt(C_PROJ, D), False, True))

                pe.wait_ge(ident_in, 16)
                pe.wait_ge(zeroed, 4)
                transposes_in(0)
                pe.wait_ge(const_in, 16 * N_CONST)
                body(0, False)
                with pe.Fori(1, NSEQ - 1) as i:
                    body(i, False)
                body(NSEQ - 1, True)


N_B = KD * 3 * D
WCH1 = 1024
N_WCH1 = N_B // WCH1
WCH1_Q = KD * D // WCH1
WCH1_LATE = (range(WCH1_Q, 2 * WCH1_Q), range(2 * WCH1_Q, N_WCH1), (), ())
NQS = 4
QPARTS = (0, 0, 0, 1, 1, 2)
KPARTS = (0, 1, 2, 0, 1, 0)
KS = len(QPARTS) * DH1
HPT = P // DH1
TPG = 4
NG = P // TPG
NCH = NT
HB = NG // 2
OB = 4
OA = NG // OB


def attention1(nc, x1_dram, w1, bias_f, bv1, ident, q3, k3, xT_dram, ctx_dram):
    with ExitStack() as ctx:
        def sb(name, shape, dt=F32):
            return ctx.enter_context(nc.sbuf_tensor(name, shape, dt))

        def sem(name):
            return ctx.enter_context(nc.semaphore(name))

        w_hi = sb("w1_hi", [P, N_B], F32R)
        w_lo = sb("w1_lo", [P, N_B], F32R)
        xin = sb("xin1", [P, NT, D])
        xT_hi = sb("xT1_hi", [P, KD, L], F32R)
        xT_lo = sb("xT1_lo", [P, KD, L], F32R)
        rf = sb("rf", [P, 2, L])
        yf = sb("yf", [P, D])
        vT = sb("vT", [P, NCH, D])
        qk3 = sb("qk3", [P, NQS, 3, L], BF16)
        vp3 = sb("vp3", [P, NG, 3, DH1], BF16)
        qb = sb("qb", [KS, 2, H1, P], BF16)
        kb = sb("kb", [KS, 2, H1, P], BF16)
        vb = sb("vb", [P, 2, NG, 2, TPG, 2, DH1], BF16)
        S = sb("S", [P, 2, NG, H1])
        T = sb("T", [P, NG * H1])
        pp = sb("pp", [P, 2, 3, NG * H1], BF16)
        osb = sb("osb", [P, OA, OB, H1])
        cx = sb("cx", [P, 2, NG, DH1])
        bf = sb("bf1", [P, N_BF])
        bvb = sb("bvb", [P, D])
        idf = sb("idf1", [P, P])
        mx = sb("mx1", [P, NG])
        sm = sb("sm1", [P, NG])
        rs = sb("rs1", [P, NG])
        stats = sb("stats1", [P, NT, 6])
        mv = sb("mv1", [P, NT, 2])
        veps = sb("veps1", [P, NT])
        rstd = sb("rstd1", [P, NT])
        mhalf = sb("mhalf1", [P, NT])
        stage = [S[:, 0, :, :].rearrange("p g t -> p (g t)"), S[:, 1, :, :].rearrange("p g t -> p (g t)"), T[:],
                 osb[:].rearrange("p a b h -> p (a b h)"), cx[:].rearrange("p s n d -> p (s n d)")]
        NST1 = len(stage)
        ps = ctx.enter_context(nc.psum_tensor("ps1", [P, 8, 512], F32))
        MM, SC, OUT, TR = 0, 2, 4, 6
        XT = (MM, MM + 1, TR, TR + 1)

        const_in, ident_in, carrier = sem("const1_in"), sem("ident1_in"), sem("carrier1")
        w_in = [sem(f"w1_in{s}") for s in range(NST1)]
        x_in = sem("x1_in")
        qk_out = [sem(f"qk_out{s}") for s in range(NQS)]
        xT_out = sem("xT_out")
        qk_in = [sem(f"qk_in{s}") for s in range(2)]
        cx_out = [sem(f"cx_out{s}") for s in range(2)]
        names = ("w_hi_ready1 w_lo_ready1 zeroed1 mhalf_set1 st_done1 ve_ready1 rstd_ready1 xn_ready1 xt_done1 xT_hi_ready1 "
                 "xT_lo_ready1 mm_full1 hi_ready r_ready mid_ready lo_ready y_ready sc_full1 mx_ready1 sub_ready exp_ready "
                 "vT_ready vh_ready vr_ready vm_ready vl_ready v_hm_placed v_l_placed sum_ready rs_ready p_ready T_ready ph_ready T_rest pm_ready pl_ready av_done1 o_ready otr_full cx_ready")
        s_ = {n: sem(n) for n in names.split()}

        def carry(eng):
            eng.sem_inc(carrier, 1)

        NU, NQK = 12, 8

        def token(g, q):
            return NG * q + g

        def chunk(i, c, lag):
            return (i - 1, c - lag) if c >= lag else (i - 2, c - lag + NCH)

        def has(i, c, lag, att, carried):
            return att if c >= lag else carried

        def upto(n):
            return max(0, n) if isinstance(n, int) else n

        with nc.Block() as block:

            @block.sync
            def _(sp):
                sp.dma_start(xin[:], x1_dram[0:L, :].rearrange("(t p) d -> p t d", p=P)).then_inc(x_in, 16)
                sp.dma_start(idf[:], ident).then_inc(ident_in, 16)
                for j in range(N_WCH1):
                    s = j % NST1
                    if j >= NST1:
                        sp.wait_ge(s_["w_hi_ready1"], j - NST1 + 1)
                        sp.wait_ge(s_["w_lo_ready1"], j - NST1 + 1)
                    sp.dma_start(stage[s], w1[:, j * WCH1:(j + 1) * WCH1]).then_inc(w_in[s], 16)
                    if j == 1:
                        sp.dma_start(bf[:], bias_f).then_inc(const_in, 16)
                        sp.dma_start(bvb[:], bass.AP(bv1.tensor, 0, [[0, P], [1, D]])).then_inc(const_in, 16)

                def load_parts(a, c, dst, src, parts):
                    for j, part in enumerate(parts):
                        view = src[bass.ds(a, 1), :, part, c, :, :].rearrange("o u (d h) t -> d (o u) (h t)", d=DH1)
                        own = dst[DH1 * j:DH1 * (j + 1), c % 2, :, :].rearrange("d (u h) t -> d u (h t)", h=HPT)
                        sp.dma_start(own, view).then_inc(qk_in[c % 2], 16)

                def load_q(a, c):
                    if c == 0:
                        for o in range(NQS):
                            sp.wait_ge(qk_out[o], 16 * NQK // NQS * (a + 1))
                            carry(sp)
                    sp.wait_ge(s_["sc_full1"], upto(NCH * a + c - 1))
                    load_parts(a, c, qb, q3, QPARTS)

                def load_k(a, c):
                    load_parts(a, c, kb, k3, KPARTS)

                def store_ctx(a, c):
                    sp.wait_ge(s_["cx_ready"], 2 * NCH * a + 2 * c + 2)
                    for b in range(OB):
                        view = ctx_dram[bass.ds(a, 1), c * P + b * NG:c * P + (b + 1) * NG, :].rearrange("o t (h d) -> h (o t) d", d=DH1)
                        sp.dma_start(view, cx[32 * b:32 * b + 32, c % 2, :, :]).then_inc(cx_out[c % 2], 16)

                def store_qk(i, u):
                    sp.wait_ge(s_["lo_ready"], NQK * i + u + 1)
                    dst = q3 if u < 4 else k3
                    view = dst[bass.ds(i, 1), u % 4, :, :, :, :].rearrange("o w c p t -> p (o w c) t")
                    sp.dma_start(view, qk3[:, u % NQS, :, :].rearrange("p w (c t) -> p (w c) t", c=NCH)).then_inc(qk_out[u % NQS], 16)

                def steps(i, c, qkv, att, carried):
                    units = range(3 * c, min(3 * c + 3, NQK)) if qkv else ()
                    ahead = [(i - 1, c + 1)] if att and c < NCH - 1 else [(i, 0)] if qkv and c == NCH - 1 else []
                    for n in ahead:
                        load_q(*n)
                        if c == 0:
                            load_k(*n)
                    for u in units[:1]:
                        store_qk(i, u)
                    for n in ahead if c > 0 else ():
                        load_k(*n)
                    if has(i, c, 3, att, carried):
                        store_ctx(*chunk(i, c, 3))
                    for u in units[1:2]:
                        store_qk(i, u)
                    if qkv and c < 2:
                        sp.wait_ge(s_["xT_lo_ready1"], KD * i + KD)
                        view = xT_dram[bass.ds(i, 1), c, :, :].rearrange("o p n -> (o p) n")
                        sp.dma_start(view, (xT_hi, xT_lo)[c][:].rearrange("p k t -> p (k t)").bitcast(F32)).then_inc(xT_out, 16)
                    for u in units[2:]:
                        store_qk(i, u)
                    if isinstance(i, int) and i == 0 and c == 1:
                        load_x(1)

                def load_x(i):
                    sp.wait_ge(s_["xt_done1"], KD * i)
                    sp.dma_start(xin[:], x1_dram[bass.ds(i * L, L), :].rearrange("(t p) d -> p t d", p=P)).then_inc(x_in, 16)

                def body(i, before, qkv, att, carried):
                    if qkv and not (isinstance(i, int) and i == 1):
                        load_x(i)
                    steps(i - 1, NCH - 1, *before, False)
                    first_steps(i, qkv, att, carried)

                def first_steps(i, qkv, att, carried):
                    for c in range(NCH - 1):
                        steps(i, c, qkv, att, carried)

                first_steps(0, True, False, False)
                body(1, (True, False), True, True, False)
                with sp.Fori(2, NSEQ) as i:
                    body(i, (True, True), True, True, True)
                body(NSEQ, (True, True), False, True, True)
                body(NSEQ + 1, (False, True), False, False, True)
                sp.wait_ge(xT_out, 32 * NSEQ)
                for s in range(2):
                    sp.wait_ge(cx_out[s], 1 + 16 * OB * NCH // 2 * NSEQ)

            @block.gpsimd
            def _(pool):
                pool.memset(mhalf[:], -0.5).then_inc(s_["mhalf_set1"], 1)
                for s in range(2):
                    pool.sem_inc(cx_out[s], 1)
                pool.wait_ge(s_["mhalf_set1"], 1)

                def normalise(a, c):
                    pool.wait_ge(s_["rs_ready"], NCH * a + c + 1)
                    v = S[:, c % 2, :, :]
                    pool.tensor_tensor(v, v, spread(rs[:], H1), ALU.mult).then_inc(s_["p_ready"], 1)

                def last_part(a, c):
                    pool.wait_ge(s_["pm_ready"], NCH * a + c + 1)
                    pool.tensor_tensor(pp[:, c % 2, 2, :], T[:], pp[:, c % 2, 1, :], ALU.subtract).then_inc(s_["pl_ready"], 1)

                def last_qk(i, u):
                    pool.wait_ge(s_["mid_ready"], NQK * i + u + 1)
                    pool.tensor_tensor(qk3[:, u % NQS, 2, :], rf[:, u % 2, :], qk3[:, u % NQS, 1, :], ALU.subtract).then_inc(s_["lo_ready"], 1)

                def v_view(c):
                    return vT[:, c, :].rearrange("p (d g) -> p g d", g=NG)

                def v_rest(a, c):
                    pool.wait_ge(s_["vh_ready"], NCH * a + c + 1)
                    pool.tensor_tensor(v_view(c), v_view(c), vp3[:, :, 0, :], ALU.subtract).then_inc(s_["vr_ready"], 1)

                def v_last(a, c):
                    pool.wait_ge(s_["vm_ready"], NCH * a + c + 1)
                    pool.wait_ge(s_["v_l_placed"], NCH * a + c)
                    pool.tensor_tensor(vp3[:, :, 2, :], v_view(c), vp3[:, :, 1, :], ALU.subtract).then_inc(s_["vl_ready"], 1)

                def rstds(i):
                    pool.wait_ge(s_["ve_ready1"], i + 1)
                    pool.tensor_tensor(rstd[:], veps[:], mhalf[:], ALU.pow).then_inc(s_["rstd_ready1"], 1)

                def steps(i, c, qkv, att, carried, ahead=None):
                    qk_units = range(3 * c, min(3 * c + 3, NQK)) if qkv else ()
                    if att:
                        v_rest(i - 1, c)
                    for u in qk_units[:1]:
                        last_qk(i, u)
                    if att:
                        v_last(i - 1, c)
                    for u in qk_units[1:2]:
                        last_qk(i, u)
                    if has(i, c, 1, att, carried):
                        last_part(*chunk(i, c, 1))
                    if att:
                        normalise(i - 1, c)
                    for u in qk_units[2:]:
                        last_qk(i, u)
                    if ahead is not None:
                        rstds(ahead)

                def first_steps(i, qkv, att, carried):
                    for c in range(NCH - 1):
                        steps(i, c, qkv, att, carried)

                def body(i, before, qkv, att, carried):
                    steps(i - 1, NCH - 1, *before, False, i if qkv else None)
                    first_steps(i, qkv, att, carried)

                rstds(0)
                pool.memset(vb[:].rearrange("p s g n q w d -> p (s g n q w d)").bitcast(U32), 0).then_inc(s_["zeroed1"], 1)
                first_steps(0, True, False, False)
                body(1, (True, False), True, True, False)
                with pool.Fori(2, NSEQ) as i:
                    body(i, (True, True), True, True, True)
                body(NSEQ, (True, True), False, True, True)
                body(NSEQ + 1, (False, True), False, False, True)

            @block.scalar
            def _(act):
                def w_his(steps):
                    for j in steps:
                        act.wait_ge(w_in[j % NST1], 16 * (j // NST1) + 16)
                        act.activation(w_hi[:, j * WCH1:(j + 1) * WCH1], stage[j % NST1], ACT.Copy).then_inc(s_["w_hi_ready1"], 1)

                def first_part(i, u):
                    s = u % 2
                    act.wait_ge(s_["mm_full1"], NU * i + u + 1)
                    act.wait_ge(qk_out[u % NQS], 16 * (NQK // NQS) * i + 16 * (u // NQS))
                    act.activation(qk3[:, u % NQS, 0, :], ps[:, MM + s, :], ACT.Identity, bias=bf[:, B_Q1 + u:B_Q1 + u + 1]).then_inc(s_["hi_ready"], 1)

                def mid_part(i, u):
                    s = u % 2
                    act.wait_ge(s_["r_ready"], NQK * i + u + 1)
                    act.activation(qk3[:, u % NQS, 1, :], rf[:, s, :], ACT.Copy).then_inc(s_["mid_ready"], 1)

                def v_view(c):
                    return vT[:, c, :].rearrange("p (d g) -> p g d", g=NG)

                def v_first(a, c):
                    act.wait_ge(s_["vT_ready"], NCH * a + c + 1)
                    act.wait_ge(s_["v_hm_placed"], NCH * a + c)
                    act.activation(vp3[:, :, 0, :], v_view(c), ACT.Copy).then_inc(s_["vh_ready"], 1)

                def v_mid(a, c):
                    act.wait_ge(s_["vr_ready"], NCH * a + c + 1)
                    act.activation(vp3[:, :, 1, :], v_view(c), ACT.Copy).then_inc(s_["vm_ready"], 1)

                def place_l(a, c):
                    act.wait_ge(s_["vl_ready"], NCH * a + c + 1)
                    act.wait_ge(s_["av_done1"], upto(NCH * a + c - 1))
                    for q in range(TPG):
                        o = slice(32 * q, 32 * q + 32)
                        last = act.activation(vb[o, c % 2, :, 1, q, 0, :], vp3[o, :, 2, :], ACT.Copy)
                    last.then_inc(s_["v_l_placed"], 1)

                def exps(a, c):
                    act.wait_ge(s_["sub_ready"], 2 * NCH * a + 2 * c + 2)
                    v = S[:, c % 2, :, :].rearrange("p g t -> p (g t)")
                    act.activation(v, v, ACT.Exp, scale=DH1 ** -0.5).then_inc(s_["exp_ready"], 1)

                def prob_hi(a, c):
                    act.wait_ge(s_["T_ready"], NCH * a + c + 1)
                    act.wait_ge(s_["av_done1"], upto(NCH * a + c - 1))
                    act.activation(pp[:, c % 2, 0, :], T[:], ACT.Copy).then_inc(s_["ph_ready"], 1)

                def prob_mid(a, c):
                    act.wait_ge(s_["T_rest"], NCH * a + c + 1)
                    act.activation(pp[:, c % 2, 1, :], T[:], ACT.Copy).then_inc(s_["pm_ready"], 1)

                def o_copy(a, c):
                    act.wait_ge(s_["av_done1"], NCH * a + c + 1)
                    act.wait_ge(s_["otr_full"], NCH * a + c)
                    for hf in range(2):
                        act.activation(osb[:, :, 2 * hf:2 * hf + 2, :].rearrange("p a b h -> p b a h"),
                                       ps[:, OUT + hf, :].rearrange("p (b a h) -> p b a h", b=2, h=H1), ACT.Copy).then_inc(s_["o_ready"], 1)

                def body(i, qkv, att, carried):
                    if isinstance(i, int) and i == 0:
                        w_his(range(WCH1_Q))
                    if has(i, 0, 2, att, carried):
                        o_copy(*chunk(i, 0, 2))
                    if qkv:
                        act.wait_ge(xT_out, 32 * i)
                        act.wait_ge(s_["mm_full1"], NU * i)
                        for k in range(KD):
                            act.wait_ge(s_["xt_done1"], KD * i + k + 1)
                            act.activation(xT_hi[:, k, :], ps[:, XT[k], :], ACT.Copy).then_inc(s_["xT_hi_ready1"], 1)
                    if has(i, 0, 1, att, carried):
                        prob_hi(*chunk(i, 0, 1))
                    if isinstance(i, int) and i == 0:
                        act.wait_ge(const_in, 32)
                    if isinstance(i, int) and i == 1:
                        act.wait_ge(s_["zeroed1"], 1)
                    for c in range(NCH):
                        qk_units = range(3 * c, min(3 * c + 3, NQK)) if qkv else ()
                        if att:
                            v_first(i - 1, c)
                        for u in qk_units[:1]:
                            first_part(i, u)
                            mid_part(i, u)
                        if isinstance(i, int) and i == 0:
                            w_his(WCH1_LATE[c])
                        if c > 0 and has(i, c, 1, att, carried):
                            prob_hi(*chunk(i, c, 1))
                        if att:
                            v_mid(i - 1, c)
                        for u in qk_units[1:2]:
                            first_part(i, u)
                        if att:
                            exps(i - 1, c)
                        for u in qk_units[1:2]:
                            mid_part(i, u)
                        if has(i, c, 1, att, carried):
                            prob_mid(*chunk(i, c, 1))
                        if c > 0 and has(i, c, 2, att, carried):
                            o_copy(*chunk(i, c, 2))
                        for u in qk_units[2:]:
                            first_part(i, u)
                            mid_part(i, u)
                        if att:
                            place_l(i - 1, c)

                body(0, True, False, False)
                body(1, True, True, False)
                with act.Fori(2, NSEQ) as i:
                    body(i, True, True, True)
                body(NSEQ, False, True, True)
                body(NSEQ + 1, False, False, True)

            @block.vector
            def _(dve):
                def w_los(steps):
                    for j in steps:
                        dve.wait_ge(s_["w_hi_ready1"], j + 1)
                        c = slice(j * WCH1, (j + 1) * WCH1)
                        dve.tensor_tensor(w_lo[:, c], stage[j % NST1], w_hi[:, c].bitcast(F32), ALU.subtract).then_inc(s_["w_lo_ready1"], 1)

                def norm_stats(i):
                    dve.wait_ge(x_in, 16 * i + 16)
                    for t in range(NT):
                        dve.bn_stats(stats[:, t, :], xin[:, t, :]).then_inc(s_["st_done1"], 1)
                    for t in range(NT):
                        dve.wait_ge(s_["st_done1"], 2 * NT * i + NT)
                        carry(dve)
                        dve.bn_aggr(mv[:, t, :], stats[:, t, :]).then_inc(s_["st_done1"], 1)
                    dve.wait_ge(s_["st_done1"], 2 * NT * i + 2 * NT)
                    dve.tensor_scalar(veps[:], mv[:, :, 1], EPS, None, ALU.add).then_inc(s_["ve_ready1"], 1)

                def normalised(i):
                    dve.wait_ge(s_["rstd_ready1"], i + 1)
                    for t in range(NT):
                        dve.tensor_scalar(xin[:, t, :], xin[:, t, :], mv[:, t, 0:1], rstd[:, t:t + 1], ALU.subtract, ALU.mult).then_inc(s_["xn_ready1"], 1)

                def xT_los(i):
                    for k in range(KD):
                        dve.wait_ge(s_["xT_hi_ready1"], KD * i + k + 1)
                        dve.tensor_tensor(xT_lo[:, k, :], ps[:, XT[k], :], xT_hi[:, k, :].bitcast(F32), ALU.subtract).then_inc(s_["xT_lo_ready1"], 1)

                def rest(i, u):
                    s = u % 2
                    if u < NQK:
                        dve.wait_ge(s_["lo_ready"], NQK * i + max(0, u - 1))
                        dve.wait_ge(s_["hi_ready"], NQK * i + u + 1)
                        dve.scalar_tensor_tensor(rf[:, s, :], ps[:, MM + s, :], bf[:, B_Q1 + u:B_Q1 + u + 1], qk3[:, u % NQS, 0, :], ALU.add, ALU.subtract).then_inc(s_["r_ready"], 1)
                        return
                    n = u - NQK
                    dve.wait_ge(s_["mm_full1"], NU * i + u + 1)
                    dve.wait_ge(s_["vT_ready"], NCH * i + n)
                    dve.tensor_tensor(yf[:], ps[:, MM + s, :], bvb[:], ALU.add).then_inc(s_["y_ready"], 1)
                    dve.wait_ge(s_["y_ready"], NCH * i + n + 1)
                    dve.wait_ge(s_["vl_ready"], upto(NCH * (i - 1) + n + 1))
                    dve.transpose(vT[:, n, :], yf[:]).then_inc(s_["vT_ready"], 1)

                def place_hm(a, c):
                    dve.wait_ge(s_["vm_ready"], NCH * a + c + 1)
                    dve.wait_ge(s_["av_done1"], upto(NCH * a + c - 1))
                    for q in range(TPG):
                        o = slice(32 * q, 32 * q + 32)
                        last = dve.tensor_copy(vb[o, c % 2, :, 0, q, :, :], vp3[o, :, 0:2, :])
                    last.then_inc(s_["v_hm_placed"], 1)

                def max_sub(a, c):
                    dve.wait_ge(s_["sc_full1"], NCH * a + c + 1)
                    for hf in range(2):
                        g = slice(hf * HB, (hf + 1) * HB)
                        v = ps[:, SC + hf, :].rearrange("p (g t) -> p g t", t=H1)
                        dve.tensor_reduce(mx[:, g], v, AX_X, ALU.max).then_inc(s_["mx_ready1"], 1)
                    for hf in range(2):
                        g = slice(hf * HB, (hf + 1) * HB)
                        v = ps[:, SC + hf, :].rearrange("p (g t) -> p g t", t=H1)
                        dve.wait_ge(s_["mx_ready1"], 2 * NCH * a + 2 * c + 2)
                        dve.tensor_tensor(S[:, c % 2, g, :], v, spread(mx[:, g], H1), ALU.subtract).then_inc(s_["sub_ready"], 1)

                def sums(a, c):
                    dve.wait_ge(s_["exp_ready"], NCH * a + c + 1)
                    dve.tensor_reduce(sm[:], S[:, c % 2, :, :], AX_X, ALU.add).then_inc(s_["sum_ready"], 1)
                    dve.wait_ge(s_["sum_ready"], NCH * a + c + 1)
                    dve.wait_ge(s_["p_ready"], NCH * a + c)
                    dve.reciprocal(rs[:], sm[:]).then_inc(s_["rs_ready"], 1)

                def turn(a, c):
                    dve.wait_ge(s_["p_ready"], NCH * a + c + 1)
                    dve.wait_ge(s_["pl_ready"], NCH * a + c)
                    dve.transpose(T[:], S[:, c % 2, :, :].rearrange("p g t -> p (g t)")).then_inc(s_["T_ready"], 1)

                def prob_rest(a, c):
                    dve.wait_ge(s_["ph_ready"], NCH * a + c + 1)
                    dve.tensor_tensor(T[:], T[:], pp[:, c % 2, 0, :], ALU.subtract).then_inc(s_["T_rest"], 1)

                def fold(a, c):
                    dve.wait_ge(s_["otr_full"], NCH * a + c + 1)
                    dve.wait_ge(cx_out[c % 2], 1 + 16 * OB * (2 * a + c // 2))
                    for hf in range(2):
                        v = ps[:, TR + hf, :].rearrange("p (n w d) -> p n d w", w=2, d=DH1)
                        dve.tensor_reduce(cx[:, c % 2, hf * HB:(hf + 1) * HB, :], v, AX_X, ALU.add).then_inc(s_["cx_ready"], 1)

                def steps(i, c, qkv, att, carried, ahead=None):
                    u = 3 * c
                    if qkv:
                        rest(i, u)
                    if isinstance(i, int) and i == 0:
                        w_los(WCH1_LATE[c])
                    if isinstance(i, int) and i == 1 and c == 0:
                        max_sub(0, 0)
                    if c > 0 and has(i, c, 1, att, carried):
                        turn(*chunk(i, c, 1))
                    if att and c > 0:
                        max_sub(i - 1, c)
                    if has(i, c, 1, att, carried):
                        prob_rest(*chunk(i, c, 1))
                    if qkv:
                        rest(i, u + 1)
                    if att:
                        sums(i - 1, c)
                        place_hm(i - 1, c)
                    if ahead is not None:
                        norm_stats(ahead)
                    if qkv:
                        rest(i, u + 2)
                    if has(i, c, 2, att, carried):
                        fold(*chunk(i, c, 2))
                    if ahead is not None:
                        normalised(ahead)

                def first_steps(i, qkv, att, carried):
                    if att and not (isinstance(i, int) and i == 1):
                        max_sub(i - 1, 0)
                    if isinstance(i, int) and i == 0:
                        w_los(range(WCH1_Q))
                    if qkv:
                        xT_los(i)
                    if has(i, 0, 1, att, carried):
                        turn(*chunk(i, 0, 1))
                    if isinstance(i, int) and i == 0:
                        dve.wait_ge(const_in, 32)
                    if isinstance(i, int) and i == 1:
                        dve.wait_ge(s_["zeroed1"], 1)
                    for c in range(NCH - 1):
                        steps(i, c, qkv, att, carried)

                def body(i, before, qkv, att, carried):
                    steps(i - 1, NCH - 1, *before, False, i if qkv else None)
                    first_steps(i, qkv, att, carried)

                norm_stats(0)
                normalised(0)
                first_steps(0, True, False, False)
                body(1, (True, False), True, True, False)
                with dve.Fori(2, NSEQ) as i:
                    body(i, (True, True), True, True, True)
                body(NSEQ, (True, True), False, True, True)
                body(NSEQ + 1, (False, True), False, False, True)

            @block.tensor
            def _(pe):
                def transposes_in(i):
                    pe.wait_ge(s_["xn_ready1"], NT * i + NT)
                    for k in range(KD):
                        if k < 2:
                            pe.wait_ge(s_["y_ready"], 4 * i)
                        else:
                            pe.wait_ge(s_["cx_ready"], upto(2 * NCH * (i - 1) - 4))
                        for t in range(NT):
                            last = pe.transpose(ps[:, XT[k], t * P:(t + 1) * P], xin[:, t, k * P:(k + 1) * P], idf[:])
                        last.then_inc(s_["xt_done1"], 1)

                def project(i, u):
                    if 2 <= u < 10:
                        pe.wait_ge(s_["r_ready"], NQK * i + u - 1)
                    elif u >= 10:
                        pe.wait_ge(s_["y_ready"], 4 * i + u - 9)
                    if isinstance(i, int) and i == 0 and u % 4 == 0:
                        pe.wait_ge(s_["w_lo_ready1"], WCH1_Q * (u // 4 + 1))
                    for k in range(KD):
                        if u == 0:
                            pe.wait_ge(s_["xT_lo_ready1"], KD * i + k + 1)
                        if u < 8:
                            c = (u // 4 * KD + k) * D + u % 4 * P
                            last = split3(pe, ps[:, MM + u % 2, :], (w_hi[:, c:c + P], w_lo[:, c:c + P]), (xT_hi[:, k, :], xT_lo[:, k, :]), k == 0, k == KD - 1)
                        else:
                            c = (2 * KD + k) * D
                            t = slice((u - 8) * P, (u - 7) * P)
                            last = split3(pe, ps[:, MM + u % 2, :], (xT_hi[:, k, t], xT_lo[:, k, t]), (w_hi[:, c:c + D], w_lo[:, c:c + D]), k == 0, k == KD - 1)
                    last.then_inc(s_["mm_full1"], 1)

                def scores(a, c):
                    s = c % 2
                    pe.wait_ge(qk_in[s], 16 * 12 * (2 * a + c // 2 + 1))
                    pe.wait_ge(s_["sub_ready"], 2 * NCH * a + 2 * c)
                    for g in range(NG):
                        for q in range(TPG):
                            t = token(g, q)
                            col = (g % HB) * H1
                            last = pe.matmul(ps[32 * q:32 * q + 32, SC + g // HB, col:col + H1], qb[:, s, :, t], kb[:, s, :, t],
                                             start=True, stop=True, skip_group_check=True)
                    last.then_inc(s_["sc_full1"], 1)

                def weighted(a, c):
                    s = c % 2
                    pe.wait_ge(s_["pl_ready"], NCH * a + c + 1)
                    pe.wait_ge(s_["v_hm_placed"], NCH * a + c + 1)
                    pe.wait_ge(s_["v_l_placed"], NCH * a + c + 1)
                    pe.wait_ge(s_["o_ready"], 2 * NCH * a + 2 * c)
                    for g in range(NG):
                        out = ps[:, OUT + g // HB, (g % HB) * H1:(g % HB + 1) * H1]
                        p3 = [pp[:, s, w, g * H1:(g + 1) * H1] for w in range(3)]
                        v_hm, v_l0 = (vb[:, s, g, n, :, :, :].rearrange("p q w d -> p (q w d)") for n in range(2))
                        for w in range(3):
                            pe.matmul(out, v_hm, p3[w], start=(w == 0), stop=False, skip_group_check=True)
                        last = pe.matmul(out, v_l0, p3[0], start=False, stop=True, skip_group_check=True)
                    last.then_inc(s_["av_done1"], 1)

                def transposes_out(a, c):
                    pe.wait_ge(s_["o_ready"], 2 * NCH * a + 2 * c + 2)
                    pe.wait_ge(s_["cx_ready"], 2 * NCH * a + 2 * c)
                    for o in range(OA):
                        last = pe.transpose(ps[:, TR + o // 4, (o % 4) * P:(o % 4 + 1) * P], osb[:, o, :, :].rearrange("p b h -> p (b h)"), idf[:])
                    last.then_inc(s_["otr_full"], 1)

                def body(i, qkv, att, carried):
                    if att and not (isinstance(i, int) and i == 1):
                        scores(i - 1, 0)
                    if has(i, 0, 2, att, carried):
                        weighted(*chunk(i, 0, 2))
                    if qkv:
                        transposes_in(i)
                    for c in range(NCH):
                        u = 3 * c
                        if qkv:
                            project(i, u)
                        if att and (c > 0 or isinstance(i, int) and i == 1):
                            scores(i - 1, c)
                        if qkv:
                            project(i, u + 1)
                        if c > 0 and has(i, c, 2, att, carried):
                            weighted(*chunk(i, c, 2))
                        if qkv:
                            project(i, u + 2)
                        if has(i, c, 2, att, carried):
                            transposes_out(*chunk(i, c, 2))

                pe.wait_ge(ident_in, 16)
                body(0, True, False, False)
                body(1, True, True, False)
                with pe.Fori(2, NSEQ) as i:
                    body(i, True, True, True)
                body(NSEQ, False, True, True)
                body(NSEQ + 1, False, False, True)


INTER = 1376
FT = -(-INTER // P)
FR = INTER - (FT - 1) * P
CC = 256
NPACK = 8
G_GU, G_D = D // P, INTER // P


def gu_chunks():
    return [(c, min(CC, INTER - c)) for c in range(0, INTER, CC)]


def feed_forward(nc, x1_dram, ctx_dram, xT_dram, out, qw_gu, qz_gu, sc_gu, gi_gu, qw_d, qz_d, sc_d, gi_d):
    gu_tables = [("gu", c, n) for c, n in gu_chunks()]
    DOWN = 2
    tables = gu_tables[:DOWN] + [("d", 0, D)] + gu_tables[DOWN:]

    def gu_table(j):
        return j if j < DOWN else j + 1

    first_units = [(gu_table(0), k) for k in range(KD)]
    step_units = []
    for m in range(FT):
        ahead = [(gu_table(m // 2 + 1), 2 * (m % 2) + n) for n in range(2)] if m // 2 + 1 < len(gu_tables) else []
        step_units.append(ahead + [(DOWN, n) for n in {FT - 2: (m, FT - 1), FT - 1: ()}.get(m, (m,))])
    units = first_units + [u for us in step_units for u in us]
    NUN = len(units)
    with ExitStack() as ctx:
        def sb(name, shape, dt=F32, scope=ctx):
            return scope.enter_context(nc.sbuf_tensor(name, shape, dt))

        def sem(name):
            return ctx.enter_context(nc.semaphore(name))

        gu_hi = sb("gu_hi", [P, KD, 2 * INTER], F32R)
        gu_lo = sb("gu_lo", [P, KD, 2 * INTER], F32R)
        d_hi = sb("d_hi", [P, FT, D], F32R)
        d_lo = sb("d_lo", [P, FT, D], F32R)
        xT_hi = sb("xT2_hi", [P, KD, L], F32R)
        xT_lo = sb("xT2_lo", [P, KD, L], F32R)
        with ExitStack() as index_scope:
            gi = {"gu": sb("idx_gu", [G_GU, D], I32, index_scope), "d": sb("idx_d", [G_D, INTER], I32, index_scope)}
            gf = sb("gf", [G_D, INTER], F32, index_scope)
            gn = sb("gn", [G_D, INTER], F32, index_scope)
        th = sb("th", [P, 2, L])
        gs = sb("gs", [P, 2, L])
        hf = sb("hf", [P, 2, L])
        h_hi = sb("h_hi", [P, 2, L], F32R)
        h_lo = sb("h_lo", [P, 2, L], F32R)
        with ExitStack() as weight_scope:
            shift = sb("shift", [P, 1], U32, weight_scope)
            part = sb("part", [G_D, 1], F32, weight_scope)
            hot = {"gu": sb("hot_gu", [G_GU, D], F32R, weight_scope), "d": sb("hot_d", [G_D, INTER], F32R, weight_scope)}
            stage = sb("stage2", [P, 2, 512], U32, weight_scope)
            nib = sb("nib", [P, 2, 512], U32, weight_scope)
            wf = sb("wf", [P, 2, 512], F32, weight_scope)
            s_hi = sb("s_hi", [G_D, 3, 512], F32R, weight_scope)
            s_lo = sb("s_lo", [G_D, 3, 512], F32R, weight_scope)
            sraw = sb("sraw", [G_D, 512], F32, weight_scope)
            zt = sb("zt", [G_D, 3, 512], F32R, weight_scope)
            znib = sb("znib", [G_D, 512], U32, weight_scope)
            zraw = sb("zraw", [G_D, 64], U32, weight_scope)
        xst = sb("xst", [P, 2, KD, L])
        xa = sb("xa", [P, NT, D])
        xb = sb("xb", [P, NT, D])
        ps = ctx.enter_context(nc.psum_tensor("ps3", [P, 8, 512], F32))
        GATE, UP, ACC = 0, 2, 4
        SG, ZG = GATE + 1, UP + 1

        gi_in = sem("gi_in")
        q_in = [sem(f"q_in{s}") for s in range(2)]
        tab_in = sem("tab_in")
        iota_done, shift_done, hot_done = sem("iota_done"), sem("shift_done"), sem("hot_done")
        s_hi_done, s_lo_done, znib_done, z_done = sem("s_hi_done"), sem("s_lo_done"), sem("znib_done"), sem("z_done")
        nib_done, gathered, wz_done, wf_done = sem("nib_done"), sem("gathered"), sem("wz_done"), sem("wf_done")
        wq_hi_done, wq_lo_done = sem("wq_hi_done"), sem("wq_lo_done")
        xT_in, xst_in, res_in, out_out = sem("xT2_in"), sem("xst_in"), sem("res2_in"), sem("out_out")
        x_hi_done, x_lo_done = sem("x_hi_done"), sem("x_lo_done")
        ctx_in, acc_out = sem("ctx_in"), sem("acc_out")
        gate_full, gu_full, th_done, gs_done, hf_done = sem("gate_full"), sem("gu_full"), sem("th_done"), sem("gs_done"), sem("hf_done")
        h_hi_done, h_lo_done = sem("h_hi_done"), sem("h_lo_done")
        down_done, y_done = sem("down_done"), sem("y_done")

        def groups(n):
            return G_GU if tables[n][0] == "gu" else G_D

        def urows(u):
            n, k = units[u]
            return FR if n == DOWN and k == FT - 1 else P

        def width(n):
            return 2 * tables[n][2] if tables[n][0] == "gu" else D

        def slot(n):
            return 2 if n == DOWN else gu_tables.index(tables[n]) % 2

        def unit_of(n, k):
            return units.index((n, k))

        def slot_used(n):
            j = gu_tables.index(tables[n]) - 2 if n != DOWN else -1
            return unit_of(gu_table(j), KD - 1) + 1 if j >= 0 else 0

        def tab_loads(n):
            return sum(2 * len(pieces(t)) for t in range(n + 1))

        def pieces(n):
            kind, c, m = tables[n]
            return [(c, 0, m), (INTER + c, m, m)] if kind == "gu" else [(0, 0, D)]

        def out_pieces(u, hi):
            n, k = units[u]
            if n != DOWN:
                _, c, m = tables[n]
                return (gu_hi if hi else gu_lo)[:, k, :].rearrange("p (s n) -> p s n", s=2)[:, :, c:c + m], m
            return (d_hi if hi else d_lo)[0:urows(u), k, :].rearrange("p (s n) -> p s n", s=2), D // 2

        def units_of(m):
            first = len(first_units) + sum(len(us) for us in step_units[:m])
            return list(range(first, first + len(step_units[m])))

        def tables_at(m):
            j = m // 2 + 2
            return [gu_table(j)] if m % 2 == 0 and j < len(gu_tables) else []

        def places(m):
            us = units_of(m)
            return us[:-2], us[-2:-1] if len(us) > 1 else us, us[-1:] if len(us) > 1 else []

        FIRST_TABLES = (gu_table(0), gu_table(1), DOWN)

        def rows(m):
            return FR if m == FT - 1 else P

        with nc.Block() as block:

            @block.sync
            def _(sp):
                for kind, src, g, n in (("gu", gi_gu, G_GU, D), ("d", gi_d, G_D, INTER)):
                    sp.dma_start(gi[kind][:], bass.AP(src.tensor, 0, [[0, g], [1, n]])).then_inc(gi_in, 16)

                def table(n):
                    g = groups(n)
                    sp.wait_ge(s_lo_done, n)
                    sp.wait_ge(znib_done, NPACK * n)
                    sc, qz = (sc_d, qz_d) if n == DOWN else (sc_gu, qz_gu)
                    for c, t, m in pieces(n):
                        sp.dma_start(sraw[0:g, t:t + m], sc[:, c:c + m]).then_inc(tab_in, 16)
                        sp.dma_start(zraw[0:g, t // NPACK:(t + m) // NPACK], qz[:, c // NPACK:(c + m) // NPACK]).then_inc(tab_in, 16)

                def packed(u):
                    n, k = units[u]
                    qw = qw_d if n == DOWN else qw_gu
                    cols = qw.shape[1]
                    if u >= 2:
                        sp.wait_ge(nib_done, u - 1)
                    for c, t, m in pieces(n):
                        src = bass.AP(qw.tensor, (k * P // NPACK) * cols + c, [[cols, urows(u) // NPACK], [0, NPACK], [1, m]])
                        sp.dma_start(stage[0:urows(u), u % 2, t:t + m], src).then_inc(q_in[u % 2], 16)

                def load_xst(i):
                    sp.dma_start(xst[:].rearrange("p s k t -> p s (k t)"), xT_dram[bass.ds(i, 1), :, :, :].rearrange("o s p n -> p (o s) n")).then_inc(xst_in, 16)

                def load_res(i):
                    sp.dma_start(xa[:], x1_dram[bass.ds(i * L, L), :].rearrange("(t p) d -> p t d", p=P)).then_inc(res_in, 16)
                    for q in range(TPG):
                        src = ctx_dram[bass.ds(i * L, L), :].rearrange("(t g q) d -> q g t d", q=TPG, g=NG)[q]
                        sp.dma_start(xb[NG * q:NG * (q + 1), :, :], src).then_inc(ctx_in, 16)

                def store(i):
                    for t in range(NT):
                        sp.wait_ge(y_done, NT * i + t + 1)
                        sp.dma_start(out[bass.ds(i * L + t * P, P), :], xa[:, t, :]).then_inc(out_out, 16)

                def body(i, last):
                    if not last:
                        sp.wait_ge(x_hi_done, KD * i)
                        sp.wait_ge(x_lo_done, KD * i)
                        load_xst(i + 1)
                    store(i - 1)
                    sp.wait_ge(out_out, 64 * i)
                    load_res(i)

                table(gu_table(0))
                packed(0)
                packed(1)
                table(gu_table(1))
                for u in range(2, len(first_units)):
                    packed(u)
                table(DOWN)
                for part, xT in ((0, xT_hi), (1, xT_lo)):
                    sp.dma_start(xT[:].rearrange("p k t -> p (k t)").bitcast(F32), xT_dram[0, part, :, :]).then_inc(xT_in, 16)
                for m in range(FT):
                    for u in units_of(m):
                        packed(u)
                    for n in tables_at(m):
                        table(n)
                sp.wait_ge(wq_lo_done, NUN)
                load_xst(1)
                load_res(0)
                with sp.Fori(1, NSEQ - 1) as i:
                    body(i, False)
                body(NSEQ - 1, True)
                store(NSEQ - 1)
                sp.wait_ge(out_out, 64 * NSEQ)

            @block.gpsimd
            def _(pool):
                pool.iota(shift[:], [[0, 1]], base=0, channel_multiplier=4).then_inc(iota_done, 1)
                pool.iota(part[:], [[0, 1]], base=0, channel_multiplier=1, allow_small_or_imprecise_dtypes=True).then_inc(iota_done, 1)

                def table(n):
                    s, g, m = slot(n), groups(n), width(n)
                    pool.wait_ge(s_hi_done, n + 1)
                    pool.tensor_tensor(s_lo[0:g, s, 0:m], sraw[0:g, 0:m], s_hi[0:g, s, 0:m].bitcast(F32), ALU.subtract).then_inc(s_lo_done, 1)

                def split(u):
                    pool.wait_ge(wq_hi_done, u + 1)
                    (hi, m), (lo, _) = out_pieces(u, True), out_pieces(u, False)
                    v = wf[0:urows(u), u % 2, 0:2 * m].rearrange("p (s n) -> p s n", s=2)
                    pool.tensor_tensor(lo, v, hi.bitcast(F32), ALU.subtract).then_inc(wq_lo_done, 1)

                def body(i):
                    pool.wait_ge(ctx_in, 16 * TPG * (i + 1))
                    for t in range(NT):
                        pool.wait_ge(acc_out, NT * i + t + 1)
                        pool.tensor_tensor(xa[:, t, :], xa[:, t, :], xb[:, t, :], ALU.add).then_inc(y_done, 1)

                for n in FIRST_TABLES[:2]:
                    table(n)
                for u in range(len(first_units)):
                    split(u)
                table(DOWN)
                for m in range(FT):
                    for u in units_of(m):
                        split(u)
                    for n in tables_at(m):
                        table(n)
                body(0)
                with pool.Fori(1, NSEQ) as i:
                    body(i)

            @block.scalar
            def _(act):
                def table(n):
                    s, g, m = slot(n), groups(n), width(n)
                    act.wait_ge(tab_in, 16 * tab_loads(n))
                    act.wait_ge(gathered, slot_used(n))
                    act.activation(s_hi[0:g, s, 0:m], sraw[0:g, 0:m], ACT.Copy).then_inc(s_hi_done, 1)

                def split(u):
                    act.wait_ge(wf_done, u + 1)
                    hi, m = out_pieces(u, True)
                    act.activation(hi, wf[0:urows(u), u % 2, 0:2 * m].rearrange("p (s n) -> p s n", s=2), ACT.Copy).then_inc(wq_hi_done, 1)

                def gate_tanh(i, m, s):
                    r = rows(m)
                    act.wait_ge(gate_full, FT * i + m + 1)
                    act.wait_ge(gs_done, FT * i + max(0, m - 1))
                    act.activation(th[0:r, m % 2, :], ps[0:r, GATE + s, :], ACT.Tanh, scale=0.5).then_inc(th_done, 1)

                def h_first(i, m):
                    r = rows(m)
                    act.wait_ge(hf_done, FT * i + m + 1)
                    act.wait_ge(down_done, FT * i + max(0, m - 1))
                    act.activation(h_hi[0:r, m % 2, :], hf[0:r, m % 2, :], ACT.Copy).then_inc(h_hi_done, 1)

                def body(i):
                    act.wait_ge(xst_in, 16 * i)
                    act.wait_ge(gu_full, FT * i)
                    for k in range(KD):
                        act.activation(xT_hi[:, k, :], xst[:, 0, k, :], ACT.Copy).then_inc(x_hi_done, 1)
                    for m in range(FT):
                        gate_tanh(i, m, m % 2)
                        h_first(i, m)

                for n in FIRST_TABLES[:2]:
                    table(n)
                for u in range(len(first_units)):
                    split(u)
                table(DOWN)
                for m in range(FT):
                    early, mid, late = places(m)
                    for u in early:
                        split(u)
                    gate_tanh(0, m, 0)
                    h_first(0, m)
                    for u in mid + late:
                        split(u)
                    for n in tables_at(m):
                        table(n)
                with act.Fori(1, NSEQ) as i:
                    body(i)

            @block.vector
            def _(dve):
                n_hot = [0]

                def step(ins):
                    n_hot[0] += 1
                    ins.then_inc(hot_done, 1)
                    dve.wait_ge(hot_done, n_hot[0])

                def one_hot(kind, g, n):
                    f, t = gf[0:g, 0:n], gn[0:g, 0:n]
                    step(dve.tensor_copy(f, gi[kind][:]))
                    step(dve.tensor_scalar(t, f, 0.0, float(g), ALU.is_lt, ALU.mult))
                    step(dve.tensor_tensor(f, f, t, ALU.add))
                    step(dve.tensor_scalar(f, f, 0.0, float(g - 1), ALU.max, ALU.min))
                    step(dve.tensor_scalar(hot[kind][:], f, part[0:g, :], None, ALU.is_equal))

                def table(n):
                    s, g, m = slot(n), groups(n), width(n)
                    dve.wait_ge(tab_in, 16 * tab_loads(n))
                    dve.wait_ge(z_done, n)
                    dve.wait_ge(gathered, slot_used(n))
                    zv = znib[0:g, 0:m].rearrange("g (c b) -> g c b", b=NPACK)
                    for b in range(NPACK):
                        dve.tensor_scalar(zv[:, :, b], zraw[0:g, 0:m // NPACK], 4 * b, 15, ALU.logical_shift_right, ALU.bitwise_and).then_inc(znib_done, 1)
                    dve.wait_ge(znib_done, NPACK * (n + 1))
                    dve.tensor_scalar(zt[0:g, s, 0:m], znib[0:g, 0:m], 1.0, None, ALU.add).then_inc(z_done, 1)

                def nibbles(u):
                    r, m = urows(u), width(units[u][0])
                    dve.wait_ge(q_in[u % 2], 16 * sum(len(pieces(units[v][0])) for v in range(u + 1) if v % 2 == u % 2))
                    dve.wait_ge(wz_done, max(0, u - 1))
                    dve.tensor_scalar(nib[0:r, u % 2, 0:m], stage[0:r, u % 2, 0:m], shift[0:r, :], 15, ALU.logical_shift_right, ALU.bitwise_and).then_inc(nib_done, 1)

                def scaled(u):
                    if u + 1 < NUN:
                        nibbles(u + 1)
                    r, m = urows(u), width(units[u][0])
                    v = wf[0:r, u % 2, 0:m]
                    dve.wait_ge(gathered, u + 1)
                    dve.wait_ge(nib_done, u + 1)
                    if u >= 2:
                        dve.wait_ge(wq_lo_done, u - 1)
                    dve.tensor_tensor(v, nib[0:r, u % 2, 0:m], ps[0:r, ZG, 0:m], ALU.subtract).then_inc(wz_done, 1)
                    dve.wait_ge(wz_done, u + 1)
                    dve.tensor_tensor(v, v, ps[0:r, SG, 0:m], ALU.mult).then_inc(wf_done, 1)

                def gated(i, m, s):
                    r, o = rows(m), m % 2
                    dve.wait_ge(th_done, FT * i + m + 1)
                    dve.wait_ge(h_lo_done, FT * i + max(0, m - 1))
                    dve.scalar_tensor_tensor(gs[0:r, o, :], th[0:r, o, :], 1.0, ps[0:r, GATE + s, :], ALU.add, ALU.mult).then_inc(gs_done, 1)
                    dve.wait_ge(gs_done, FT * i + m + 1)
                    dve.wait_ge(gu_full, FT * i + m + 1)
                    dve.scalar_tensor_tensor(hf[0:r, o, :], gs[0:r, o, :], 0.5, ps[0:r, UP + s, :], ALU.mult, ALU.mult).then_inc(hf_done, 1)

                def h_rest(i, m):
                    r, o = rows(m), m % 2
                    dve.wait_ge(h_hi_done, FT * i + m + 1)
                    dve.tensor_tensor(h_lo[0:r, o, :], hf[0:r, o, :], h_hi[0:r, o, :].bitcast(F32), ALU.subtract).then_inc(h_lo_done, 1)

                def sums(i):
                    dve.wait_ge(res_in, 16 * i + 16)
                    dve.wait_ge(down_done, FT * i + FT)
                    for t in range(NT):
                        dve.tensor_tensor(xa[:, t, :], ps[:, ACC + t, :], xa[:, t, :], ALU.add).then_inc(acc_out, 1)

                def next_x(i):
                    dve.wait_ge(xst_in, 16 * i)
                    dve.wait_ge(gu_full, FT * i)
                    for k in range(KD):
                        dve.tensor_copy(xT_lo[:, k, :], xst[:, 1, k, :]).then_inc(x_lo_done, 1)

                def body(i):
                    next_x(i)
                    sums(i - 1)
                    for m in range(FT):
                        gated(i, m, m % 2)
                        h_rest(i, m)

                dve.wait_ge(iota_done, 2)
                dve.tensor_scalar(shift[:], shift[:], 31, None, ALU.bitwise_and).then_inc(shift_done, 1)
                dve.wait_ge(gi_in, 32)
                dve.wait_ge(shift_done, 1)
                one_hot("gu", G_GU, D)
                table(gu_table(0))
                nibbles(0)
                for u in range(len(first_units)):
                    scaled(u)
                    if u == 0:
                        table(gu_table(1))
                        one_hot("d", G_D, INTER)
                for m in range(FT):
                    early, mid, late = places(m)
                    for u in early:
                        scaled(u)
                    if m == 0:
                        table(DOWN)
                    gated(0, m, 0)
                    for u in mid:
                        scaled(u)
                    h_rest(0, m)
                    for u in late:
                        scaled(u)
                    for n in tables_at(m):
                        table(n)
                body(1)
                with dve.Fori(2, NSEQ) as i:
                    body(i)
                sums(NSEQ - 1)

            @block.tensor
            def _(pe):
                def gather(u):
                    n, k = units[u]
                    kind, s, g, r, m = tables[n][0], slot(n), groups(n), urows(u), width(n)
                    pe.wait_ge(hot_done, 5 if kind == "gu" else 10)
                    pe.wait_ge(s_lo_done, n + 1)
                    pe.wait_ge(z_done, n + 1)
                    pe.wait_ge(wf_done, u)
                    oh = hot[kind][:, k * P:k * P + r]
                    pe.matmul(ps[0:r, ZG, 0:m], oh, zt[0:g, s, 0:m], start=True, stop=True)
                    pe.matmul(ps[0:r, SG, 0:m], oh, s_hi[0:g, s, 0:m], start=True, stop=False)
                    pe.matmul(ps[0:r, SG, 0:m], oh, s_lo[0:g, s, 0:m], start=False, stop=True).then_inc(gathered, 1)

                def half(i, m, s, bank, c0):
                    r = rows(m)
                    c = slice(c0 + m * P, c0 + m * P + r)
                    for k in range(KD):
                        if m == 0 and bank == GATE and not (isinstance(i, int) and i == 0):
                            pe.wait_ge(x_hi_done, KD * (i - 1) + k + 1)
                            pe.wait_ge(x_lo_done, KD * (i - 1) + k + 1)
                        if isinstance(i, int) and i == 0:
                            pe.wait_ge(wq_lo_done, unit_of(gu_table(m // 2), k) + 1)
                        last = split3(pe, ps[0:r, bank + s, :], (gu_hi[:, k, c], gu_lo[:, k, c]), (xT_hi[:, k, :], xT_lo[:, k, :]), k == 0, k == KD - 1)
                    last.then_inc(gate_full if bank == GATE else gu_full, 1)

                def gate_up(i, m):
                    pe.wait_ge(hf_done, FT * i + max(0, m - 1))
                    half(i, m, m % 2, GATE, 0)
                    half(i, m, m % 2, UP, INTER)

                def down(i, m):
                    r, s = rows(m), m % 2
                    pe.wait_ge(h_lo_done, FT * i + m + 1)
                    if m == 0:
                        pe.wait_ge(acc_out, NT * i)
                    if isinstance(i, int) and i == 0:
                        pe.wait_ge(wq_lo_done, unit_of(DOWN, m) + 1)
                    for t in range(NT):
                        ts = slice(t * P, (t + 1) * P)
                        last = split3(pe, ps[:, ACC + t, :], (h_hi[0:r, s, ts], h_lo[0:r, s, ts]), (d_hi[0:r, m, :], d_lo[0:r, m, :]), m == 0, m == FT - 1)
                    last.then_inc(down_done, 1)

                def body(i):
                    gate_up(i, 0)
                    for m in range(FT):
                        if m + 1 < FT:
                            gate_up(i, m + 1)
                        down(i, m)

                for u in range(len(first_units)):
                    gather(u)
                pe.wait_ge(xT_in, 32)
                for m in range(FT):
                    early, mid, late = places(m)
                    pe.wait_ge(hf_done, m)
                    half(0, m, 0, GATE, 0)
                    for u in early:
                        gather(u)
                    half(0, m, 0, UP, INTER)
                    for u in mid:
                        gather(u)
                    if m > 0:
                        down(0, m - 1)
                    for u in late:
                        gather(u)
                down(0, FT - 1)
                with pe.Fori(1, NSEQ) as i:
                    body(i)


def block_kernel(nc, x, w0, bias_f, proj_b, base_b, w1, bv1, qw_gu, qz_gu, sc_gu, gi_gu, qw_d, qz_d, sc_d, gi_d,
                 ident, ident_bf, causal, iota8, out):
    def scratch(name, shape, dt=F32):
        return nc.dram_tensor(name, shape, dt, kind="Internal").ap()

    x1_dram = scratch("x1_dram", [NSEQ * L, D])
    ctx_dram = scratch("ctx_dram", [NSEQ, L, D])
    xT_dram = scratch("xT_dram", [NSEQ, 2, P, KD * L])
    q3 = scratch("q3", [NSEQ, D // P, 3, NCH, P, P], BF16)
    k3 = scratch("k3", [NSEQ, D // P, 3, NCH, P, P], BF16)
    layer0(nc, x, w0, bias_f, proj_b, base_b, ident, ident_bf, causal, iota8, x1_dram)
    attention1(nc, x1_dram, w1, bias_f, bv1, ident, q3, k3, xT_dram, ctx_dram)
    feed_forward(nc, x1_dram, ctx_dram.rearrange("s t d -> (s t) d"), xT_dram, out, qw_gu, qz_gu, sc_gu, gi_gu, qw_d, qz_d, sc_d, gi_d)


def tiles(a):
    import numpy as np
    return np.ascontiguousarray(a.reshape(-1, P, a.shape[1]).transpose(1, 0, 2).reshape(P, -1))


def kernel(**inputs):
    import ml_dtypes
    import numpy as np
    import concourse.bacc as bacc
    from concourse.bass_utils import run_bass_kernel_spmd

    a = {k: np.asarray(v) for k, v in inputs.items()}
    w0 = np.concatenate([
        tiles(a["L0_attn_conv_w"].reshape(TAPS * D, 3 * W)),
        a["L0_attn_wq"].reshape(W, H0 * DH0), a["L0_attn_wk"].reshape(W, H0 * DH0), a["L0_attn_wv"].reshape(W, H0 * DH0),
        tiles(a["L0_attn_wo"].reshape(H0 * DH0, W)), a["L0_attn_proj_w"], tiles(a["L0_ffn_W_base"].T),
        tiles(np.concatenate([a["L0_ffn_A_stack"].reshape(ER, D).T, a["L0_ffn_W_router"].T, np.zeros((D, AR - ER - NE), np.float32)], 1)),
        a["L0_ffn_B_stack"].transpose(0, 2, 1).reshape(ER, D)], 1)
    by_d = lambda w: np.ascontiguousarray(w.reshape(-1, HPT, DH1, *w.shape[1:]).swapaxes(1, 2)).reshape(w.shape)
    bias_f = np.concatenate([a[n].reshape(-1, P).T for n in (
        "L0_attn_conv_b", "L0_attn_bq", "L0_attn_bk", "L0_attn_bv", "L0_attn_bo")]
        + [by_d(a[n]).reshape(-1, P).T for n in ("L1_attn_bq", "L1_attn_bk")], 1)
    wv1 = a["L1_attn_wv"].reshape(H1, DH1, D).transpose(1, 0, 2).reshape(D, D)
    bv1 = a["L1_attn_bv"].reshape(H1, DH1).T.reshape(D)
    w1 = np.concatenate([tiles(w.T) for w in (by_d(a["L1_attn_wq"]), by_d(a["L1_attn_wk"]), wv1)], 1)
    above = np.where(np.arange(P)[None, :] <= np.arange(P)[:, None], 0.0, -1e30).astype(ml_dtypes.bfloat16)
    arrays = {
        "x": a["L0_attn_inputs"].reshape(NSEQ * L, D), "w0": w0, "bias_f": bias_f,
        "proj_b": a["L0_attn_proj_b"], "base_b": a["L0_ffn_b_base"], "w1": w1, "bv1": bv1,
        "qw_gu": a["L1_ffn_qweight_gu"], "qz_gu": a["L1_ffn_qzeros_gu"], "sc_gu": a["L1_ffn_scales_gu"], "gi_gu": a["L1_ffn_g_idx_gu"],
        "qw_d": a["L1_ffn_qweight_down"], "qz_d": a["L1_ffn_qzeros_down"], "sc_d": a["L1_ffn_scales_down"], "gi_d": a["L1_ffn_g_idx_down"],
        "ident": np.eye(P, dtype=np.float32), "ident_bf": np.eye(P).astype(ml_dtypes.bfloat16),
        "causal": np.tile(above, (1, HG)), "iota8": np.tile(np.arange(NE, dtype=np.float32), (P, NT)),
    }
    arrays = {k: np.ascontiguousarray(v) for k, v in arrays.items()}
    nc = bacc.Bacc("TRN2", target_bir_lowering=False, num_devices=1)
    args = {k: nc.dram_tensor(k, v.shape, mybir.dt.from_np(v.dtype), kind="ExternalInput").ap() for k, v in arrays.items()}
    out = nc.dram_tensor("out", [NSEQ * L, D], F32, kind="ExternalOutput").ap()
    block_kernel(nc, **args, out=out)
    r = run_bass_kernel_spmd(nc, [arrays], core_ids=[0])
    return r.results[0]["out"].reshape(NSEQ, L, D)
```
